# Optimizing a Trainium2 kernel written in Bass

```python
import numpy as np
import jax
import jax.numpy as jnp

def _softmax(x, axis=-1):
    return jax.nn.softmax(x, axis=axis)

def _gelu(x):
    return jax.nn.gelu(x, approximate=True)

def _silu(x):
    return jax.nn.silu(x)

def _sigmoid(x):
    return jax.nn.sigmoid(x)

def _layernorm(x, axis=-1, eps=1e-05):
    m = jnp.mean(x, axis=axis, keepdims=True)
    v = jnp.var(x, axis=axis, keepdims=True)
    return (x - m) / jnp.sqrt(v + eps)

def _scatter_add(tgt, idx, src, axis=0):
    return tgt.at[idx].add(src)

def _segment_sum(src, seg, n):
    return jax.ops.segment_sum(src, seg, n)
kernel_name = 'mk_flamingo_gated_d2_seqx_r8_4b876e'

def setup_inputs(seed: int=0):
    np.random.seed(seed)
    _w = jnp.asarray

    def _rec_inputs():
        import jax
        import jax.numpy as jnp
        _rk = jax.random.key(seed)
        x = -0.0003929 + 0.9999 * jax.random.normal(jax.random.fold_in(_rk, 1), (16, 128, 128), jnp.float32)
        _lenS = 128 - jax.random.randint(jax.random.fold_in(_rk, 7), (16,), 0, max(1, 128 // 4) + 1, jnp.int32)
        _lenS2 = 77 - jax.random.randint(jax.random.fold_in(_rk, 8), (16,), 0, max(1, 77 // 4) + 1, jnp.int32)
        _ctx_1024P = jax.random.normal(jax.random.fold_in(_rk, 11), (16, 16, 128), jnp.float32)
        _ctx_1024c = jax.random.dirichlet(jax.random.fold_in(_rk, 511), 0.3 * jnp.ones((16,), jnp.float32), (16, 77))
        _ctx_1024t = jnp.einsum('bsk,bkd->bsd', _ctx_1024c, _ctx_1024P)
        _ctx_1024t = _ctx_1024t * jax.lax.rsqrt(jnp.mean(jnp.square(_ctx_1024t)) + 1e-12) * 0.953939
        ctx_1024 = 2.81802e-05 + 1.00001 * (_ctx_1024t + 0.3 * jax.random.normal(jax.random.fold_in(_rk, 611), (16, 77, 128), jnp.float32))
        _g = jax.random.normal(jax.random.fold_in(_rk, 9001), (2, 2), jnp.float32)
        _g = jnp.sign(_g) * jnp.maximum(jnp.abs(_g), 1.0) + (_g == 0) * 1.0
        g_xattn = _g[0]
        g_ffn = _g[1]
        return (x, ctx_1024, g_xattn, g_ffn)
    x, ctx_1024, g_xattn, g_ffn = _rec_inputs()

    def _L0_xattn_setup():
        import jax, jax.numpy as jnp
        import numpy as np
        QUERY_DIM = 128
        HIDDEN_DIM = 128
        key = jax.random.key(seed)
        k1, k2, k3, k4 = jax.random.split(key, 4)
        query = jax.random.normal(k1, (8, 256, QUERY_DIM), dtype=jnp.float32)
        info = jax.random.normal(k2, (8, 256, HIDDEN_DIM), dtype=jnp.float32)
        bound = 1.0 / np.sqrt(QUERY_DIM)
        W = jax.random.uniform(k3, (HIDDEN_DIM, QUERY_DIM), jnp.float32, -bound, bound)
        b = jax.random.uniform(k4, (HIDDEN_DIM,), jnp.float32, -bound, bound)
        return {'query': query, 'info': info, 'W': W, 'b': b}
    _L0_xattn_all = _L0_xattn_setup()
    _L0_xattn_in = {k: v for k, v in _L0_xattn_all.items() if k in ('W', 'b')}
    del _L0_xattn_all

    def _L0_ffn_setup():
        import jax, jax.numpy as jnp
        import numpy as np
        from jax import lax
        DIM = 128
        INTER = 64
        N_EXPERTS = 16
        TOPK = 4
        ROUTE_SCALE = 2.5
        VOCAB = 4000

        def _silu_and_mul(gu):
            gate, up = jnp.split(gu, 2, axis=-1)
            return jax.nn.silu(gate) * up
        key = jax.random.key(seed)
        ks = jax.random.split(key, 8)
        x = jax.random.normal(ks[0], (2, 64, DIM), dtype=jnp.float32)
        input_ids = jax.random.randint(ks[1], (2, 64), 0, VOCAB)
        s = 0.02
        gate_w = jax.random.normal(ks[2], (N_EXPERTS, DIM), dtype=jnp.float32) * s
        gate_b = jax.random.normal(ks[3], (N_EXPERTS,), dtype=jnp.float32) * s
        w13 = jax.random.normal(ks[4], (N_EXPERTS, 2 * INTER, DIM), dtype=jnp.float32) * s
        w2 = jax.random.normal(ks[5], (N_EXPERTS, DIM, INTER), dtype=jnp.float32) * s
        w13_s = jax.random.normal(ks[6], (2 * INTER, DIM), dtype=jnp.float32) * s
        w2_s = jax.random.normal(ks[7], (DIM, INTER), dtype=jnp.float32) * s
        return {'x': x, 'input_ids': input_ids, 'gate_w': gate_w, 'gate_b': gate_b, 'w13': w13, 'w2': w2, 'w13_s': w13_s, 'w2_s': w2_s}
    _L0_ffn_all = _L0_ffn_setup()
    _L0_ffn_in = {k: v for k, v in _L0_ffn_all.items() if k in ('input_ids', 'gate_w', 'gate_b', 'w13', 'w2', 'w13_s', 'w2_s')}
    del _L0_ffn_all

    def _L1_xattn_setup():
        import jax, jax.numpy as jnp
        import numpy as np
        HIDDEN = 128
        NUM_HEADS = 16
        HEAD_DIM = HIDDEN // NUM_HEADS
        SCALE = 1.0 / float(np.sqrt(HEAD_DIM))
        key = jax.random.key(seed)
        ks = jax.random.split(key, 10)
        B, SQ, SKV = (2, 256, 512)
        init = 0.02
        return {'query_states': jax.random.normal(ks[0], (B, SQ, HIDDEN), dtype=jnp.float32), 'key_value_states': jax.random.normal(ks[1], (B, SKV, HIDDEN), dtype=jnp.float32), 'Wq': jax.random.normal(ks[2], (HIDDEN, HIDDEN), dtype=jnp.float32) * init, 'bq': jnp.zeros((HIDDEN,), dtype=jnp.float32), 'Wk': jax.random.normal(ks[3], (HIDDEN, HIDDEN), dtype=jnp.float32) * init, 'bk': jnp.zeros((HIDDEN,), dtype=jnp.float32), 'Wv': jax.random.normal(ks[4], (HIDDEN, HIDDEN), dtype=jnp.float32) * init, 'bv': jnp.zeros((HIDDEN,), dtype=jnp.float32), 'Wo': jax.random.normal(ks[5], (HIDDEN, HIDDEN), dtype=jnp.float32) * init, 'bo': jnp.zeros((HIDDEN,), dtype=jnp.float32)}
    _L1_xattn_all = _L1_xattn_setup()
    _L1_xattn_in = {k: v for k, v in _L1_xattn_all.items() if k in ('Wq', 'bq', 'Wk', 'bk', 'Wv', 'bv', 'Wo', 'bo')}
    del _L1_xattn_all

    def _L1_ffn_setup():
        import jax, jax.numpy as jnp
        import numpy as np
        E = 8
        H = 128
        D = 128
        TOP_K = 2
        key = jax.random.key(seed)
        k0, k1, k2, k3 = jax.random.split(key, 4)
        x = jax.random.normal(k0, (1, 256, H), dtype=jnp.float32)
        router_w = jax.random.normal(k1, (E, H), dtype=jnp.float32) * (1.0 / np.sqrt(H))
        up_proj = jax.random.normal(k2, (E, H, 2 * D), dtype=jnp.float32) * (1.0 / np.sqrt(H))
        down_proj = jax.random.normal(k3, (E, D, H), dtype=jnp.float32) * (1.0 / np.sqrt(D))
        return {'x': x, 'router_w': router_w, 'up_proj': up_proj, 'down_proj': down_proj}
    _L1_ffn_all = _L1_ffn_setup()
    _L1_ffn_in = {k: v for k, v in _L1_ffn_all.items() if k in ('router_w', 'up_proj', 'down_proj')}
    del _L1_ffn_all
    return {'x': x, 'ctx_1024': ctx_1024, 'g_xattn': g_xattn, 'g_ffn': g_ffn, 'L0_xattn_W': _L0_xattn_in['W'], 'L0_xattn_b': _L0_xattn_in['b'], 'L0_ffn_input_ids': _L0_ffn_in['input_ids'], 'L0_ffn_gate_w': _L0_ffn_in['gate_w'], 'L0_ffn_gate_b': _L0_ffn_in['gate_b'], 'L0_ffn_w13': _L0_ffn_in['w13'], 'L0_ffn_w2': _L0_ffn_in['w2'], 'L0_ffn_w13_s': _L0_ffn_in['w13_s'], 'L0_ffn_w2_s': _L0_ffn_in['w2_s'], 'L1_xattn_Wq': _L1_xattn_in['Wq'], 'L1_xattn_bq': _L1_xattn_in['bq'], 'L1_xattn_Wk': _L1_xattn_in['Wk'], 'L1_xattn_bk': _L1_xattn_in['bk'], 'L1_xattn_Wv': _L1_xattn_in['Wv'], 'L1_xattn_bv': _L1_xattn_in['bv'], 'L1_xattn_Wo': _L1_xattn_in['Wo'], 'L1_xattn_bo': _L1_xattn_in['bo'], 'L1_ffn_router_w': _L1_ffn_in['router_w'], 'L1_ffn_up_proj': _L1_ffn_in['up_proj'], 'L1_ffn_down_proj': _L1_ffn_in['down_proj']}

def reference(x, ctx_1024, g_xattn, g_ffn, L0_xattn_W, L0_xattn_b, L0_ffn_input_ids, L0_ffn_gate_w, L0_ffn_gate_b, L0_ffn_w13, L0_ffn_w2, L0_ffn_w13_s, L0_ffn_w2_s, L1_xattn_Wq, L1_xattn_bq, L1_xattn_Wk, L1_xattn_bk, L1_xattn_Wv, L1_xattn_bv, L1_xattn_Wo, L1_xattn_bo, L1_ffn_router_w, L1_ffn_up_proj, L1_ffn_down_proj):
    import jax
    import jax.numpy as jnp

    def _L0_xattn_ref(query, info, W, b):
        import jax, jax.numpy as jnp
        import numpy as np
        QUERY_DIM = 128
        HIDDEN_DIM = 128
        q = jnp.einsum('bsq,hq->bsh', query, W) + b
        scores = jax.nn.softmax(jnp.einsum('bsh,bmh->bsm', q, info), axis=-1)
        return jnp.einsum('bsm,bmh->bsh', scores, info)

    def _L0_ffn_ref(x, input_ids, gate_w, gate_b, w13, w2, w13_s, w2_s):
        import jax, jax.numpy as jnp
        import numpy as np
        from jax import lax
        DIM = 128
        INTER = 64
        N_EXPERTS = 16
        TOPK = 4
        ROUTE_SCALE = 2.5
        VOCAB = 4000

        def _silu_and_mul(gu):
            gate, up = jnp.split(gu, 2, axis=-1)
            return jax.nn.silu(gate) * up
        B, S, D = x.shape
        xt = x.reshape(-1, D)
        T = xt.shape[0]
        scores = jax.nn.sigmoid(xt.astype(jnp.float32) @ gate_w.T)
        biased = scores + gate_b
        _, idx = lax.top_k(biased, TOPK)
        w = jnp.take_along_axis(scores, idx, axis=-1)
        w = w / jnp.sum(w, axis=-1, keepdims=True)
        w = w * ROUTE_SCALE
        comb = jnp.zeros((T, N_EXPERTS), jnp.float32)
        comb = comb.at[jnp.arange(T)[:, None], idx].add(w)
        comb = comb.astype(x.dtype)

        def expert_body(y, args):
            w13_e, w2_e, c_e = args
            h = _silu_and_mul(xt @ w13_e.T)
            return (y + c_e[:, None] * (h @ w2_e.T), None)
        y, _ = lax.scan(expert_body, jnp.zeros_like(xt), (w13, w2, comb.T))
        y = y + _silu_and_mul(xt @ w13_s.T) @ w2_s.T
        return y.astype(x.dtype).reshape(B, S, D)

    def _L1_xattn_ref(query_states, key_value_states, Wq, bq, Wk, bk, Wv, bv, Wo, bo):
        import jax, jax.numpy as jnp
        import numpy as np
        HIDDEN = 128
        NUM_HEADS = 16
        HEAD_DIM = HIDDEN // NUM_HEADS
        SCALE = 1.0 / float(np.sqrt(HEAD_DIM))
        B, SQ, _ = query_states.shape
        _, SKV, _ = key_value_states.shape
        q = query_states @ Wq.T + bq
        k = key_value_states @ Wk.T + bk
        v = key_value_states @ Wv.T + bv
        q = q.reshape(B, SQ, NUM_HEADS, HEAD_DIM).transpose(0, 2, 1, 3) * SCALE
        k = k.reshape(B, SKV, NUM_HEADS, HEAD_DIM).transpose(0, 2, 1, 3)
        v = v.reshape(B, SKV, NUM_HEADS, HEAD_DIM).transpose(0, 2, 1, 3)
        scores = jnp.einsum('bhqd,bhkd->bhqk', q, k)
        attn = jax.nn.softmax(scores, axis=-1)
        ctx = jnp.einsum('bhqk,bhkd->bhqd', attn, v)
        ctx = ctx.transpose(0, 2, 1, 3).reshape(B, SQ, HIDDEN)
        return ctx @ Wo.T + bo

    def _L1_ffn_ref(x, router_w, up_proj, down_proj):
        import jax, jax.numpy as jnp
        import numpy as np
        E = 8
        H = 128
        D = 128
        TOP_K = 2
        B, T, _ = x.shape
        xt = x.reshape(-1, H)
        N = xt.shape[0]
        logits = jnp.einsum('nh,eh->ne', xt, router_w)
        probs = jax.nn.softmax(logits, axis=-1)
        scores, expert_idx = jax.lax.top_k(probs, TOP_K)
        scores = scores / jnp.sum(scores, axis=-1, keepdims=True)
        gate = jnp.zeros((N, E), dtype=xt.dtype).at[jnp.arange(N)[:, None], expert_idx].add(scores)
        h = jnp.einsum('nh,ehd->end', xt, up_proj)
        hidden = jax.nn.silu(h[..., :D]) * h[..., D:]
        out_e = jnp.einsum('end,edh->enh', hidden, down_proj)
        out = jnp.einsum('ne,enh->nh', gate, out_e)
        return out.reshape(B, T, H)
    x = x + jnp.tanh(g_xattn[0]) * _L0_xattn_ref(_layernorm(x, axis=-1), ctx_1024, L0_xattn_W, L0_xattn_b)
    x = x + jnp.tanh(g_ffn[0]) * _L0_ffn_ref(_layernorm(x, axis=-1), L0_ffn_input_ids, L0_ffn_gate_w, L0_ffn_gate_b, L0_ffn_w13, L0_ffn_w2, L0_ffn_w13_s, L0_ffn_w2_s)
    x = x + jnp.tanh(g_xattn[1]) * _L1_xattn_ref(_layernorm(x, axis=-1), ctx_1024, L1_xattn_Wq, L1_xattn_bq, L1_xattn_Wk, L1_xattn_bk, L1_xattn_Wv, L1_xattn_bv, L1_xattn_Wo, L1_xattn_bo)
    x = x + jnp.tanh(g_ffn[1]) * _L1_ffn_ref(_layernorm(x, axis=-1), L1_ffn_router_w, L1_ffn_up_proj, L1_ffn_down_proj)
    return x

_drawn_inputs = setup_inputs


def setup_inputs(seed=0):
    import zlib

    import numpy as np

    out = dict(_drawn_inputs(seed))
    spreads = {'g_ffn': (-1.0, 0.6),
     'L1_xattn_bq': (0.0, 2.0),
     'L1_xattn_bk': (0.0, 2.0),
     'L1_xattn_bv': (0.0, 0.573),
     'L1_xattn_bo': (0.0, 0.1)}
    factors = {'L0_ffn_gate_w': 7.774,
     'L0_ffn_gate_b': 6.525,
     'L0_ffn_w13': 8.0,
     'L0_ffn_w2': 5.705,
     'L0_ffn_w13_s': 5.518,
     'L0_ffn_w2_s': 6.466,
     'L1_xattn_Wq': 26.456,
     'L1_xattn_Wk': 24.902}
    for name, (base, spread) in spreads.items():
        noise = np.random.default_rng([zlib.crc32(name.encode()), seed]).standard_normal(out[name].shape)
        drawn = base * np.exp(spread * noise) if base else spread * noise
        out[name] = jnp.asarray(drawn.astype(out[name].dtype))
    for name, factor in factors.items():
        out[name] = (out[name] * factor).astype(out[name].dtype)
    return out
```

```python
from contextlib import ExitStack

import concourse.bass as bass
from concourse import mybir

F32 = mybir.dt.float32
F32R = mybir.dt.float32r
ALU = mybir.AluOpType
ACT = mybir.ActivationFunctionType
AX = mybir.AxisListType.X

P = 128
NB = 16
S = 77
GB = 4
NG = NB // GB
GT = GB * P
GS = GB * S
NH, HD = 16, 8
HG = 4
NHG = NH // HG
HK = NH * S
NC = -(-HK // P)
HV = HD + 1
VW = 3 * HV
EPS = 1e-5
START = 1
LOW = -1e30
GONE = -3e30
QSCALE = float(HD) ** -0.5


def chunk_rows(c):
    return min(P, HK - c * P)


def chunk_heads(c):
    first = c * P // S
    return first, (c * P + chunk_rows(c) - 1) // S - first + 1


def value_pieces():
    out = []
    for h in range(NH):
        k = 0
        while k < S:
            row = h * S + k
            n = min(S - k, P - row % P)
            out.append((h, row // P, row % P, k, n))
            k += n
    return out


class Moe:

    def __init__(self, name, phase, experts, topk, units, shared, scale, x_base, lo_base, route_base):
        self.name, self.phase, self.E, self.K = name, phase, experts, topk
        self.units, self.shared, self.scale = units, shared, scale
        self.H = units + shared
        self.W = experts + 8 - topk
        self.x_base, self.lo_base, self.route_base = x_base, lo_base, route_base


def flamingo(nc, x, ctx, g_xattn, g_ffn, w0, b0, gate_w, gate_b, w13, w2, w13_s, w2_s,
             wq, bq, wk, bk, wv, bv, wo, bo, router_w, up, down, ident, vs_seed, out):
    with ExitStack() as stack:
        at = [16512]

        def sb(name, shape, dt=F32, offset=None):
            size = 4
            for n in shape[1:]:
                size *= n
            if offset is None:
                offset = at[0]
                at[0] += -(-size // 32) * 32
            place[name] = offset
            return nc.alloc_sbuf_tensor_at(name, shape, dt, offset=offset)

        place = {}

        def psum(name, shape=(P, 512)):
            return stack.enter_context(nc.psum_tensor(name, list(shape), F32))

        def sem(name):
            return stack.enter_context(nc.semaphore(name))

        X = sb("X", [P, NB * P])
        xh = sb("xh", [P, 2 * GT], F32R)
        xl = sb("xl", [P, 2 * GT], F32R)
        xf = sb("xf", [P, GT], F32, place["xl"])
        w2raw = sb("w2raw", [P, NB * 64 + 128], F32, place["xh"])
        KS = sb("KS", [P, NB * HK], F32R)
        VS = sb("VS", [P, NB, NC * VW])
        WBH = sb("WBH", [P, 17 * P], F32R)
        WBL = sb("WBL", [P, 17 * P], F32R)
        UPH = sb("UPH", [P, 8 * 2 * P], F32R, place["WBH"])
        UPL = sb("UPL", [P, 8 * 2 * P], F32R, place["WBL"])
        W2T = sb("W2T", [P, 9, P])
        sg = sb("sg", [P, 2, GT])
        hb = sb("hb", [P, 2, GT])
        hs = sb("hs", [64, GT])
        w13raw = sb("w13raw", [P, 17 * P], F32, place["sg"])
        PX = sb("PX", [P, 2, HK], F32, place["sg"])
        kr = sb("kr", [P, NHG, NB * S])
        QS = sb("QS", [P, NHG * GT], F32R, place["kr"])
        CN = sb("CN", [P, NB, P])
        upraw = sb("upraw", [P, 8 * 2 * P], F32, place["CN"])
        cT = sb("cT", [P, NB * S])
        downw = sb("downw", [P, 8, P], F32, place["cT"])
        MT = sb("MT", [P, NB * S + 48])
        pt = sb("pt", [P, NC * P], F32, place["MT"])
        Vn = sb("Vn", [P, NB, P])
        bctx = sb("bctx", [1, NB * S])
        ct = sb("ct", [P, GT], F32R, place["bctx"])
        selB = sb("selB", [P, 16, 64], F32R, place["Vn"])
        selD = sb("selD", [16, 8], F32R)
        ql = sb("ql", [P, GT], F32R, place["QS"] + 4 * NHG * GT)
        RK = sb("RK", [P, NHG, 6, 32], F32R)
        RQ = sb("RQ", [P, NHG, 5, 32], F32R, None)
        I = sb("I", [P, P])
        xn = sb("xn", [P, GT])
        wraw = sb("wraw", [P, 4, P], F32, place["xn"])
        WX = sb("WX", [P, 3, P])
        WQH = sb("WQH", [P, P], F32R)
        WQL = sb("WQL", [P, P], F32R)
        W0 = sb("W0", [P, P])
        graw = sb("graw", [24, P])
        GWH = sb("GWH", [P, 24], F32R)
        GWL = sb("GWL", [P, 24], F32R)
        kf = sb("kf", [P, GS], F32, place["sg"])
        kh = sb("kh", [P, GS], F32R, place["sg"] + 1 * 1280)
        kl = sb("kl", [P, GS], F32R, place["sg"] + 2 * 1280)
        PA = sb("PA", [P, GS], F32, place["sg"] + 3 * 1280)
        ptA = sb("ptA", [S, GT], F32, place["sg"] + 4 * 1280)
        qf = sb("qf", [P, GT], F32, place["W2T"])
        qh = sb("qh", [P, GT], F32R, place["W2T"] + 4 * GT)
        On = sb("On", [P, P], F32, place["Vn"])
        OTs = sb("OTs", [P, P], F32, place["Vn"] + 4 * P)
        bvr = sb("bvr", [P, P])
        tgbo = sb("tgbo", [P, P])
        gbr = sb("gbr", [P, 16])
        mask4 = sb("mask4", [P, HG])
        ones = sb("ones", [1, P])
        cols = sb("cols", [P, 4])
        tg = sb("tg", [P, 4])
        mhalf = sb("mhalf", [P, GB])
        st = sb("st", [P, GB, 6])
        mv = sb("mv", [P, GB, 2])
        ve = sb("ve", [P, GB])
        rstd = sb("rstd", [P, GB])
        amax = sb("amax", [P, GB])
        asum = sb("asum", [P, 3, GB])
        cmx = sb("cmx", [P, NHG, HG])
        crs = sb("crs", [P, NH])
        lgT = sb("lgT", [16, GT], F32, place["bctx"] + 4 * GT)
        lgt = sb("lgt", [P, GB, 16])
        score = sb("score", [P, GB, 16])
        valsB = sb("valsB", [P, GB, 20])
        valsD = sb("valsD", [P, GB, 14])
        repB = sb("repB", [P, GB, 20])
        repD = sb("repD", [P, GB, 14])
        top = sb("top", [P, GB, 8])
        keepB = sb("keepB", [P, GB, 8])
        keepD = sb("keepD", [P, GB, 8])
        rsm = sb("rsm", [P, 2, GB])
        comb = sb("comb", [P, GB, 16])
        CH = sb("CH", [P, GB, 32], F32R)
        assert at[0] <= 229344, at[0]

        bank = [psum(f"bank{i}") for i in range(5)]
        Ybank = psum("Ybank", (P, 2 * 512))
        Tb = psum("Tb")
        Gb, Ub, Cb = bank[0:2], bank[2:4], bank[4]

        in_id, in_ctx, in_x, in_small, in_w = map(sem, ("in_id", "in_ctx", "in_x", "in_small", "in_w"))
        in_w13, in_w2, in_up, in_seed, in_vs = map(sem, ("in_w13", "in_w2", "in_up", "in_seed", "in_vs"))
        built = sem("built")
        d_set = sem("d_set")
        tg_rdy = sem("tg_rdy")
        su_mm, su_a, su_d = map(sem, ("su_mm", "su_a", "su_d"))
        stats, aggr, var_rdy, rstd_rdy, xn_rdy, xnT, xh_rdy, xl_rdy, x_done = map(sem, (
            "stats", "aggr", "var_rdy", "rstd_rdy", "xn_rdy", "xnT", "xh_rdy", "xl_rdy", "x_done"))
        a_sc, a_max, a_sub, a_exp, a_ptr, a_ptc, a_sum, a_rec, a_r, a_pv = map(sem, (
            "a_sc", "a_max", "a_sub", "a_exp", "a_ptr", "a_ptc", "a_sum", "a_rec", "a_r", "a_pv"))
        v_mm, v_done, k_mm, k_f, k_h, k_l, rk_mm, kr_done, ks_done = map(sem, (
            "v_mm", "v_done", "k_mm", "k_f", "k_h", "k_l", "rk_mm", "kr_done", "ks_done"))
        route = {n: sem("route_" + n) for n in (
            "mm", "act", "lgT", "exp", "mx", "sub", "score", "vals", "top", "keep", "rep", "msk", "w", "sum", "rec",
            "comb", "hi", "lo", "tr", "rdy")}
        q_mm, q_f, q_h, q_l, qs_mm, qs_done, bo_add = map(sem, (
            "q_mm", "q_f", "q_h", "q_l", "qs_mm", "qs_done", "bo_add"))
        c_sc, c_mx, c_sub, c_exp, c_tr, c_ev, c_pv, c_rs, c_norm, c_ot, c_otc, c_wo, c_fin = map(sem, (
            "c_sc", "c_mx", "c_sub", "c_exp", "c_tr", "c_ev", "c_pv", "c_rs", "c_norm", "c_ot",
            "c_otc", "c_wo", "c_fin"))
        up_split = sem("up_split")
        stored = sem("stored")

        mB = Moe("B", 1, 16, 4, 8, 1, 2.5, 4, 0, 0)
        mD = Moe("D", 3, 8, 2, 8, 0, 1.0, 8, 8, 4)
        for m in (mB, mD):
            m.g_done, m.u_done = sem(m.name + "_gate"), sem(m.name + "_up")
            m.c_done, m.dn = sem(m.name + "_spread"), sem(m.name + "_down")
            m.s_done, m.t2 = sem(m.name + "_silu"), sem(m.name + "_gated")
            m.h_done = sem(m.name + "_hidden")
            m.us_done, m.ss_done = sem(m.name + "_s_up"), sem(m.name + "_s_silu")
        mB.wh, mB.wl, mB.wd, mB.sel, mB.vals, mB.rep, mB.keep = WBH, WBL, W2T, selB, valsB, repB, keepB
        mD.wh, mD.wl, mD.wd, mD.sel, mD.vals, mD.rep, mD.keep = UPH, UPL, downw, selD, valsD, repD, keepD
        mB.gcol, mB.ucol = (lambda k: k * P), (lambda k: (8 + k) * P)
        mD.gcol, mD.ucol = (lambda k: 2 * k * P), (lambda k: (2 * k + 1) * P)
        mB.gw, mD.gw = 0, 16
        mB.crow, mD.crow = 96, 0
        mB.spread = lambda k: selB[96:P, 2 * k:2 * k + 2, :].rearrange("p e i -> p (e i)")
        mD.spread = lambda k: selD[:, k:k + 1].to_broadcast([16, P])
        mB.tg, mD.tg = 2, 3

        passed = {e: sem(f"passed_{n}") for e, n in (
            (nc.vector, "dve"), (nc.tensor, "pe"), (nc.gpsimd, "pool"))}

        def wait_apart(eng, semaphore, value):
            eng.wait_ge(semaphore, value)
            eng.sem_inc(passed[eng], 1)

        def slot(g):
            return (g % 2) * GT

        pieces = value_pieces()

        block = stack.enter_context(nc.Block())

        @block.sync
        def _(sp):
            sp.dma_start(I[:], ident).then_inc(in_id, 16)
            sp.dma_start(CN[0:S, :, :], ctx.rearrange("b s d -> s b d")).then_inc(in_ctx, 16)
            for g in range(NG):
                sp.dma_start(X[:, g * GT:(g + 1) * GT].rearrange("p (b d) -> p b d", b=GB),
                             x[g * GB:(g + 1) * GB].rearrange("b t d -> t b d")).then_inc(in_x, 16)
            sp.dma_start(w2raw[:, 0:NB * 64].rearrange("p (e i) -> p e i", e=16),
                         w2.rearrange("e d i -> d e i")).then_inc(in_w2, 16)
            for n in range(2):
                sp.dma_start(w2raw[:, NB * 64 + 64 * n:NB * 64 + 64 * n + 64], w2_s).then_inc(in_w2, 16)
            for b in range(NB):
                sp.dma_start(VS[:, b, :], vs_seed).then_inc(in_seed, 16)
            sp.wait_ge(in_seed, 16 * NB)
            sp.wait_ge(v_done, NG)
            for h, c, row, key, n in pieces:
                col = c * VW + (h - chunk_heads(c)[0]) * HV
                sp.dma_start(VS[row:row + n, :, col:col + HD],
                             Vn[key:key + n, :, h * HD:(h + 1) * HD]).then_inc(in_vs, 16)
            sp.wait_ge(a_pv, START + NG)
            sp.wait_ge(rk_mm, START + NG * NHG)
            sp.dma_start(upraw[:].rearrange("p (e n) -> p e n", e=8),
                         up.rearrange("e k n -> k e n")).then_inc(in_up, 16)
            sp.dma_start(downw[:], down.rearrange("e k n -> k e n")).then_inc(in_up, 16)
            for g in range(NG):
                sp.wait_ge(x_done, START + mD.x_base + g + 1)
                sp.dma_start(out[g * GB:(g + 1) * GB].rearrange("b t d -> t b d"),
                             X[:, g * GT:(g + 1) * GT].rearrange("p (b d) -> p b d", b=GB)).then_inc(stored, 16)
            sp.wait_ge(stored, 16 * NG)

        @block.gpsimd
        def _(pool):
            nc.gpsimd.memset(mhalf[:], -0.5)
            nc.gpsimd.memset(valsB[:], LOW)
            nc.gpsimd.memset(valsD[:], LOW)
            nc.gpsimd.memset(keepB[:], LOW)
            nc.gpsimd.memset(keepD[:], LOW)
            nc.gpsimd.memset(RK[:].bitcast(F32), 0.0)
            nc.gpsimd.memset(RQ[:].bitcast(F32), 0.0)
            nc.gpsimd.memset(ones[:], 1.0).then_inc(built, 1)

            def inv_std(n):
                pool.wait_ge(var_rdy, n)
                nc.gpsimd.tensor_tensor(rstd[:], ve[:], mhalf[:], ALU.pow).then_inc(rstd_rdy, 1)

            def spread_keys(g):
                for s in range(NHG):
                    keys = kr[:, s, bass.ds(g * GS, GS)].rearrange("p (b k) -> p b k", b=GB)
                    dst = KS[:, bass.ds(g * (GB * HK), GB * HK)].rearrange(
                        "p (b s h k) -> p b s h k", b=GB, s=NHG, h=HG)[:, :, s]
                    for h in range(HG):
                        nc.gpsimd.tensor_tensor(dst[:, :, h], keys,
                                                mask4[:, h:h + 1].unsqueeze(2).to_broadcast([P, GB, S]),
                                                ALU.mult).then_inc(ks_done, 1)

            pool.wait_ge(built, 1)
            with pool.Fori(0, NG + 1) as g:
                inv_std(g + 1)
            pool.wait_ge(d_set, 1)
            pool.wait_ge(kr_done, START + NG * NHG)
            with pool.Fori(0, NG) as g:
                inv_std(NG + g + 2)
                spread_keys(g)
            pool.wait_ge(mB.dn, START + NG * mB.H)
            pool.wait_ge(in_up, 32)
            for n in range(4):
                part = slice(n * 512, (n + 1) * 512)
                nc.gpsimd.tensor_copy(UPH[:, part], upraw[:, part]).then_inc(up_split, 1)
                pool.wait_ge(up_split, 2 * n + 1)
                nc.gpsimd.tensor_tensor(UPL[:, part], upraw[:, part], UPH[:, part].bitcast(F32),
                                        ALU.subtract).then_inc(up_split, 1)

            def add_bo(g):
                wait_apart(pool, xn_rdy, 2 * NG + g + 1)
                xg = X[:, bass.ds(g * GT, GT)].rearrange("p (b d) -> p b d", b=GB)
                nc.gpsimd.tensor_tensor(xg, xg, tgbo[:].unsqueeze(1).to_broadcast([P, GB, P]),
                                        ALU.add).then_inc(bo_add, 1)

            with pool.Fori(0, NG - 1) as g:
                add_bo(g)
                inv_std(2 * NG + g + 2)
            add_bo(NG - 1)
            with pool.Fori(0, NG) as g:
                inv_std(3 * NG + g + 1)

        @block.tensor
        def _(pe):
            mm, tr = nc.tensor.matmul, nc.tensor.transpose
            for s in (rk_mm, a_ptr, a_pv, mB.dn, mD.dn, c_tr, c_pv, c_ot, c_wo):
                pe.sem_inc(s, START)

            pe.wait_ge(in_id, 16)
            pe.wait_ge(in_ctx, 16)
            for g in range(NG):
                for b in range(GB):
                    i = tr(bank[g][:, b * S:(b + 1) * S], CN[0:S, g * GB + b, :], I[0:S, 0:S])
                i.then_inc(su_mm, 1)
            pe.wait_ge(in_w, 16 * 6)
            for n in range(4):
                i = tr(bank[4][:, n * P:(n + 1) * P], wraw[:, n, :], I[:])
            i.then_inc(su_mm, 1)
            i = tr(Tb[:, 0:24], graw[:], I[0:24, 0:24])
            i.then_inc(su_mm, 1)
            pe.wait_ge(in_small, 16 * 10)
            for g in range(NG):
                pe.wait_ge(su_a, g + 1)
                mm(bank[g][:, 0:GS], W0[:], cT[:, g * GS:(g + 1) * GS], start=True, stop=True).then_inc(su_mm, 1)
            for g in range(NG):
                if g == 0:
                    pe.wait_ge(su_d, 2)
                else:
                    pe.wait_ge(su_d, g + 2)
                mm(Tb[0:1, 0:GS], cols[:, 0:1], cT[:, g * GS:(g + 1) * GS], start=True, stop=True).then_inc(su_mm, 1)
            pe.wait_ge(in_w13, 16 * 6)
            for n in range(5):
                bk = bank[n % 4] if n < 4 else bank[4]
                pe.wait_ge(su_a, 7 + n if n < 4 else 10)
                for j in range(4 * n, min(17, 4 * n + 4)):
                    i = tr(bk[:, j % 4 * P:j % 4 * P + P], w13raw[:, j * P:(j + 1) * P], I[:])
                i.then_inc(su_mm, 1)
            pe.wait_ge(in_w2, 16 * 3)
            for n in range(3):
                pe.wait_ge(su_a, 11 + n)
                pe.wait_ge(su_d, 7 + n)
                for j in range(4 * n, min(9, 4 * n + 4)):
                    i = tr(bank[n][:, j % 4 * P:j % 4 * P + P], w2raw[:, j * P:(j + 1) * P], I[:])
                i.then_inc(su_mm, 1)
            for g in range(NG):
                pe.wait_ge(su_a, 16 + min(g, 2))
                pe.wait_ge(su_d, 11)
                for t in range(GB):
                    b = g * GB + t
                    i = mm(bank[g][0:S, t * P:(t + 1) * P], cT[:, b * S:(b + 1) * S], WX[:, 1, :], start=True, stop=True)
                i.then_inc(v_mm, 1)
            pe.wait_ge(v_done, NG)

            def norm_T(n):
                pe.wait_ge(xn_rdy, n)
                for t in range(GB):
                    i = tr(Tb[:, t * P:(t + 1) * P], xn[:, t * P:(t + 1) * P], I[:])
                i.then_inc(xnT, 1)

            bS, bT, bO = bank[0], bank[1], Ybank[:, 0:GT]

            def a_scores(g):
                pe.wait_ge(xh_rdy, g + 1)
                pe.wait_ge(a_sub, START + g)
                for t in range(GB):
                    c = g * GS + t * S
                    mm(bS[:, t * S:(t + 1) * S], ones[0:1, :], bctx[0:1, bass.ds(c, S)], start=True, stop=False)
                    i = mm(bS[:, t * S:(t + 1) * S], xf[:, t * P:(t + 1) * P], MT[:, bass.ds(c, S)],
                           start=False, stop=True)
                i.then_inc(a_sc, 1)

            bV = [bank[2], bank[3], bank[4], Ybank[:, GT:2 * GT]]

            def a_keys(g):
                pe.wait_ge(kr_done, START + NHG * g)
                mm(bV[1][:, 0:GS], WX[:, 0, :], cT[:, bass.ds(g * GS, GS)], start=True, stop=True).then_inc(k_mm, 1)

            def a_repeat(g):
                pe.wait_ge(k_l, g + 1)
                for s in range(NHG):
                    mm(bV[s][:, 0:GS], RK[:, s, 2:6, :].rearrange("p a b -> p (a b)"), kh[:], start=True, stop=False)
                    mm(bV[s][:, 0:GS], RK[:, s, 0:4, :].rearrange("p a b -> p (a b)"), kl[:],
                       start=False, stop=True).then_inc(rk_mm, 1)

            def a_probs_T(g):
                pe.wait_ge(a_exp, g + 1)
                pe.wait_ge(a_ptc, START + g)
                for t in range(GB):
                    i = tr(bT[0:S, t * P:(t + 1) * P], PA[:, t * S:(t + 1) * S], I[:])
                i.then_inc(a_ptr, 1)

            def a_mix(g):
                pe.wait_ge(a_ptc, START + g + 1)
                pe.wait_ge(x_done, START + g)
                for t in range(GB):
                    i = mm(bO[:, t * P:(t + 1) * P], ptA[:, t * P:(t + 1) * P],
                           CN[0:S, bass.ds(g * GB + t, 1), :].rearrange("p a d -> p (a d)"), start=True, stop=True)
                i.then_inc(a_pv, 1)

            pe.wait_ge(built, 1)
            pe.wait_ge(d_set, 1)
            norm_T(1)

            def a_body(g):
                a_scores(g)
                a_keys(g)
                a_probs_T(g)
                norm_T(g + 2)
                a_repeat(g)
                a_mix(g)

            with pe.Fori(0, NG) as g:
                a_body(g)

            def split3(dst, w, col, xs, inc):
                for n, (wp, xp) in enumerate(((w[0], xh), (w[0], xl), (w[1], xh))):
                    i = mm(dst, wp[:, col:col + P], xp[:, bass.ds(xs, GT)], start=n == 0, stop=n == 2)
                i.then_inc(inc, 1)

            def m_up(m, g, k, ring=True):
                if ring:
                    pe.wait_ge(m.t2, m.units * g + k - 1)
                if k == 0:
                    pe.wait_ge(xl_rdy, m.lo_base + g + 1)
                split3(Gb[k % 2][:], (m.wh, m.wl), m.gcol(k), slot(g), m.g_done)
                split3(Ub[k % 2][:], (m.wh, m.wl), m.ucol(k), slot(g), m.u_done)

            def m_spread(m, g, k):
                pe.wait_ge(m.h_done, START + m.H * g + k)
                if k == 0:
                    pe.wait_ge(route["rdy"], m.route_base + g + 1)
                mm(Cb[:], m.spread(k), ct[m.crow:m.crow + 2 * m.E, :], start=True, stop=True).then_inc(m.c_done, 1)

            def m_down(m, g, k):
                wait_apart(pe, m.h_done, START + m.H * g + k + 1)
                if k == 0:
                    pe.wait_ge(x_done, START + m.x_base + g - 1)
                rows = slice(0, 64) if k == m.units else slice(0, P)
                for t in range(GB):
                    lhs = hs[rows, t * P:(t + 1) * P] if k == m.units else hb[:, k % 2, t * P:(t + 1) * P]
                    i = mm(Ybank[:, bass.ds(slot(g) + t * P, P)], lhs, m.wd[rows, k, :],
                           start=(k == 0 and t == 0), stop=(k == m.H - 1), skip_group_check=True)
                i.then_inc(m.dn, 1)

            def m_logits(m, g):
                pe.wait_ge(xl_rdy, m.lo_base + g + 1)
                for n, (wp, xp) in enumerate(((GWH, xh), (GWH, xl), (GWL, xh))):
                    i = mm(Tb[0:m.E, :], wp[:, m.gw:m.gw + m.E], xp[:, bass.ds(slot(g), GT)], start=n == 0, stop=n == 2)
                i.then_inc(route["mm"], 1)

            def m_logits_T(m, g):
                wait_apart(pe, route["act"], m.route_base + g + 1)
                for t in range(GB):
                    i = tr(Tb[:, t * m.E:(t + 1) * m.E], lgT[0:m.E, t * P:(t + 1) * P], I[0:m.E, 0:m.E])
                i.then_inc(route["lgT"], 1)

            def m_route_T(m, g):
                pe.wait_ge(route["lo"], m.route_base + g + 1)
                for t in range(GB):
                    i = tr(Tb[0:2 * m.E, t * P:(t + 1) * P], CH[:, t, 0:2 * m.E].bitcast(F32), I[:])
                i.then_inc(route["tr"], 1)

            def m_body(m, g, nxt):
                more = nxt is not None and nxt[1] is m
                m_spread(m, g, 0)
                for k in range(m.units):
                    if k + 2 < m.units:
                        m_up(m, g, k + 2)
                    elif more:
                        m_up(m, g + 1, k + 2 - m.units)
                    if k + 1 < m.units:
                        m_spread(m, g, k + 1)
                    elif m.shared:
                        pe.wait_ge(m.h_done, START + m.H * g + m.units)
                        split3(Cb[:], (m.wh, m.wl), 2 * m.units * P, slot(g), m.us_done)
                    m_down(m, g, k)
                    if nxt is not None and k == 1:
                        norm_T(nxt[0])
                    if nxt is not None and nxt[1] is not None and k == 3:
                        m_logits(nxt[1], nxt[2])
                    if nxt is not None and nxt[1] is not None and k == 4:
                        m_logits_T(nxt[1], nxt[2])
                    if nxt is not None and nxt[1] is not None and k == m.units - 2:
                        m_route_T(nxt[1], nxt[2])
                if m.shared:
                    m_down(m, g, m.units)

            m = mB
            pe.wait_ge(kr_done, START + NG * NHG)
            m_logits(m, 0)
            m_up(m, 0, 0, ring=False)
            m_logits_T(m, 0)
            m_up(m, 0, 1, ring=False)
            m_route_T(m, 0)
            with pe.Fori(0, NG - 1) as g:
                m_body(m, g, (NG + g + 2, m, g + 1))
            m_body(m, NG - 1, (2 * NG + 1, None, 0))

            bS3 = [bank[0], bank[1], bank[2], bank[0]]
            bR = bank[3]
            bP = [bank[4], Ybank[:, 0:GT], bank[4]]
            bOut = Ybank[:, GT:2 * GT]

            def c_query(g):
                pe.wait_ge(xl_rdy, NG + g + 1)
                for n, (wp, xp) in enumerate(((WQH, xh), (WQH, xl), (WQL, xh))):
                    i = mm(Tb[:], wp[:], xp[:, bass.ds(slot(g), GT)], start=n == 0, stop=n == 2)
                i.then_inc(q_mm, 1)

            def c_repeat(g, s):
                if s == 0:
                    pe.wait_ge(q_l, g + 1)
                pe.wait_ge(qs_done, NHG * g + s)
                mm(Tb[:], RQ[:, s, 1:5, :].rearrange("p a b -> p (a b)"), qh[:], start=True, stop=False)
                mm(Tb[:], RQ[:, s, 0:4, :].rearrange("p a b -> p (a b)"), ql[:],
                   start=False, stop=True).then_inc(qs_mm, 1)

            def c_scores(g, t, s):
                n = GB * g + t
                if s == 0:
                    if t == 0:
                        pe.wait_ge(qs_done, NHG * g + NHG)
                    pe.wait_ge(c_sub, NHG * n)
                if s == 3:
                    pe.wait_ge(c_sub, NHG * n + 1)
                q = QS[:, s * GT + t * P:s * GT + (t + 1) * P]
                mm(bS3[s][:, 0:HG * S], q, KS[:, bass.ds(n * HK + s * HG * S, HG * S)],
                   start=True, stop=True).then_inc(c_sc, 1)

            need = [2, 4, 4]

            def c_transpose(g, t, r):
                n = GB * g + t
                pe.wait_ge(c_exp, NHG * n + need[r])
                pe.wait_ge(c_ev, START + 3 * n + (1 if r == 2 else 0))
                for c in range(4 * r, min(NC, 4 * r + 4)):
                    w = chunk_rows(c)
                    i = tr(bP[r][0:w, c % 4 * P:c % 4 * P + P], PX[:, t % 2, c * P:c * P + w], I[:])
                i.then_inc(c_tr, 1)

            def c_mix(g, t):
                n = GB * g + t
                pe.wait_ge(c_ev, START + 3 * n + 3)
                pe.wait_ge(c_norm, START + n)
                for c in range(NC):
                    w = chunk_rows(c)
                    h, nh = chunk_heads(c)
                    v = VS[0:w, bass.ds(n, 1), c * VW:c * VW + nh * HV].rearrange("p a d -> p (a d)")
                    i = mm(bOut[:, h * HV:(h + nh) * HV], pt[0:w, c * P:(c + 1) * P], v,
                           start=c == 0, stop=c == NC - 1, skip_group_check=True)
                i.then_inc(c_pv, 1)

            def c_out_T(g, t):
                n = GB * g + t
                pe.wait_ge(c_norm, START + n + 1)
                pe.wait_ge(c_fin, START + n)
                tr(bR[:, 0:P], On[:], I[:]).then_inc(c_ot, 1)

            def c_project(g, t):
                pe.wait_ge(c_otc, GB * g + t + 1)
                mm(bR[:, 2 * P:3 * P], OTs[:], WX[:, 2, :], start=True, stop=True).then_inc(c_wo, 1)

            def c_body(g, nxt):
                for t in range(GB):
                    n1 = (g, t + 1) if t + 1 < GB else (g + 1, 0)
                    ahead = t + 1 < GB or nxt is not None
                    for s in range(NHG):
                        if s < 3:
                            c_transpose(g, t, s)
                        if s == 3 and t:
                            c_out_T(g, t - 1)
                        if ahead:
                            c_scores(*n1, s)
                        if t == 2 and nxt is not None:
                            c_repeat(g + 1, s)
                    if t:
                        c_project(g, t - 1)
                    c_mix(g, t)
                    if t == 0:
                        norm_T(2 * NG + 2 + g)
                    if t == 1:
                        if nxt is not None:
                            c_query(g + 1)
                        else:
                            m_logits(mD, 0)
                    if t == 2 and nxt is None:
                        m_logits_T(mD, 0)
                c_out_T(g, GB - 1)
                c_project(g, GB - 1)

            c_query(0)
            for s in range(NHG):
                c_repeat(0, s)
            pe.wait_ge(ks_done, NG * NHG * HG)
            pe.wait_ge(in_vs, 16 * len(pieces))
            pe.wait_ge(x_done, START + 2 * NG)
            pe.wait_ge(mB.h_done, START + NG * mB.H)
            for s in range(NHG):
                c_scores(0, 0, s)
            with pe.Fori(0, NG - 1) as g:
                c_body(g, g + 1)
            c_body(NG - 1, None)
            m_route_T(mD, 0)

            m = mD
            pe.wait_ge(up_split, 8)
            pe.wait_ge(in_up, 32)
            pe.wait_ge(c_fin, START + NB)
            m_up(m, 0, 0, ring=False)
            m_up(m, 0, 1, ring=False)
            with pe.Fori(0, NG - 1) as g:
                m_body(m, g, (3 * NG + g + 2, m, g + 1))
            m_body(m, NG - 1, None)

        @block.scalar
        def _(act):
            A = nc.scalar.activation
            for s in (kr_done, a_ptc, c_ev):
                act.sem_inc(s, START)
            for n, w in enumerate((wq, wk, wv, wo)):
                act.dma_start(wraw[:, n, :], w).then_inc(in_w, 16)
            act.dma_start(graw[0:16, :], gate_w).then_inc(in_w, 16)
            act.dma_start(graw[16:24, :], router_w).then_inc(in_w, 16)
            act.dma_start(W0[:], w0).then_inc(in_small, 16)
            act.dma_start(cols[:, 0:1], b0.unsqueeze(1)).then_inc(in_small, 16)
            act.dma_start(cols[:, 1:2], bq.unsqueeze(1)).then_inc(in_small, 16)
            act.dma_start(cols[:, 2:3], bk.unsqueeze(1)).then_inc(in_small, 16)
            act.dma_start(cols[:, 3:4], bq.unsqueeze(1)).then_inc(in_small, 16)
            act.dma_start(tg[:, 0:2], g_xattn.partition_broadcast(P)).then_inc(in_small, 16)
            act.dma_start(tg[:, 2:4], g_ffn.partition_broadcast(P)).then_inc(in_small, 16)
            act.dma_start(bvr[:], bv.partition_broadcast(P)).then_inc(in_small, 16)
            act.dma_start(tgbo[:], bo.partition_broadcast(P)).then_inc(in_small, 16)
            act.dma_start(gbr[:], gate_b.partition_broadcast(P)).then_inc(in_small, 16)
            raw = w13raw[:, 0:16 * P].rearrange("p (u j d) -> p u j d", u=2, j=8)
            for e in range(2):
                for u in range(2):
                    src = w13[e::2, 64 * u:64 * u + 64, :].rearrange("j i d -> i j d")
                    act.dma_start(raw[64 * e:64 * e + 64, u], src).then_inc(in_w13, 16)
            act.dma_start(w13raw[0:64, 16 * P:17 * P], w13_s[64:P, :]).then_inc(in_w13, 16)
            act.dma_start(w13raw[64:P, 16 * P:17 * P], w13_s[0:64, :]).then_inc(in_w13, 16)

            act.wait_ge(in_small, 16 * 10)
            A(tg[:], tg[:], ACT.Tanh).then_inc(tg_rdy, 1)
            A(cols[:, 1:2], cols[:, 1:2], ACT.Copy, scale=QSCALE).then_inc(tg_rdy, 1)
            for g in range(NG):
                act.wait_ge(su_mm, g + 1)
                A(cT[:, g * GS:(g + 1) * GS], bank[g][:, 0:GS], ACT.Copy).then_inc(su_a, 1)
            act.wait_ge(su_mm, 5)
            A(WQH[:], bank[4][:, 0:P], ACT.Copy).then_inc(su_a, 1)
            A(WX[:].rearrange("p a d -> p (a d)"), bank[4][:, P:4 * P], ACT.Copy).then_inc(su_a, 1)
            for g in range(NG):
                act.wait_ge(su_mm, 7 + g)
                A(MT[:, g * GS:(g + 1) * GS], bank[g][:, 0:GS], ACT.Copy).then_inc(su_a, 1)
            for n in range(5):
                act.wait_ge(su_mm, 15 + n)
                w = (min(17, 4 * n + 4) - 4 * n) * P
                A(WBH[:, 4 * n * P:4 * n * P + w], bank[n][:, 0:w], ACT.Copy).then_inc(su_a, 1)
            for n in range(3):
                act.wait_ge(su_mm, 20 + n)
                w = min(9, 4 * n + 4) - 4 * n
                A(W2T[:, 4 * n:4 * n + w, :].rearrange("p a d -> p (a d)"), bank[n][:, 0:w * P],
                  ACT.Copy).then_inc(su_a, 1)

            def norm_hi(n, dst):
                act.wait_ge(xnT, n)
                A(dst, Tb[:], ACT.Copy).then_inc(xh_rdy, 1)

            norm_hi(1, xf[:])

            def a_body(g, last):
                act.wait_ge(a_sub, START + g + 1)
                A(PA[:], PA[:], ACT.Exp).then_inc(a_exp, 1)
                act.wait_ge(k_mm, g + 1)
                A(kf[:], bank[3][:, 0:GS], ACT.Identity, bias=cols[:, 2:3]).then_inc(k_f, 1)
                act.wait_ge(k_f, g + 1)
                act.wait_ge(rk_mm, START + NHG * g)
                A(kh[:], kf[:], ACT.Copy).then_inc(k_h, 1)
                act.wait_ge(a_ptr, START + g + 1)
                act.wait_ge(a_pv, START + g)
                A(ptA[:], bank[1][0:S, :], ACT.Copy).then_inc(a_ptc, 1)
                norm_hi(g + 2, xh[:, 0:GT] if last else xf[:])
                for s in range(NHG):
                    act.wait_ge(rk_mm, START + NHG * g + s + 1)
                    src = [bank[2], bank[3], bank[4], Ybank[:, GT:2 * GT]][s]
                    A(kr[:, s, bass.ds(g * GS, GS)], src[:, 0:GS], ACT.Copy).then_inc(kr_done, 1)

            with act.Fori(0, NG - 1) as g:
                a_body(g, False)
            a_body(NG - 1, True)

            def m_silu(m, g, k):
                act.wait_ge(m.g_done, m.units * g + k + 1)
                act.wait_ge(m.h_done, START + m.H * g + max(0, k - 1))
                A(sg[:, k % 2, :], Gb[k % 2][:], ACT.Silu).then_inc(m.s_done, 1)

            def m_route_act(m, g):
                act.wait_ge(route["mm"], m.route_base + g + 1)
                if m is mB:
                    A(lgT[0:m.E, :], Tb[0:m.E, :], ACT.Tanh, scale=0.5).then_inc(route["act"], 1)
                else:
                    A(lgT[0:m.E, :], Tb[0:m.E, :], ACT.Copy).then_inc(route["act"], 1)

            def m_route_exp(m, g):
                if m is mD:
                    act.wait_ge(route["sub"], g + 1)
                    A(score[:, :, 0:8], lgt[:, :, 0:8], ACT.Exp).then_inc(route["exp"], 1)

            def m_route_copy(m, g):
                act.wait_ge(route["tr"], m.route_base + g + 1)
                A(ct[m.crow:m.crow + 2 * m.E, :], Tb[0:2 * m.E, :], ACT.Copy).then_inc(route["rdy"], 1)

            def m_body(m, g, nxt):
                for k in range(m.units):
                    m_silu(m, g, k)
                    if nxt is not None and k == 2:
                        norm_hi(nxt[0], xh[:, bass.ds(slot(nxt[2]), GT)])
                    if nxt is not None and nxt[1] is not None and k == 4:
                        m_route_act(nxt[1], nxt[2])
                    if nxt is not None and nxt[1] is not None and k == 5:
                        m_route_exp(nxt[1], nxt[2])
                if m.shared:
                    act.wait_ge(m.us_done, g + 1)
                    act.wait_ge(m.dn, START + m.H * g)
                    A(hs[:], Cb[64:P, :], ACT.Silu).then_inc(m.ss_done, 1)
                if nxt is not None and nxt[1] is not None:
                    m_route_copy(nxt[1], nxt[2])

            m = mB
            m_route_act(m, 0)
            m_route_copy(m, 0)
            with act.Fori(0, NG - 1) as g:
                m_body(m, g, (NG + g + 2, m, g + 1))
            m_body(m, NG - 1, (2 * NG + 1, None, 0))

            def c_query(g):
                act.wait_ge(q_mm, g + 1)
                act.wait_ge(q_l, g)
                A(qf[:], Tb[:], ACT.Identity, bias=cols[:, 1:2], scale=QSCALE).then_inc(q_f, 1)

            def c_repeat(g, s):
                act.wait_ge(qs_mm, NHG * g + s + 1)
                A(QS[:, s * GT:(s + 1) * GT], Tb[:], ACT.Copy).then_inc(qs_done, 1)

            def c_exps(g, t, s):
                n = GB * g + t
                act.wait_ge(c_sub, NHG * n + s + 1)
                p = PX[:, t % 2, s * HG * S:(s + 1) * HG * S]
                A(p, p, ACT.Exp).then_inc(c_exp, 1)

            bPa = [bank[4], Ybank[:, 0:GT], bank[4]]

            def c_copy(g, t, r):
                n = GB * g + t
                act.wait_ge(c_tr, START + 3 * n + r + 1)
                act.wait_ge(c_pv, START + n)
                w = min(NC, 4 * r + 4) * P - 4 * r * P
                A(pt[:, 4 * r * P:4 * r * P + w], bPa[r][:, 0:w], ACT.Copy).then_inc(c_ev, 1)

            def c_out_copy(g, t):
                act.wait_ge(c_ot, START + GB * g + t + 1)
                act.wait_ge(c_wo, START + GB * g + t)
                A(OTs[:], bank[3][:, 0:P], ACT.Copy).then_inc(c_otc, 1)

            def c_body(g, more):
                for t in range(GB):
                    n1 = (g, t + 1) if t + 1 < GB else (g + 1, 0)
                    ahead = t + 1 < GB or more
                    for s in range(NHG):
                        if s < 3:
                            c_copy(g, t, s)
                        if s == 3 and t:
                            c_out_copy(g, t - 1)
                        if t == 2 and more:
                            c_repeat(g + 1, s)
                        if ahead:
                            c_exps(*n1, s)
                    if t == 0:
                        norm_hi(2 * NG + 2 + g, xh[:, bass.ds(slot(g + 1), GT)])
                    if t == 1 and more:
                        c_query(g + 1)
                    if t == 1 and not more:
                        m_route_act(mD, 0)
                    if t == 2 and not more:
                        m_route_exp(mD, 0)
                c_out_copy(g, GB - 1)

            c_query(0)
            act.wait_ge(ks_done, NG * NHG * HG)
            for s in range(NHG):
                c_repeat(0, s)
            for s in range(NHG):
                c_exps(0, 0, s)
            with act.Fori(0, NG - 1) as g:
                c_body(g, True)
            c_body(NG - 1, False)
            m_route_copy(mD, 0)

            m = mD
            with act.Fori(0, NG - 1) as g:
                m_body(m, g, (3 * NG + g + 2, m, g + 1))
            m_body(m, NG - 1, None)

        @block.vector
        def _(dve):
            V = nc.vector
            for s in (a_sub, x_done, mB.h_done, mD.h_done, c_norm, c_fin):
                dve.sem_inc(s, START)
            dve.wait_ge(in_id, 16)
            dve.wait_ge(built, 1)
            dve.wait_ge(in_small, 16 * 10)
            heads = I[:].rearrange("p (s r) -> p s r", s=NHG)
            for n in (2, 3):
                V.tensor_copy(RK[:, :, n, :], heads)
            for n in (3,):
                V.tensor_copy(RQ[:, :, n, :], heads)
            V.tensor_reduce(mask4[:], I[:].rearrange("p (t h d) -> p h t d", t=4, h=HG), mybir.AxisListType.XY, ALU.add)
            V.tensor_tensor(selB[96:P], I[96:P, 96:112].unsqueeze(2).to_broadcast([32, 16, 64]),
                            I[96:P, 112:P].unsqueeze(2).to_broadcast([32, 16, 64]), ALU.add)
            V.tensor_tensor(selD[:], I[0:16, 0:8], I[0:16, 8:16], ALU.add)
            V.tensor_copy(RQ[:, :, 1, :], heads).then_inc(d_set, 1)
            dve.wait_ge(tg_rdy, 1)
            V.tensor_scalar(tgbo[:], tgbo[:], tg[:, 1:2], None, ALU.mult).then_inc(d_set, 1)
            dve.wait_ge(su_a, 6)
            V.tensor_tensor(WQL[:], bank[4][:, 0:P], WQH[:].bitcast(F32), ALU.subtract).then_inc(su_d, 1)
            dve.wait_ge(su_mm, 6)
            V.tensor_copy(GWH[:], Tb[:, 0:24]).then_inc(d_set, 1)
            dve.wait_ge(d_set, 3)
            V.tensor_tensor(GWL[:], Tb[:, 0:24], GWH[:].bitcast(F32), ALU.subtract).then_inc(su_d, 1)
            for g in range(NG):
                dve.wait_ge(su_mm, 11 + g)
                V.tensor_copy(bctx[0:1, g * GS:(g + 1) * GS], Tb[0:1, 0:GS]).then_inc(su_d, 1)
            for n in range(5):
                dve.wait_ge(su_a, 11 + n)
                w = (min(17, 4 * n + 4) - 4 * n) * P
                c = 4 * n * P
                V.tensor_tensor(WBL[:, c:c + w], bank[n][:, 0:w], WBH[:, c:c + w].bitcast(F32),
                                ALU.subtract).then_inc(su_d, 1)
            for g in range(NG):
                dve.wait_ge(v_mm, g + 1)
                V.tensor_tensor(Vn[0:S, g * GB:(g + 1) * GB, :], bank[g][0:S, :].rearrange("p (b d) -> p b d", b=GB),
                                bvr[0:S, :].unsqueeze(1).to_broadcast([S, GB, P]), ALU.add).then_inc(v_done, 1)

            def xt(g, t):
                return X[:, bass.ds(g * GT + t * P, P)]

            def norm_stats(n, g):
                for t in range(GB):
                    i = V.bn_stats(st[:, t, :], xt(g, t))
                i.then_inc(stats, 1)
                wait_apart(dve, stats, n)
                for t in range(GB):
                    i = V.bn_aggr(mv[:, t, :], st[:, t, :])
                i.then_inc(aggr, 1)
                dve.wait_ge(aggr, n)
                V.tensor_scalar(ve[:], mv[:, :, 1], EPS, None, ALU.add).then_inc(var_rdy, 1)

            def norm_apply(n, g, first=False):
                dve.wait_ge(rstd_rdy, n)
                if not first:
                    dve.wait_ge(xnT, n - 1)
                for t in range(GB):
                    i = V.tensor_scalar(xn[:, t * P:(t + 1) * P], xt(g, t), mv[:, t, 0:1], rstd[:, t:t + 1],
                                        ALU.subtract, ALU.mult)
                i.then_inc(xn_rdy, 1)

            def norm_lo(n, g):
                dve.wait_ge(xh_rdy, n)
                V.tensor_tensor(xl[:, bass.ds(slot(g), GT)], Tb[:], xh[:, bass.ds(slot(g), GT)].bitcast(F32),
                                ALU.subtract).then_inc(xl_rdy, 1)

            dve.wait_ge(in_x, 16 * NG)
            dve.wait_ge(su_mm, 5)
            norm_stats(1, 0)
            norm_apply(1, 0, first=True)

            def a_body(g, nxt, last):
                dve.wait_ge(a_sc, g + 1)
                sc = bank[0][:, 0:GS].rearrange("p (t k) -> p t k", t=GB)
                pa = PA[:].rearrange("p (t k) -> p t k", t=GB)
                V.reduce_max(amax[:], sc, AX).then_inc(a_max, 1)
                dve.wait_ge(a_max, g + 1)
                dve.wait_ge(a_ptr, START + g)
                V.tensor_tensor(pa, sc, amax[:].unsqueeze(2).to_broadcast([P, GB, S]), ALU.subtract).then_inc(a_sub, 1)
                if last:
                    dve.wait_ge(x_done, START + 1)
                norm_stats(g + 2, nxt)
                dve.wait_ge(a_exp, g + 1)
                V.reduce_sum(asum[:, 0, :], pa, AX).then_inc(a_sum, 1)
                norm_apply(g + 2, nxt)
                dve.wait_ge(a_sum, g + 1)
                V.reciprocal(asum[:, 1, :], asum[:, 0, :]).then_inc(a_rec, 1)
                dve.wait_ge(k_h, g + 1)
                V.tensor_tensor(kl[:], kf[:], kh[:].bitcast(F32), ALU.subtract).then_inc(k_l, 1)
                dve.wait_ge(a_rec, g + 1)
                V.tensor_scalar(asum[:, 2, :], asum[:, 1, :], tg[:, 0:1], None, ALU.mult).then_inc(a_r, 1)
                dve.wait_ge(a_r, g + 1)
                dve.wait_ge(a_pv, START + g + 1)
                for t in range(GB):
                    i = V.scalar_tensor_tensor(out=xt(g, t), in0=Ybank[:, t * P:(t + 1) * P],
                                               scalar=asum[:, 2, t:t + 1], in1=xt(g, t), op0=ALU.mult, op1=ALU.add)
                i.then_inc(x_done, 1)

            with dve.Fori(0, NG - 1) as g:
                a_body(g, g + 1, False)
            a_body(NG - 1, 0, True)
            norm_lo(NG + 1, 0)

            def route_vals(m, g):
                n = m.route_base + g + 1
                if m is mB:
                    dve.wait_ge(route["lgT"], n)
                    V.tensor_scalar(score[:], Tb[:, 0:GB * 16].rearrange("p (t e) -> p t e", t=GB), 0.5, 0.5, ALU.mult, ALU.add).then_inc(route["score"], 1)
                    dve.wait_ge(route["score"], n)
                    V.tensor_tensor(m.vals[:, :, 0:m.E], score[:], gbr[:].unsqueeze(1).to_broadcast([P, GB, 16]),
                                    ALU.add).then_inc(route["vals"], 1)
                else:
                    dve.wait_ge(route["exp"], g + 1)
                    V.tensor_copy(m.vals[:, :, 0:m.E], score[:, :, 0:8]).then_inc(route["vals"], 1)

            def route_sub(g):
                dve.wait_ge(route["lgT"], mD.route_base + g + 1)
                lg = Tb[:, 0:GB * 8].rearrange("p (t e) -> p t e", t=GB)
                V.reduce_max(rsm[:, 0, :], lg, AX).then_inc(route["mx"], 1)
                dve.wait_ge(route["mx"], g + 1)
                V.tensor_tensor(lgt[:, :, 0:8], lg, rsm[:, 0, :].unsqueeze(2).to_broadcast([P, GB, 8]),
                                ALU.subtract).then_inc(route["sub"], 1)

            def route_pick(m, g):
                n = m.route_base + g + 1
                wait_apart(dve, route["vals"], n)
                for t in range(GB):
                    i = V.max(top[:, t, :], m.vals[:, t, :])
                i.then_inc(route["top"], 1)
                dve.wait_ge(route["top"], n)
                V.tensor_copy(m.keep[:, :, 0:m.K], top[:, :, 0:m.K]).then_inc(route["keep"], 1)
                wait_apart(dve, route["keep"], n)
                for t in range(GB):
                    i = V.match_replace(m.rep[:, t, :], m.keep[:, t, :], m.vals[:, t, :], GONE)
                i.then_inc(route["rep"], 1)

            def route_weights(m, g):
                n = m.route_base + g + 1
                E = m.E
                dve.wait_ge(route["rep"], n)
                V.tensor_tensor(comb[:, :, 0:E], m.rep[:, :, 0:E], m.vals[:, :, 0:E], ALU.is_lt).then_inc(route["msk"], 1)
                dve.wait_ge(route["msk"], n)
                V.tensor_tensor(comb[:, :, 0:E], comb[:, :, 0:E], score[:, :, 0:E], ALU.mult).then_inc(route["w"], 1)
                dve.wait_ge(route["w"], n)
                V.reduce_sum(rsm[:, 0, :], comb[:, :, 0:E], AX).then_inc(route["sum"], 1)
                dve.wait_ge(route["sum"], n)
                V.reciprocal(rsm[:, 1, :], rsm[:, 0, :]).then_inc(route["rec"], 1)
                dve.wait_ge(route["rec"], n)
                V.scalar_tensor_tensor(out=comb[:, :, 0:E], in0=comb[:, :, 0:E], scalar=m.scale,
                                       in1=rsm[:, 1, :].unsqueeze(2).to_broadcast([P, GB, E]),
                                       op0=ALU.mult, op1=ALU.mult).then_inc(route["comb"], 1)
                dve.wait_ge(route["comb"], n)
                V.tensor_copy(CH[:, :, 0:E], comb[:, :, 0:E]).then_inc(route["hi"], 1)
                dve.wait_ge(route["hi"], n)
                V.tensor_tensor(CH[:, :, E:2 * E], comb[:, :, 0:E], CH[:, :, 0:E].bitcast(F32),
                                ALU.subtract).then_inc(route["lo"], 1)

            def m_hidden(m, g, k):
                dve.wait_ge(m.s_done, m.units * g + k + 1)
                dve.wait_ge(m.u_done, m.units * g + k + 1)
                V.tensor_tensor(sg[:, k % 2, :], sg[:, k % 2, :], Ub[k % 2][:], ALU.mult).then_inc(m.t2, 1)
                dve.wait_ge(m.t2, m.units * g + k + 1)
                dve.wait_ge(m.c_done, m.units * g + k + 1)
                dve.wait_ge(m.dn, START + m.H * g + max(0, k - 1))
                V.tensor_tensor(hb[:, k % 2, :], sg[:, k % 2, :], Cb[:], ALU.mult).then_inc(m.h_done, 1)

            def m_body(m, g, nxt):
                for k in range(m.units):
                    m_hidden(m, g, k)
                    if nxt is None:
                        continue
                    n, nm, ng = nxt
                    if k == 0:
                        norm_stats(n, ng)
                    if k == 1:
                        norm_apply(n, ng)
                    if k == 2:
                        norm_lo(n, ng)
                    if nm is mD and k == 4:
                        route_sub(ng)
                    if nm is not None and k == 5:
                        route_vals(nm, ng)
                        route_pick(nm, ng)
                        route_weights(nm, ng)
                if m.shared:
                    dve.wait_ge(m.ss_done, g + 1)
                    V.tensor_tensor(hs[:], hs[:], Cb[0:64, :], ALU.mult).then_inc(m.h_done, 1)
                dve.wait_ge(m.dn, START + m.H * g + m.H)
                for t in range(GB):
                    i = V.scalar_tensor_tensor(out=xt(g, t), in0=Ybank[:, bass.ds(slot(g) + t * P, P)],
                                               scalar=tg[:, m.tg:m.tg + 1], in1=xt(g, t), op0=ALU.mult, op1=ALU.add)
                i.then_inc(x_done, 1)

            m = mB
            route_vals(m, 0)
            route_pick(m, 0)
            route_weights(m, 0)
            with dve.Fori(0, NG - 1) as g:
                m_body(m, g, (NG + g + 2, m, g + 1))
            m_body(m, NG - 1, (2 * NG + 1, None, 0))

            def c_split(g):
                dve.wait_ge(q_f, g + 1)
                dve.wait_ge(qs_mm, NHG * g)
                V.tensor_copy(qh[:], qf[:]).then_inc(q_h, 1)
                dve.wait_ge(q_h, g + 1)
                V.tensor_tensor(ql[:], qf[:], qh[:].bitcast(F32), ALU.subtract).then_inc(q_l, 1)

            bSd = [bank[0], bank[1], bank[2], bank[0]]

            def c_center(g, t, s, first=False):
                n = GB * g + t
                sc = bSd[s][:, 0:HG * S].rearrange("p (h k) -> p h k", h=HG)
                dve.wait_ge(c_sc, NHG * n + s + 1)
                V.reduce_max(cmx[:, s, :], sc, AX).then_inc(c_mx, 1)
                dve.wait_ge(c_mx, NHG * n + s + 1)
                if not first:
                    dve.wait_ge(c_tr, START + 3 * n - 3)
                V.tensor_tensor(PX[:, t % 2, s * HG * S:(s + 1) * HG * S].rearrange("p (h k) -> p h k", h=HG), sc,
                                cmx[:, s, :].unsqueeze(2).to_broadcast([P, HG, S]), ALU.subtract).then_inc(c_sub, 1)

            def c_normalize(g, t):
                n = GB * g + t
                o = Ybank[:, GT:GT + NH * HV].rearrange("p (h d) -> p h d", h=NH)
                dve.wait_ge(c_pv, START + n + 1)
                V.reciprocal(crs[:].unsqueeze(2), o[:, :, HD:HV]).then_inc(c_rs, 1)
                dve.wait_ge(c_rs, n + 1)
                dve.wait_ge(c_ot, START + n)
                V.tensor_tensor(On[:].rearrange("p (h d) -> p h d", h=NH), o[:, :, 0:HD],
                                crs[:].unsqueeze(2).to_broadcast([P, NH, HD]), ALU.mult).then_inc(c_norm, 1)

            def c_final(g, t):
                n = GB * g + t
                if t == 0:
                    dve.wait_ge(bo_add, g + 1)
                dve.wait_ge(c_wo, START + n + 1)
                V.scalar_tensor_tensor(out=xt(g, t), in0=bank[3][:, 2 * P:3 * P], scalar=tg[:, 1:2], in1=xt(g, t),
                                       op0=ALU.mult, op1=ALU.add).then_inc(c_fin, 1)

            def c_body(g, more):
                nxt = g + 1 if more else 0
                for t in range(GB):
                    n1 = (g, t + 1) if t + 1 < GB else (g + 1, 0)
                    ahead = t + 1 < GB or more
                    if t == 1:
                        norm_lo(2 * NG + 2 + g, g + 1)
                    for s in range(NHG):
                        if ahead:
                            c_center(*n1, s)
                        if s == 2 and t:
                            c_final(g, t - 1)
                        if s == 1 and t == 0:
                            norm_stats(2 * NG + 2 + g, nxt)
                        if s == 3 and t == 0:
                            norm_apply(2 * NG + 2 + g, nxt)
                        if s == 3 and t == 1 and more:
                            pass
                    c_normalize(g, t)
                    if t == 1 and more:
                        c_split(g + 1)
                    if t == 2 and not more:
                        route_sub(0)
                        route_vals(mD, 0)
                        route_pick(mD, 0)
                        route_weights(mD, 0)
                c_final(g, GB - 1)

            dve.wait_ge(ks_done, NG * NHG * HG)
            c_split(0)
            for s in range(NHG):
                c_center(0, 0, s, first=True)
            with dve.Fori(0, NG - 1) as g:
                c_body(g, True)
            c_body(NG - 1, False)

            m = mD
            with dve.Fori(0, NG - 1) as g:
                m_body(m, g, (3 * NG + g + 2, m, g + 1))
            m_body(m, NG - 1, None)


_INS = ['x', 'ctx_1024', 'g_xattn', 'g_ffn', 'L0_xattn_W', 'L0_xattn_b', 'L0_ffn_gate_w', 'L0_ffn_gate_b',
        'L0_ffn_w13', 'L0_ffn_w2', 'L0_ffn_w13_s', 'L0_ffn_w2_s', 'L1_xattn_Wq', 'L1_xattn_bq', 'L1_xattn_Wk',
        'L1_xattn_bk', 'L1_xattn_Wv', 'L1_xattn_bv', 'L1_xattn_Wo', 'L1_xattn_bo', 'L1_ffn_router_w',
        'L1_ffn_up_proj', 'L1_ffn_down_proj']


def kernel(**inputs):
    import numpy as _np
    import concourse.bacc as _bacc
    from concourse import mybir as _mybir
    from concourse.bass_utils import run_bass_kernel_spmd as _run

    seed = _np.zeros((P, NC * VW), _np.float32)
    for h, c, row, _, n in value_pieces():
        seed[row:row + n, c * VW + (h - chunk_heads(c)[0]) * HV + HD] = 1.0
    consts = {'ident': _np.eye(P, dtype=_np.float32), 'vs_seed': seed}

    nc = _bacc.Bacc("TRN2", target_bir_lowering=False, num_devices=1)
    arrays, args = {}, []
    for name in _INS + list(consts):
        a = _np.ascontiguousarray(consts[name] if name in consts else inputs[name])
        arrays[f"in_{name}"] = a
        args.append(nc.dram_tensor(f"in_{name}", a.shape, _mybir.dt.from_np(a.dtype), kind="ExternalInput").ap())
    args.append(nc.dram_tensor("out_x", (NB, P, P), _mybir.dt.float32, kind="ExternalOutput").ap())
    flamingo(nc, *args)
    r = _run(nc, [arrays], core_ids=[0])
    return r.results[0]["out_x"]
```

```python
from contextlib import ExitStack

import concourse.bass as bass
from concourse import mybir

F32 = mybir.dt.float32
F32R = mybir.dt.float32r
ALU = mybir.AluOpType
ACT = mybir.ActivationFunctionType
AX = mybir.AxisListType.X

P = 128
NB = 16
S = 77
GB = 4
NG = NB // GB
GT = GB * P
GS = GB * S
NH, HD = 16, 8
HG = 4
NHG = NH // HG
HK = NH * S
NU = 2
UH = NH // NU
UK = UH * S
UD = UH * HD
CU = -(-UK // P)
NC = NU * CU
VW = 3 * HD
EPS = 1e-5
START = 1
LOW = -1e30
GONE = -3e30
SUB_EXP = (0, 2)
BIAS_EXP = (1, 3)
QSCALE = float(HD) ** -0.5


def chunk_rows(c):
    return min(P, UK - c % CU * P)


def chunk_col(c):
    return c // CU * UK + c % CU * P


def chunk_head(c):
    return c % CU * P // S


def value_pieces():
    out = []
    for h in range(NH):
        k = 0
        while k < S:
            at = h % UH * S + k
            n = min(S - k, P - at % P)
            out.append((h, h // UH * CU + at // P, at % P, k, n))
            k += n
    return out


class Moe:

    def __init__(self, name, phase, experts, topk, units, shared, scale, x_base, lo_base, route_base):
        self.name, self.phase, self.E, self.K = name, phase, experts, topk
        self.units, self.shared, self.scale = units, shared, scale
        self.H = units + shared
        self.W = experts + 8 - topk
        self.x_base, self.lo_base, self.route_base = x_base, lo_base, route_base


def flamingo(nc, x, ctx, g_xattn, g_ffn, w0, b0, gate_w, gate_b, w13, w2, w13_s, w2_s,
             wq, bq, wk, bk, wv, bv, wo, bo, router_w, up, down, ident, vs_seed, out):
    with ExitStack() as stack:
        at = [16512]

        def sb(name, shape, dt=F32, offset=None):
            size = 4
            for n in shape[1:]:
                size *= n
            if offset is None:
                offset = at[0]
                at[0] += -(-size // 32) * 32
            place[name] = offset
            return nc.alloc_sbuf_tensor_at(name, shape, dt, offset=offset)

        place = {}

        def psum(name, shape=(P, 512)):
            return stack.enter_context(nc.psum_tensor(name, list(shape), F32))

        def sem(name):
            return stack.enter_context(nc.semaphore(name))

        X = sb("X", [P, NB * P])
        xh = sb("xh", [P, 2 * GT], F32R)
        xl = sb("xl", [P, 2 * GT], F32R)
        xf = sb("xf", [P, GT], F32, place["xl"])
        w2raw = sb("w2raw", [P, NB * 64 + 128], F32, place["xh"])
        KS = sb("KS", [P, NB * HK], F32R)
        VS = sb("VS", [P, NB, NC * VW])
        WBH = sb("WBH", [P, 17 * P], F32R)
        WBL = sb("WBL", [P, 17 * P], F32R)
        UPH = sb("UPH", [P, 8 * 2 * P], F32R, place["WBH"])
        UPL = sb("UPL", [P, 8 * 2 * P], F32R, place["WBL"])
        W2T = sb("W2T", [P, 9, P])
        sg = sb("sg", [P, 2, GT])
        hb = sb("hb", [P, 2, GT])
        hs = sb("hs", [64, GT])
        w13raw = sb("w13raw", [P, 17 * P], F32, place["sg"])
        PX = sb("PX", [P, 2, HK], F32, place["sg"])
        kr = sb("kr", [P, NHG, NB * S])
        QS = sb("QS", [P, NHG * GT], F32R, place["kr"])
        VX = sb("VX", [P, 2 * NC * P + 320], F32, place["kr"] + 4 * NHG * GT)
        CN = sb("CN", [P, NB, P])
        upraw = sb("upraw", [P, 8 * 2 * P], F32, place["CN"])
        cT = sb("cT", [P, NB * S])
        downw = sb("downw", [P, 8, P], F32, place["cT"])
        MT = sb("MT", [P, NB * S + 48])
        pt = sb("pt", [P, NC * P], F32, place["MT"])
        Vn = sb("Vn", [P, NB, P])
        bctx = sb("bctx", [1, NB * S])
        ct = sb("ct", [P, GT], F32R, place["bctx"])
        selB = sb("selB", [P, 16, 64], F32R, place["Vn"])
        selD = sb("selD", [16, 8], F32R)
        ql = sb("ql", [P, GT], F32R, place["ct"])
        RK = sb("RK", [P, NHG, 6, 32], F32R)
        RQ = sb("RQ", [P, NHG, 5, 32], F32R, None)
        I = sb("I", [P, P])
        xn = sb("xn", [P, GT])
        wraw = sb("wraw", [P, 4, P], F32, place["xn"])
        WX = sb("WX", [P, 3, P])
        WQH = sb("WQH", [P, P], F32R)
        WQL = sb("WQL", [P, P], F32R)
        W0 = sb("W0", [P, P])
        graw = sb("graw", [24, P])
        GWH = sb("GWH", [P, 24], F32R)
        GWL = sb("GWL", [P, 24], F32R)
        kf = sb("kf", [P, GS], F32, place["sg"])
        kh = sb("kh", [P, GS], F32R, place["sg"] + 1 * 1280)
        kl = sb("kl", [P, GS], F32R, place["sg"] + 2 * 1280)
        PA = sb("PA", [P, GS], F32, place["sg"] + 3 * 1280)
        ptA = sb("ptA", [S, GT], F32, place["sg"] + 4 * 1280)
        qf = sb("qf", [P, GT], F32, place["W2T"])
        qh = sb("qh", [P, GT], F32R, place["W2T"] + 4 * GT)
        sumT = sb("sumT", [P, P], F32, place["Vn"])
        recT = sb("recT", [P, P], F32, place["Vn"] + 4 * P)
        OTs = sb("OTs", [P, P], F32, place["Vn"] + 8 * P)
        bvr = sb("bvr", [P, P])
        tgbo = sb("tgbo", [P, P])
        gbr = sb("gbr", [P, 16])
        mask4 = sb("mask4", [P, HG])
        ones = sb("ones", [1, P])
        cols = sb("cols", [P, 4])
        tg = sb("tg", [P, 4])
        mhalf = sb("mhalf", [P, GB])
        st = sb("st", [P, GB, 6])
        mv = sb("mv", [P, GB, 2])
        ve = sb("ve", [P, GB])
        rstd = sb("rstd", [P, GB])
        amax = sb("amax", [P, GB])
        asum = sb("asum", [P, 3, GB])
        cmx = sb("cmx", [P, NHG, HG])
        lgT = sb("lgT", [16, GT], F32, place["bctx"] + 4 * GT)
        lgt = sb("lgt", [P, GB, 16])
        score = sb("score", [P, GB, 16])
        valsB = sb("valsB", [P, GB, 20])
        valsD = sb("valsD", [P, GB, 14])
        repB = sb("repB", [P, GB, 20])
        repD = sb("repD", [P, GB, 14])
        top = sb("top", [P, GB, 8])
        keepB = sb("keepB", [P, GB, 8])
        keepD = sb("keepD", [P, GB, 8])
        rsm = sb("rsm", [P, 2, GB])
        comb = sb("comb", [P, GB, 16])
        CH = sb("CH", [P, GB, 32], F32R)
        assert at[0] <= 229344, at[0]

        bank = [psum(f"bank{i}") for i in range(5)]
        Ybank = psum("Ybank", (P, 2 * 512))
        Tb = psum("Tb")
        Gb, Ub, Cb = bank[0:2], bank[2:4], bank[4]

        in_id, in_ctx, in_x, in_small, in_w = map(sem, ("in_id", "in_ctx", "in_x", "in_small", "in_w"))
        in_w13, in_w2, in_up, in_seed, in_vs = map(sem, ("in_w13", "in_w2", "in_up", "in_seed", "in_vs"))
        built = sem("built")
        d_set = sem("d_set")
        tg_rdy = sem("tg_rdy")
        su_mm, su_a, su_d = map(sem, ("su_mm", "su_a", "su_d"))
        stats, aggr, var_rdy, rstd_rdy, xn_rdy, xnT, xh_rdy, xl_rdy, x_done = map(sem, (
            "stats", "aggr", "var_rdy", "rstd_rdy", "xn_rdy", "xnT", "xh_rdy", "xl_rdy", "x_done"))
        a_sc, a_max, a_sub, a_exp, a_ptr, a_ptc, a_sum, a_rec, a_r, a_pv = map(sem, (
            "a_sc", "a_max", "a_sub", "a_exp", "a_ptr", "a_ptc", "a_sum", "a_rec", "a_r", "a_pv"))
        v_mm, v_done, k_mm, k_f, k_h, k_l, rk_mm, kr_done, ks_done = map(sem, (
            "v_mm", "v_done", "k_mm", "k_f", "k_h", "k_l", "rk_mm", "kr_done", "ks_done"))
        route = {n: sem("route_" + n) for n in (
            "mm", "act", "lgT", "exp", "mx", "sub", "score", "vals", "top", "keep", "rep", "msk", "w", "sum", "rec",
            "comb", "hi", "lo", "tr", "rdy")}
        q_mm, q_f, q_h, q_l, qs_mm, qs_done, bo_add = map(sem, (
            "q_mm", "q_f", "q_h", "q_l", "qs_mm", "qs_done", "bo_add"))
        c_sc, c_mx, c_sub, c_exp, c_tr, c_ev, c_pv, c_sum, c_rs, c_norm, c_wo, c_fin = map(sem, (
            "c_sc", "c_mx", "c_sub", "c_exp", "c_tr", "c_ev", "c_pv", "c_sum", "c_rs", "c_norm", "c_wo", "c_fin"))
        vs_zero, vx_rdy, wo_rdy = sem("vs_zero"), sem("vx_rdy"), sem("wo_rdy")
        up_split = sem("up_split")
        stored = sem("stored")

        mB = Moe("B", 1, 16, 4, 8, 1, 2.5, 4, 0, 0)
        mD = Moe("D", 3, 8, 2, 8, 0, 1.0, 8, 8, 4)
        for m in (mB, mD):
            m.g_done, m.u_done = sem(m.name + "_gate"), sem(m.name + "_up")
            m.c_done, m.dn = sem(m.name + "_spread"), sem(m.name + "_down")
            m.s_done, m.t2 = sem(m.name + "_silu"), sem(m.name + "_gated")
            m.h_done = sem(m.name + "_hidden")
            m.us_done, m.ss_done = sem(m.name + "_s_up"), sem(m.name + "_s_silu")
        mB.wh, mB.wl, mB.wd, mB.sel, mB.vals, mB.rep, mB.keep = WBH, WBL, W2T, selB, valsB, repB, keepB
        mD.wh, mD.wl, mD.wd, mD.sel, mD.vals, mD.rep, mD.keep = UPH, UPL, downw, selD, valsD, repD, keepD
        mB.gcol, mB.ucol = (lambda k: k * P), (lambda k: (8 + k) * P)
        mD.gcol, mD.ucol = (lambda k: 2 * k * P), (lambda k: (2 * k + 1) * P)
        mB.gw, mD.gw = 0, 16
        mB.crow, mD.crow = 96, 0
        mB.spread = lambda k: selB[96:P, 2 * k:2 * k + 2, :].rearrange("p e i -> p (e i)")
        mD.spread = lambda k: selD[:, k:k + 1].to_broadcast([16, P])
        mB.tg, mD.tg = 2, 3

        passed = {e: sem(f"passed_{n}") for e, n in (
            (nc.vector, "dve"), (nc.tensor, "pe"), (nc.gpsimd, "pool"))}

        def wait_apart(eng, semaphore, value):
            eng.wait_ge(semaphore, value)
            eng.sem_inc(passed[eng], 1)

        def slot(g):
            return (g % 2) * GT

        pieces = value_pieces()

        block = stack.enter_context(nc.Block())

        @block.sync
        def _(sp):
            sp.dma_start(I[:], ident).then_inc(in_id, 16)
            sp.dma_start(CN[0:S, :, :], ctx.rearrange("b s d -> s b d")).then_inc(in_ctx, 16)
            for g in range(NG):
                sp.dma_start(X[:, g * GT:(g + 1) * GT].rearrange("p (b d) -> p b d", b=GB),
                             x[g * GB:(g + 1) * GB].rearrange("b t d -> t b d")).then_inc(in_x, 16)
            sp.dma_start(w2raw[:, 0:NB * 64].rearrange("p (e i) -> p e i", e=16),
                         w2.rearrange("e d i -> d e i")).then_inc(in_w2, 16)
            for n in range(2):
                sp.dma_start(w2raw[:, NB * 64 + 64 * n:NB * 64 + 64 * n + 64], w2_s).then_inc(in_w2, 16)
            sp.wait_ge(vs_zero, 1)
            sp.wait_ge(v_done, NG)
            for h, c, row, key, n in pieces:
                col = c * VW + (h % UH - chunk_head(c)) * HD
                sp.dma_start(VS[row:row + n, :, col:col + HD],
                             Vn[key:key + n, :, h * HD:(h + 1) * HD]).then_inc(in_vs, 16)
            sp.wait_ge(a_pv, START + NG)
            sp.wait_ge(rk_mm, START + NG * NHG)
            sp.dma_start(upraw[:].rearrange("p (e n) -> p e n", e=8),
                         up.rearrange("e k n -> k e n")).then_inc(in_up, 16)
            sp.dma_start(downw[:], down.rearrange("e k n -> k e n")).then_inc(in_up, 16)
            sp.wait_ge(ks_done, NG * NHG * HG)
            for n in range(2):
                sp.dma_start(VX[:, n * NC * P:(n + 1) * NC * P], vs_seed).then_inc(in_seed, 16)
            for g in range(NG):
                sp.wait_ge(x_done, START + mD.x_base + g + 1)
                sp.dma_start(out[g * GB:(g + 1) * GB].rearrange("b t d -> t b d"),
                             X[:, g * GT:(g + 1) * GT].rearrange("p (b d) -> p b d", b=GB)).then_inc(stored, 16)
            sp.wait_ge(stored, 16 * NG)

        @block.gpsimd
        def _(pool):
            nc.gpsimd.memset(mhalf[:], -0.5)
            nc.gpsimd.memset(valsB[:], LOW)
            nc.gpsimd.memset(valsD[:], LOW)
            nc.gpsimd.memset(keepB[:], LOW)
            nc.gpsimd.memset(keepD[:], LOW)
            nc.gpsimd.memset(RK[:].bitcast(F32), 0.0)
            nc.gpsimd.memset(RQ[:].bitcast(F32), 0.0)
            nc.gpsimd.memset(ones[:], 1.0).then_inc(built, 1)
            nc.gpsimd.memset(VS[:], 0.0).then_inc(vs_zero, 1)

            def inv_std(n):
                pool.wait_ge(var_rdy, n)
                nc.gpsimd.tensor_tensor(rstd[:], ve[:], mhalf[:], ALU.pow).then_inc(rstd_rdy, 1)

            def spread_keys(g):
                for s in range(NHG):
                    keys = kr[:, s, bass.ds(g * GS, GS)].rearrange("p (b k) -> p b k", b=GB)
                    dst = KS[:, bass.ds(g * (GB * HK), GB * HK)].rearrange(
                        "p (b s h k) -> p b s h k", b=GB, s=NHG, h=HG)[:, :, s]
                    for h in range(HG):
                        nc.gpsimd.tensor_tensor(dst[:, :, h], keys,
                                                mask4[:, h:h + 1].unsqueeze(2).to_broadcast([P, GB, S]),
                                                ALU.mult).then_inc(ks_done, 1)

            pool.wait_ge(built, 1)
            with pool.Fori(0, NG + 1) as g:
                inv_std(g + 1)
            pool.wait_ge(d_set, 1)
            pool.wait_ge(kr_done, START + NG * NHG)
            with pool.Fori(0, NG) as g:
                inv_std(NG + g + 2)
                spread_keys(g)

            def split_up(n):
                part = bass.ds(n * 512, 512)
                nc.gpsimd.tensor_copy(UPH[:, part], upraw[:, part]).then_inc(up_split, 1)
                wait_apart(pool, up_split, 2 * n + 1)
                nc.gpsimd.tensor_tensor(UPL[:, part], upraw[:, part], UPH[:, part].bitcast(F32),
                                        ALU.subtract).then_inc(up_split, 1)

            def add_bo(g):
                wait_apart(pool, xn_rdy, 2 * NG + g + 1)
                xg = X[:, bass.ds(g * GT, GT)].rearrange("p (b d) -> p b d", b=GB)
                nc.gpsimd.tensor_tensor(xg, xg, tgbo[:].unsqueeze(1).to_broadcast([P, GB, P]),
                                        ALU.add).then_inc(bo_add, 1)

            def place_values(n, par, first=False):
                if not first:
                    wait_apart(pool, c_pv, START + n - 1)
                src = VS[:, bass.ds(n, 1), :].rearrange("p a (u j d) -> p (a u) j d", u=NU, j=CU)
                step = 2 * P + 3 * HD
                half = CU * P + UD
                for j in (0, 1):
                    at = par * NC * P + j * P + chunk_head(j) * HD
                    dst = VX[:, at:at + NU * half].rearrange("p (u r) -> p u r", u=NU)[:, :, 0:2 * step]
                    dst = dst.rearrange("p u (i r) -> p u i r", i=2)[:, :, :, 0:VW]
                    nc.gpsimd.tensor_copy(dst, src[:, :, j:j + 3:2, :])
                for u in range(NU):
                    at = par * NC * P + u * half + 4 * P + chunk_head(4) * HD
                    i = nc.gpsimd.tensor_copy(VX[:, at:at + 2 * HD], src[:, u, 4, 0:2 * HD])
                i.then_inc(vx_rdy, 1)

            def c_body(g, nxt, last):
                add_bo(g)
                for t in range(GB):
                    if not (last and t == GB - 1):
                        place_values(GB * g + t + 1, (t + 1) % 2)
                    if t == 0:
                        inv_std(nxt)
                    if t == 1:
                        split_up(g)

            pool.wait_ge(in_seed, 32)
            pool.wait_ge(in_vs, 16 * len(pieces))
            place_values(0, 0, first=True)
            pool.wait_ge(mB.dn, START + NG * mB.H)
            pool.wait_ge(in_up, 32)
            with pool.Fori(0, NG - 1) as g:
                c_body(g, 2 * NG + g + 2, False)
            c_body(NG - 1, 3 * NG + 1, True)
            with pool.Fori(0, NG - 1) as g:
                inv_std(3 * NG + g + 2)

        @block.tensor
        def _(pe):
            mm, tr = nc.tensor.matmul, nc.tensor.transpose
            for s in (rk_mm, a_ptr, a_pv, mB.dn, mD.dn, c_tr, c_pv, c_wo):
                pe.sem_inc(s, START)

            pe.wait_ge(in_id, 16)
            pe.wait_ge(in_ctx, 16)
            for g in range(NG):
                for b in range(GB):
                    i = tr(bank[g][:, b * S:(b + 1) * S], CN[0:S, g * GB + b, :], I[0:S, 0:S])
                i.then_inc(su_mm, 1)
            pe.wait_ge(in_w, 16 * 6)
            for n in range(4):
                i = tr(bank[4][:, n * P:(n + 1) * P], wraw[:, n, :], I[:])
            i.then_inc(su_mm, 1)
            i = tr(Tb[:, 0:24], graw[:], I[0:24, 0:24])
            i.then_inc(su_mm, 1)
            pe.wait_ge(in_small, 16 * 10)
            for g in range(NG):
                pe.wait_ge(su_a, g + 1)
                mm(bank[g][:, 0:GS], W0[:], cT[:, g * GS:(g + 1) * GS], start=True, stop=True).then_inc(su_mm, 1)
            for g in range(NG):
                if g == 0:
                    pe.wait_ge(su_d, 2)
                else:
                    pe.wait_ge(su_d, g + 2)
                mm(Tb[0:1, 0:GS], cols[:, 0:1], cT[:, g * GS:(g + 1) * GS], start=True, stop=True).then_inc(su_mm, 1)
            pe.wait_ge(in_w13, 16 * 6)
            for n in range(5):
                bk = bank[n % 4] if n < 4 else bank[4]
                pe.wait_ge(su_a, 7 + n if n < 4 else 10)
                for j in range(4 * n, min(17, 4 * n + 4)):
                    i = tr(bk[:, j % 4 * P:j % 4 * P + P], w13raw[:, j * P:(j + 1) * P], I[:])
                i.then_inc(su_mm, 1)
            pe.wait_ge(in_w2, 16 * 3)
            for n in range(3):
                pe.wait_ge(su_a, 11 + n)
                pe.wait_ge(su_d, 7 + n)
                for j in range(4 * n, min(9, 4 * n + 4)):
                    i = tr(bank[n][:, j % 4 * P:j % 4 * P + P], w2raw[:, j * P:(j + 1) * P], I[:])
                i.then_inc(su_mm, 1)
            for g in range(NG):
                pe.wait_ge(su_a, 16 + min(g, 2))
                pe.wait_ge(su_d, 11)
                for t in range(GB):
                    b = g * GB + t
                    i = mm(bank[g][0:S, t * P:(t + 1) * P], cT[:, b * S:(b + 1) * S], WX[:, 1, :], start=True, stop=True)
                i.then_inc(v_mm, 1)
            pe.wait_ge(v_done, NG)

            def norm_T(n):
                pe.wait_ge(xn_rdy, n)
                for t in range(GB):
                    i = tr(Tb[:, t * P:(t + 1) * P], xn[:, t * P:(t + 1) * P], I[:])
                i.then_inc(xnT, 1)

            bS, bT, bO = bank[0], bank[1], Ybank[:, 0:GT]

            def a_scores(g):
                pe.wait_ge(xh_rdy, g + 1)
                pe.wait_ge(a_sub, START + g)
                for t in range(GB):
                    c = g * GS + t * S
                    mm(bS[:, t * S:(t + 1) * S], ones[0:1, :], bctx[0:1, bass.ds(c, S)], start=True, stop=False)
                    i = mm(bS[:, t * S:(t + 1) * S], xf[:, t * P:(t + 1) * P], MT[:, bass.ds(c, S)],
                           start=False, stop=True)
                i.then_inc(a_sc, 1)

            bV = [bank[2], bank[3], bank[4], Ybank[:, GT:2 * GT]]

            def a_keys(g):
                pe.wait_ge(kr_done, START + NHG * g)
                mm(bV[1][:, 0:GS], WX[:, 0, :], cT[:, bass.ds(g * GS, GS)], start=True, stop=True).then_inc(k_mm, 1)

            def a_repeat(g):
                pe.wait_ge(k_l, g + 1)
                for s in range(NHG):
                    mm(bV[s][:, 0:GS], RK[:, s, 2:6, :].rearrange("p a b -> p (a b)"), kh[:], start=True, stop=False)
                    mm(bV[s][:, 0:GS], RK[:, s, 0:4, :].rearrange("p a b -> p (a b)"), kl[:],
                       start=False, stop=True).then_inc(rk_mm, 1)

            def a_probs_T(g):
                pe.wait_ge(a_exp, g + 1)
                pe.wait_ge(a_ptc, START + g)
                for t in range(GB):
                    i = tr(bT[0:S, t * P:(t + 1) * P], PA[:, t * S:(t + 1) * S], I[:])
                i.then_inc(a_ptr, 1)

            def a_mix(g):
                pe.wait_ge(a_ptc, START + g + 1)
                pe.wait_ge(x_done, START + g)
                for t in range(GB):
                    i = mm(bO[:, t * P:(t + 1) * P], ptA[:, t * P:(t + 1) * P],
                           CN[0:S, bass.ds(g * GB + t, 1), :].rearrange("p a d -> p (a d)"), start=True, stop=True)
                i.then_inc(a_pv, 1)

            pe.wait_ge(built, 1)
            pe.wait_ge(d_set, 1)
            norm_T(1)

            def a_body(g):
                a_scores(g)
                a_keys(g)
                a_probs_T(g)
                norm_T(g + 2)
                a_repeat(g)
                a_mix(g)

            with pe.Fori(0, NG) as g:
                a_body(g)

            def split3(dst, w, col, xs, inc):
                for n, (wp, xp) in enumerate(((w[0], xh), (w[0], xl), (w[1], xh))):
                    i = mm(dst, wp[:, col:col + P], xp[:, bass.ds(xs, GT)], start=n == 0, stop=n == 2)
                i.then_inc(inc, 1)

            def m_up(m, g, k, ring=True):
                if ring:
                    pe.wait_ge(m.t2, m.units * g + k - 1)
                if k == 0:
                    pe.wait_ge(xl_rdy, m.lo_base + g + 1)
                split3(Gb[k % 2][:], (m.wh, m.wl), m.gcol(k), slot(g), m.g_done)
                split3(Ub[k % 2][:], (m.wh, m.wl), m.ucol(k), slot(g), m.u_done)

            def m_spread(m, g, k):
                pe.wait_ge(m.h_done, START + m.H * g + k)
                if k == 0:
                    pe.wait_ge(route["rdy"], m.route_base + g + 1)
                mm(Cb[:], m.spread(k), ct[m.crow:m.crow + 2 * m.E, :], start=True, stop=True).then_inc(m.c_done, 1)

            def m_down(m, g, k):
                wait_apart(pe, m.h_done, START + m.H * g + k + 1)
                if k == 0:
                    pe.wait_ge(x_done, START + m.x_base + g - 1)
                rows = slice(0, 64) if k == m.units else slice(0, P)
                for t in range(GB):
                    lhs = hs[rows, t * P:(t + 1) * P] if k == m.units else hb[:, k % 2, t * P:(t + 1) * P]
                    i = mm(Ybank[:, bass.ds(slot(g) + t * P, P)], lhs, m.wd[rows, k, :],
                           start=(k == 0 and t == 0), stop=(k == m.H - 1), skip_group_check=True)
                i.then_inc(m.dn, 1)

            def m_logits(m, g):
                pe.wait_ge(xl_rdy, m.lo_base + g + 1)
                for n, (wp, xp) in enumerate(((GWH, xh), (GWH, xl), (GWL, xh))):
                    i = mm(Tb[0:m.E, :], wp[:, m.gw:m.gw + m.E], xp[:, bass.ds(slot(g), GT)], start=n == 0, stop=n == 2)
                i.then_inc(route["mm"], 1)

            def m_logits_T(m, g):
                wait_apart(pe, route["act"], m.route_base + g + 1)
                for t in range(GB):
                    i = tr(Tb[:, t * m.E:(t + 1) * m.E], lgT[0:m.E, t * P:(t + 1) * P], I[0:m.E, 0:m.E])
                i.then_inc(route["lgT"], 1)

            def m_route_T(m, g):
                pe.wait_ge(route["lo"], m.route_base + g + 1)
                for t in range(GB):
                    i = tr(Tb[0:2 * m.E, t * P:(t + 1) * P], CH[:, t, 0:2 * m.E].bitcast(F32), I[:])
                i.then_inc(route["tr"], 1)

            def m_body(m, g, nxt):
                more = nxt is not None and nxt[1] is m
                m_spread(m, g, 0)
                for k in range(m.units):
                    if k + 2 < m.units:
                        m_up(m, g, k + 2)
                    elif more:
                        m_up(m, g + 1, k + 2 - m.units)
                    if k + 1 < m.units:
                        m_spread(m, g, k + 1)
                    elif m.shared:
                        pe.wait_ge(m.h_done, START + m.H * g + m.units)
                        split3(Cb[:], (m.wh, m.wl), 2 * m.units * P, slot(g), m.us_done)
                    m_down(m, g, k)
                    if nxt is not None and k == 1:
                        norm_T(nxt[0])
                    if nxt is not None and nxt[1] is not None and k == 3:
                        m_logits(nxt[1], nxt[2])
                    if nxt is not None and nxt[1] is not None and k == 4:
                        m_logits_T(nxt[1], nxt[2])
                    if nxt is not None and nxt[1] is not None and k == m.units - 2:
                        m_route_T(nxt[1], nxt[2])
                if m.shared:
                    m_down(m, g, m.units)

            m = mB
            pe.wait_ge(kr_done, START + NG * NHG)
            m_logits(m, 0)
            m_up(m, 0, 0, ring=False)
            m_logits_T(m, 0)
            m_up(m, 0, 1, ring=False)
            m_route_T(m, 0)
            with pe.Fori(0, NG - 1) as g:
                m_body(m, g, (NG + g + 2, m, g + 1))
            m_body(m, NG - 1, (2 * NG + 1, None, 0))

            bS3 = [bank[0], bank[1], bank[2], bank[0]]
            bR = bank[3]
            bP = [bank[4], Ybank[:, 0:GT], bank[4]]
            bOut = Ybank[:, GT:2 * GT]

            def c_query(g):
                pe.wait_ge(xl_rdy, NG + g + 1)
                for n, (wp, xp) in enumerate(((WQH, xh), (WQH, xl), (WQL, xh))):
                    i = mm(Tb[:], wp[:], xp[:, bass.ds(slot(g), GT)], start=n == 0, stop=n == 2)
                i.then_inc(q_mm, 1)

            def c_repeat(g, s):
                if s == 0:
                    pe.wait_ge(q_l, g + 1)
                pe.wait_ge(qs_done, NHG * g + s)
                mm(Tb[:], RQ[:, s, 1:5, :].rearrange("p a b -> p (a b)"), qh[:], start=True, stop=False)
                mm(Tb[:], RQ[:, s, 0:4, :].rearrange("p a b -> p (a b)"), ql[:],
                   start=False, stop=True).then_inc(qs_mm, 1)

            def c_scores(g, t, s):
                n = GB * g + t
                if s == 0:
                    if t == 0:
                        pe.wait_ge(qs_done, NHG * g + NHG)
                    pe.wait_ge(c_exp, NHG * n)
                if s == 3:
                    pe.wait_ge(c_sub, len(SUB_EXP) * n + 1)
                q = QS[:, s * GT + t * P:s * GT + (t + 1) * P]
                mm(bS3[s][:, 0:HG * S], q, KS[:, bass.ds(n * HK + s * HG * S, HG * S)],
                   start=True, stop=True).then_inc(c_sc, 1)

            need = [2, 4, 4]

            def c_transpose(g, t, r):
                n = GB * g + t
                pe.wait_ge(c_exp, NHG * n + need[r])
                pe.wait_ge(c_ev, START + 3 * n + (1 if r == 2 else 0))
                for c in range(4 * r, min(NC, 4 * r + 4)):
                    w = chunk_rows(c)
                    i = tr(bP[r][0:w, c % 4 * P:c % 4 * P + P], PX[:, t % 2, chunk_col(c):chunk_col(c) + w], I[:])
                i.then_inc(c_tr, 1)

            def c_mix(g, t, u):
                n = GB * g + t
                if u == 0:
                    pe.wait_ge(c_ev, START + 3 * n + 3)
                    pe.wait_ge(vx_rdy, n + 1)
                    pe.wait_ge(c_norm, START + n)
                for c in range(u * CU, (u + 1) * CU):
                    w = chunk_rows(c)
                    v = (t % 2 * NC + c) * P
                    i = mm(bOut[:, u * P:(u + 1) * P], VX[0:w, v:v + P], pt[0:w, c * P:(c + 1) * P],
                           start=c % CU == 0, stop=c % CU == CU - 1)
                if u == NU - 1:
                    i.then_inc(c_pv, 1)

            def c_project(g, t):
                n = GB * g + t
                pe.wait_ge(c_norm, START + n + 1)
                pe.wait_ge(c_fin, START + n)
                mm(bR[:, 0:P], OTs[:], WX[:, 2, :], start=True, stop=True).then_inc(c_wo, 1)

            def c_body(g, first, last):
                for t in range(GB):
                    n1 = (g, t + 1) if t + 1 < GB else (g + 1, 0)
                    ahead = t + 1 < GB or not last
                    repeat = t == 2 and not last
                    for s in range(3):
                        c_transpose(g, t, s)
                        if s == 2 and repeat:
                            c_repeat(g + 1, 0)
                        if ahead:
                            c_scores(*n1, s)
                        if s == 1 and t == 1:
                            norm_T(2 * NG + 2 + g)
                    if t or not first:
                        c_project(*((g, t - 1) if t else (g - 1, GB - 1)))
                    if repeat:
                        c_repeat(g + 1, 1)
                    c_mix(g, t, 0)
                    if ahead:
                        c_scores(*n1, 3)
                    if repeat:
                        c_repeat(g + 1, 2)
                    c_mix(g, t, 1)
                    if repeat:
                        c_repeat(g + 1, 3)
                    if t == 1:
                        if not last:
                            c_query(g + 1)
                        else:
                            m_logits(mD, 0)
                    if t == 2 and last:
                        m_logits_T(mD, 0)

            pe.wait_ge(wo_rdy, 1)
            c_query(0)
            for s in range(NHG):
                c_repeat(0, s)
            pe.wait_ge(ks_done, NG * NHG * HG)
            pe.wait_ge(x_done, START + 2 * NG)
            pe.wait_ge(mB.h_done, START + NG * mB.H)
            for s in range(NHG):
                c_scores(0, 0, s)
            c_body(0, True, False)
            with pe.Fori(1, NG - 1) as g:
                c_body(g, False, False)
            c_body(NG - 1, False, True)
            c_project(NG - 1, GB - 1)
            m_route_T(mD, 0)

            m = mD
            pe.wait_ge(up_split, 8)
            pe.wait_ge(in_up, 32)
            pe.wait_ge(c_fin, START + NB)
            m_up(m, 0, 0, ring=False)
            m_up(m, 0, 1, ring=False)
            with pe.Fori(0, NG - 1) as g:
                m_body(m, g, (3 * NG + g + 2, m, g + 1))
            m_body(m, NG - 1, None)

        @block.scalar
        def _(act):
            A = nc.scalar.activation
            for s in (kr_done, a_ptc, c_ev):
                act.sem_inc(s, START)
            for n, w in enumerate((wq, wk, wv, wo)):
                act.dma_start(wraw[:, n, :], w).then_inc(in_w, 16)
            act.dma_start(graw[0:16, :], gate_w).then_inc(in_w, 16)
            act.dma_start(graw[16:24, :], router_w).then_inc(in_w, 16)
            act.dma_start(W0[:], w0).then_inc(in_small, 16)
            act.dma_start(cols[:, 0:1], b0.unsqueeze(1)).then_inc(in_small, 16)
            act.dma_start(cols[:, 1:2], bq.unsqueeze(1)).then_inc(in_small, 16)
            act.dma_start(cols[:, 2:3], bk.unsqueeze(1)).then_inc(in_small, 16)
            act.dma_start(cols[:, 3:4], bq.unsqueeze(1)).then_inc(in_small, 16)
            act.dma_start(tg[:, 0:2], g_xattn.partition_broadcast(P)).then_inc(in_small, 16)
            act.dma_start(tg[:, 2:4], g_ffn.partition_broadcast(P)).then_inc(in_small, 16)
            act.dma_start(bvr[:], bv.partition_broadcast(P)).then_inc(in_small, 16)
            act.dma_start(tgbo[:], bo.partition_broadcast(P)).then_inc(in_small, 16)
            act.dma_start(gbr[:], gate_b.partition_broadcast(P)).then_inc(in_small, 16)
            raw = w13raw[:, 0:16 * P].rearrange("p (u j d) -> p u j d", u=2, j=8)
            for e in range(2):
                for u in range(2):
                    src = w13[e::2, 64 * u:64 * u + 64, :].rearrange("j i d -> i j d")
                    act.dma_start(raw[64 * e:64 * e + 64, u], src).then_inc(in_w13, 16)
            act.dma_start(w13raw[0:64, 16 * P:17 * P], w13_s[64:P, :]).then_inc(in_w13, 16)
            act.dma_start(w13raw[64:P, 16 * P:17 * P], w13_s[0:64, :]).then_inc(in_w13, 16)

            act.wait_ge(in_small, 16 * 10)
            A(tg[:], tg[:], ACT.Tanh).then_inc(tg_rdy, 1)
            A(cols[:, 1:2], cols[:, 1:2], ACT.Copy, scale=QSCALE).then_inc(tg_rdy, 1)
            for g in range(NG):
                act.wait_ge(su_mm, g + 1)
                A(cT[:, g * GS:(g + 1) * GS], bank[g][:, 0:GS], ACT.Copy).then_inc(su_a, 1)
            act.wait_ge(su_mm, 5)
            A(WQH[:], bank[4][:, 0:P], ACT.Copy).then_inc(su_a, 1)
            A(WX[:].rearrange("p a d -> p (a d)"), bank[4][:, P:4 * P], ACT.Copy).then_inc(su_a, 1)
            for g in range(NG):
                act.wait_ge(su_mm, 7 + g)
                A(MT[:, g * GS:(g + 1) * GS], bank[g][:, 0:GS], ACT.Copy).then_inc(su_a, 1)
            for n in range(5):
                act.wait_ge(su_mm, 15 + n)
                w = (min(17, 4 * n + 4) - 4 * n) * P
                A(WBH[:, 4 * n * P:4 * n * P + w], bank[n][:, 0:w], ACT.Copy).then_inc(su_a, 1)
            for n in range(3):
                act.wait_ge(su_mm, 20 + n)
                w = min(9, 4 * n + 4) - 4 * n
                A(W2T[:, 4 * n:4 * n + w, :].rearrange("p a d -> p (a d)"), bank[n][:, 0:w * P],
                  ACT.Copy).then_inc(su_a, 1)

            def norm_hi(n, dst):
                act.wait_ge(xnT, n)
                A(dst, Tb[:], ACT.Copy).then_inc(xh_rdy, 1)

            norm_hi(1, xf[:])

            def a_body(g, last):
                act.wait_ge(a_sub, START + g + 1)
                A(PA[:], PA[:], ACT.Exp).then_inc(a_exp, 1)
                act.wait_ge(k_mm, g + 1)
                A(kf[:], bank[3][:, 0:GS], ACT.Identity, bias=cols[:, 2:3]).then_inc(k_f, 1)
                act.wait_ge(k_f, g + 1)
                act.wait_ge(rk_mm, START + NHG * g)
                A(kh[:], kf[:], ACT.Copy).then_inc(k_h, 1)
                act.wait_ge(a_ptr, START + g + 1)
                act.wait_ge(a_pv, START + g)
                A(ptA[:], bank[1][0:S, :], ACT.Copy).then_inc(a_ptc, 1)
                norm_hi(g + 2, xh[:, 0:GT] if last else xf[:])
                for s in range(NHG):
                    act.wait_ge(rk_mm, START + NHG * g + s + 1)
                    src = [bank[2], bank[3], bank[4], Ybank[:, GT:2 * GT]][s]
                    A(kr[:, s, bass.ds(g * GS, GS)], src[:, 0:GS], ACT.Copy).then_inc(kr_done, 1)

            with act.Fori(0, NG - 1) as g:
                a_body(g, False)
            a_body(NG - 1, True)

            def m_silu(m, g, k):
                act.wait_ge(m.g_done, m.units * g + k + 1)
                act.wait_ge(m.h_done, START + m.H * g + max(0, k - 1))
                A(sg[:, k % 2, :], Gb[k % 2][:], ACT.Silu).then_inc(m.s_done, 1)

            def m_route_act(m, g):
                act.wait_ge(route["mm"], m.route_base + g + 1)
                if m is mB:
                    A(lgT[0:m.E, :], Tb[0:m.E, :], ACT.Tanh, scale=0.5).then_inc(route["act"], 1)
                else:
                    A(lgT[0:m.E, :], Tb[0:m.E, :], ACT.Copy).then_inc(route["act"], 1)

            def m_route_exp(m, g):
                if m is mD:
                    act.wait_ge(route["sub"], g + 1)
                    A(score[:, :, 0:8], lgt[:, :, 0:8], ACT.Exp).then_inc(route["exp"], 1)

            def m_route_copy(m, g):
                act.wait_ge(route["tr"], m.route_base + g + 1)
                A(ct[m.crow:m.crow + 2 * m.E, :], Tb[0:2 * m.E, :], ACT.Copy).then_inc(route["rdy"], 1)

            def m_body(m, g, nxt):
                for k in range(m.units):
                    m_silu(m, g, k)
                    if nxt is not None and k == 2:
                        norm_hi(nxt[0], xh[:, bass.ds(slot(nxt[2]), GT)])
                    if nxt is not None and nxt[1] is not None and k == 4:
                        m_route_act(nxt[1], nxt[2])
                    if nxt is not None and nxt[1] is not None and k == 5:
                        m_route_exp(nxt[1], nxt[2])
                if m.shared:
                    act.wait_ge(m.us_done, g + 1)
                    act.wait_ge(m.dn, START + m.H * g)
                    A(hs[:], Cb[64:P, :], ACT.Silu).then_inc(m.ss_done, 1)
                if nxt is not None and nxt[1] is not None:
                    m_route_copy(nxt[1], nxt[2])

            m = mB
            m_route_act(m, 0)
            m_route_copy(m, 0)
            with act.Fori(0, NG - 1) as g:
                m_body(m, g, (NG + g + 2, m, g + 1))
            m_body(m, NG - 1, (2 * NG + 1, None, 0))

            def c_query(g):
                act.wait_ge(q_mm, g + 1)
                act.wait_ge(q_l, g)
                A(qf[:], Tb[:], ACT.Identity, bias=cols[:, 1:2], scale=QSCALE).then_inc(q_f, 1)

            def c_repeat(g, s):
                act.wait_ge(qs_mm, NHG * g + s + 1)
                A(QS[:, s * GT:(s + 1) * GT], Tb[:], ACT.Copy).then_inc(qs_done, 1)

            bSa = [bank[0], bank[1], bank[2], bank[0]]

            def c_exps(g, t, s, first=False):
                n = GB * g + t
                p = PX[:, t % 2, s * HG * S:(s + 1) * HG * S]
                if s in BIAS_EXP:
                    act.wait_ge(c_mx, NHG * n + s + 1)
                    if not first:
                        act.wait_ge(c_tr, START + 3 * n - 3)
                    for h in range(HG):
                        i = A(p[:, h * S:(h + 1) * S], bSa[s][:, h * S:(h + 1) * S], ACT.Exp,
                              bias=cmx[:, s, h:h + 1])
                else:
                    act.wait_ge(c_sub, 2 * n + SUB_EXP.index(s) + 1)
                    i = A(p, p, ACT.Exp)
                i.then_inc(c_exp, 1)

            bPa = [bank[4], Ybank[:, 0:GT], bank[4]]

            def c_copy(g, t, r):
                n = GB * g + t
                act.wait_ge(c_tr, START + 3 * n + r + 1)
                act.wait_ge(c_pv, START + n)
                w = min(NC, 4 * r + 4) * P - 4 * r * P
                A(pt[:, 4 * r * P:4 * r * P + w], bPa[r][:, 0:w], ACT.Copy).then_inc(c_ev, 1)

            def c_sums(g, t):
                n = GB * g + t
                act.wait_ge(c_pv, START + n + 1)
                act.wait_ge(c_rs, START + n)
                A(sumT[0:UD, :], Ybank[UD:P, GT:GT + P], ACT.Copy)
                A(sumT[UD:P, :], Ybank[0:UD, GT + P:GT + 2 * P], ACT.Copy).then_inc(c_sum, 1)

            def c_body(g, first, last):
                for t in range(GB):
                    n1 = (g, t + 1) if t + 1 < GB else (g + 1, 0)
                    if t or not first:
                        c_sums(*((g, t - 1) if t else (g - 1, GB - 1)))
                    for r in range(3):
                        c_copy(g, t, r)
                    if t == 1:
                        norm_hi(2 * NG + 2 + g, xh[:, bass.ds(slot(g + 1), GT)])
                    for s in range(NHG):
                        if t == 2 and not last and s != 1:
                            c_repeat(g + 1, (0, None, 1, 2)[s])
                        if t + 1 < GB or not last:
                            c_exps(*n1, s)
                    if t == 2 and not last:
                        c_repeat(g + 1, 3)
                    if t == 1 and not last:
                        c_query(g + 1)
                    if t == 1 and last:
                        m_route_act(mD, 0)
                    if t == 2 and last:
                        m_route_exp(mD, 0)

            c_query(0)
            act.wait_ge(ks_done, NG * NHG * HG)
            for s in range(NHG):
                c_repeat(0, s)
            for s in range(NHG):
                c_exps(0, 0, s, first=True)
            c_body(0, True, False)
            with act.Fori(1, NG - 1) as g:
                c_body(g, False, False)
            c_body(NG - 1, False, True)
            c_sums(NG - 1, GB - 1)
            m_route_copy(mD, 0)

            m = mD
            with act.Fori(0, NG - 1) as g:
                m_body(m, g, (3 * NG + g + 2, m, g + 1))
            m_body(m, NG - 1, None)

        @block.vector
        def _(dve):
            V = nc.vector
            for s in (a_sub, x_done, mB.h_done, mD.h_done, c_norm, c_fin, c_rs):
                dve.sem_inc(s, START)
            dve.wait_ge(in_id, 16)
            dve.wait_ge(built, 1)
            dve.wait_ge(in_small, 16 * 10)
            heads = I[:].rearrange("p (s r) -> p s r", s=NHG)
            for n in (2, 3):
                V.tensor_copy(RK[:, :, n, :], heads)
            for n in (3,):
                V.tensor_copy(RQ[:, :, n, :], heads)
            V.tensor_reduce(mask4[:], I[:].rearrange("p (t h d) -> p h t d", t=4, h=HG), mybir.AxisListType.XY, ALU.add)
            V.tensor_tensor(selB[96:P], I[96:P, 96:112].unsqueeze(2).to_broadcast([32, 16, 64]),
                            I[96:P, 112:P].unsqueeze(2).to_broadcast([32, 16, 64]), ALU.add)
            V.tensor_tensor(selD[:], I[0:16, 0:8], I[0:16, 8:16], ALU.add)
            V.tensor_copy(RQ[:, :, 1, :], heads).then_inc(d_set, 1)
            dve.wait_ge(tg_rdy, 1)
            V.tensor_scalar(tgbo[:], tgbo[:], tg[:, 1:2], None, ALU.mult).then_inc(d_set, 1)
            dve.wait_ge(su_a, 6)
            V.tensor_tensor(WQL[:], bank[4][:, 0:P], WQH[:].bitcast(F32), ALU.subtract).then_inc(su_d, 1)
            V.tensor_scalar(WX[:, 2, :], WX[:, 2, :], tg[:, 1:2], None, ALU.mult).then_inc(wo_rdy, 1)
            dve.wait_ge(su_mm, 6)
            V.tensor_copy(GWH[:], Tb[:, 0:24]).then_inc(d_set, 1)
            dve.wait_ge(d_set, 3)
            V.tensor_tensor(GWL[:], Tb[:, 0:24], GWH[:].bitcast(F32), ALU.subtract).then_inc(su_d, 1)
            for g in range(NG):
                dve.wait_ge(su_mm, 11 + g)
                V.tensor_copy(bctx[0:1, g * GS:(g + 1) * GS], Tb[0:1, 0:GS]).then_inc(su_d, 1)
            for n in range(5):
                dve.wait_ge(su_a, 11 + n)
                w = (min(17, 4 * n + 4) - 4 * n) * P
                c = 4 * n * P
                V.tensor_tensor(WBL[:, c:c + w], bank[n][:, 0:w], WBH[:, c:c + w].bitcast(F32),
                                ALU.subtract).then_inc(su_d, 1)
            for g in range(NG):
                dve.wait_ge(v_mm, g + 1)
                V.tensor_tensor(Vn[0:S, g * GB:(g + 1) * GB, :], bank[g][0:S, :].rearrange("p (b d) -> p b d", b=GB),
                                bvr[0:S, :].unsqueeze(1).to_broadcast([S, GB, P]), ALU.add).then_inc(v_done, 1)

            def xt(g, t):
                return X[:, bass.ds(g * GT + t * P, P)]

            def norm_stats(n, g):
                for t in range(GB):
                    i = V.bn_stats(st[:, t, :], xt(g, t))
                i.then_inc(stats, 1)
                wait_apart(dve, stats, n)
                for t in range(GB):
                    i = V.bn_aggr(mv[:, t, :], st[:, t, :])
                i.then_inc(aggr, 1)
                dve.wait_ge(aggr, n)
                V.tensor_scalar(ve[:], mv[:, :, 1], EPS, None, ALU.add).then_inc(var_rdy, 1)

            def norm_apply(n, g, first=False):
                dve.wait_ge(rstd_rdy, n)
                if not first:
                    dve.wait_ge(xnT, n - 1)
                for t in range(GB):
                    i = V.tensor_scalar(xn[:, t * P:(t + 1) * P], xt(g, t), mv[:, t, 0:1], rstd[:, t:t + 1],
                                        ALU.subtract, ALU.mult)
                i.then_inc(xn_rdy, 1)

            def norm_lo(n, g):
                dve.wait_ge(xh_rdy, n)
                V.tensor_tensor(xl[:, bass.ds(slot(g), GT)], Tb[:], xh[:, bass.ds(slot(g), GT)].bitcast(F32),
                                ALU.subtract).then_inc(xl_rdy, 1)

            dve.wait_ge(in_x, 16 * NG)
            dve.wait_ge(su_mm, 5)
            norm_stats(1, 0)
            norm_apply(1, 0, first=True)

            def a_body(g, nxt, last):
                dve.wait_ge(a_sc, g + 1)
                sc = bank[0][:, 0:GS].rearrange("p (t k) -> p t k", t=GB)
                pa = PA[:].rearrange("p (t k) -> p t k", t=GB)
                V.reduce_max(amax[:], sc, AX).then_inc(a_max, 1)
                dve.wait_ge(a_max, g + 1)
                dve.wait_ge(a_ptr, START + g)
                V.tensor_tensor(pa, sc, amax[:].unsqueeze(2).to_broadcast([P, GB, S]), ALU.subtract).then_inc(a_sub, 1)
                if last:
                    dve.wait_ge(x_done, START + 1)
                norm_stats(g + 2, nxt)
                dve.wait_ge(a_exp, g + 1)
                V.reduce_sum(asum[:, 0, :], pa, AX).then_inc(a_sum, 1)
                norm_apply(g + 2, nxt)
                dve.wait_ge(a_sum, g + 1)
                V.reciprocal(asum[:, 1, :], asum[:, 0, :]).then_inc(a_rec, 1)
                dve.wait_ge(k_h, g + 1)
                V.tensor_tensor(kl[:], kf[:], kh[:].bitcast(F32), ALU.subtract).then_inc(k_l, 1)
                dve.wait_ge(a_rec, g + 1)
                V.tensor_scalar(asum[:, 2, :], asum[:, 1, :], tg[:, 0:1], None, ALU.mult).then_inc(a_r, 1)
                dve.wait_ge(a_r, g + 1)
                dve.wait_ge(a_pv, START + g + 1)
                for t in range(GB):
                    i = V.scalar_tensor_tensor(out=xt(g, t), in0=Ybank[:, t * P:(t + 1) * P],
                                               scalar=asum[:, 2, t:t + 1], in1=xt(g, t), op0=ALU.mult, op1=ALU.add)
                i.then_inc(x_done, 1)

            with dve.Fori(0, NG - 1) as g:
                a_body(g, g + 1, False)
            a_body(NG - 1, 0, True)
            norm_lo(NG + 1, 0)

            def route_vals(m, g):
                n = m.route_base + g + 1
                if m is mB:
                    dve.wait_ge(route["lgT"], n)
                    V.tensor_scalar(score[:], Tb[:, 0:GB * 16].rearrange("p (t e) -> p t e", t=GB), 0.5, 0.5, ALU.mult, ALU.add).then_inc(route["score"], 1)
                    dve.wait_ge(route["score"], n)
                    V.tensor_tensor(m.vals[:, :, 0:m.E], score[:], gbr[:].unsqueeze(1).to_broadcast([P, GB, 16]),
                                    ALU.add).then_inc(route["vals"], 1)
                else:
                    dve.wait_ge(route["exp"], g + 1)
                    V.tensor_copy(m.vals[:, :, 0:m.E], score[:, :, 0:8]).then_inc(route["vals"], 1)

            def route_sub(g):
                dve.wait_ge(route["lgT"], mD.route_base + g + 1)
                lg = Tb[:, 0:GB * 8].rearrange("p (t e) -> p t e", t=GB)
                V.reduce_max(rsm[:, 0, :], lg, AX).then_inc(route["mx"], 1)
                dve.wait_ge(route["mx"], g + 1)
                V.tensor_tensor(lgt[:, :, 0:8], lg, rsm[:, 0, :].unsqueeze(2).to_broadcast([P, GB, 8]),
                                ALU.subtract).then_inc(route["sub"], 1)

            def route_pick(m, g):
                n = m.route_base + g + 1
                wait_apart(dve, route["vals"], n)
                for t in range(GB):
                    i = V.max(top[:, t, :], m.vals[:, t, :])
                i.then_inc(route["top"], 1)
                dve.wait_ge(route["top"], n)
                V.tensor_copy(m.keep[:, :, 0:m.K], top[:, :, 0:m.K]).then_inc(route["keep"], 1)
                wait_apart(dve, route["keep"], n)
                for t in range(GB):
                    i = V.match_replace(m.rep[:, t, :], m.keep[:, t, :], m.vals[:, t, :], GONE)
                i.then_inc(route["rep"], 1)

            def route_weights(m, g):
                n = m.route_base + g + 1
                E = m.E
                dve.wait_ge(route["rep"], n)
                V.tensor_tensor(comb[:, :, 0:E], m.rep[:, :, 0:E], m.vals[:, :, 0:E], ALU.is_lt).then_inc(route["msk"], 1)
                dve.wait_ge(route["msk"], n)
                V.tensor_tensor(comb[:, :, 0:E], comb[:, :, 0:E], score[:, :, 0:E], ALU.mult).then_inc(route["w"], 1)
                dve.wait_ge(route["w"], n)
                V.reduce_sum(rsm[:, 0, :], comb[:, :, 0:E], AX).then_inc(route["sum"], 1)
                dve.wait_ge(route["sum"], n)
                V.reciprocal(rsm[:, 1, :], rsm[:, 0, :]).then_inc(route["rec"], 1)
                dve.wait_ge(route["rec"], n)
                V.scalar_tensor_tensor(out=comb[:, :, 0:E], in0=comb[:, :, 0:E], scalar=m.scale,
                                       in1=rsm[:, 1, :].unsqueeze(2).to_broadcast([P, GB, E]),
                                       op0=ALU.mult, op1=ALU.mult).then_inc(route["comb"], 1)
                dve.wait_ge(route["comb"], n)
                V.tensor_copy(CH[:, :, 0:E], comb[:, :, 0:E]).then_inc(route["hi"], 1)
                dve.wait_ge(route["hi"], n)
                V.tensor_tensor(CH[:, :, E:2 * E], comb[:, :, 0:E], CH[:, :, 0:E].bitcast(F32),
                                ALU.subtract).then_inc(route["lo"], 1)

            def m_hidden(m, g, k):
                dve.wait_ge(m.s_done, m.units * g + k + 1)
                dve.wait_ge(m.u_done, m.units * g + k + 1)
                V.tensor_tensor(sg[:, k % 2, :], sg[:, k % 2, :], Ub[k % 2][:], ALU.mult).then_inc(m.t2, 1)
                dve.wait_ge(m.t2, m.units * g + k + 1)
                dve.wait_ge(m.c_done, m.units * g + k + 1)
                dve.wait_ge(m.dn, START + m.H * g + max(0, k - 1))
                V.tensor_tensor(hb[:, k % 2, :], sg[:, k % 2, :], Cb[:], ALU.mult).then_inc(m.h_done, 1)

            def m_body(m, g, nxt):
                for k in range(m.units):
                    m_hidden(m, g, k)
                    if nxt is None:
                        continue
                    n, nm, ng = nxt
                    if k == 0:
                        norm_stats(n, ng)
                    if k == 1:
                        norm_apply(n, ng)
                    if k == 2:
                        norm_lo(n, ng)
                    if nm is mD and k == 4:
                        route_sub(ng)
                    if nm is not None and k == 5:
                        route_vals(nm, ng)
                        route_pick(nm, ng)
                        route_weights(nm, ng)
                if m.shared:
                    dve.wait_ge(m.ss_done, g + 1)
                    V.tensor_tensor(hs[:], hs[:], Cb[0:64, :], ALU.mult).then_inc(m.h_done, 1)
                dve.wait_ge(m.dn, START + m.H * g + m.H)
                for t in range(GB):
                    i = V.scalar_tensor_tensor(out=xt(g, t), in0=Ybank[:, bass.ds(slot(g) + t * P, P)],
                                               scalar=tg[:, m.tg:m.tg + 1], in1=xt(g, t), op0=ALU.mult, op1=ALU.add)
                i.then_inc(x_done, 1)

            m = mB
            route_vals(m, 0)
            route_pick(m, 0)
            route_weights(m, 0)
            with dve.Fori(0, NG - 1) as g:
                m_body(m, g, (NG + g + 2, m, g + 1))
            m_body(m, NG - 1, (2 * NG + 1, None, 0))

            def c_split(g):
                dve.wait_ge(q_f, g + 1)
                dve.wait_ge(qs_mm, NHG * g)
                V.tensor_copy(qh[:], qf[:]).then_inc(q_h, 1)
                dve.wait_ge(q_h, g + 1)
                V.tensor_tensor(ql[:], qf[:], qh[:].bitcast(F32), ALU.subtract).then_inc(q_l, 1)

            bSd = [bank[0], bank[1], bank[2], bank[0]]

            def c_max(g, t, s):
                n = GB * g + t
                dve.wait_ge(c_sc, NHG * n + s + 1)
                V.tensor_reduce(cmx[:, s, :], bSd[s][:, 0:HG * S].rearrange("p (h k) -> p h k", h=HG), AX, ALU.max,
                                negate=True).then_inc(c_mx, 1)

            def c_center(g, t, s, first=False):
                n = GB * g + t
                dve.wait_ge(c_mx, NHG * n + s + 1)
                if not first:
                    dve.wait_ge(c_tr, START + 3 * n - 3)
                V.tensor_tensor(PX[:, t % 2, s * HG * S:(s + 1) * HG * S].rearrange("p (h k) -> p h k", h=HG),
                                bSd[s][:, 0:HG * S].rearrange("p (h k) -> p h k", h=HG),
                                cmx[:, s, :].unsqueeze(2).to_broadcast([P, HG, S]), ALU.add).then_inc(c_sub, 1)

            def c_reciprocal(g, t):
                n = GB * g + t
                dve.wait_ge(c_sum, n + 1)
                V.reciprocal(recT[:], sumT[:]).then_inc(c_rs, 1)

            def c_normalize(g, t):
                n = GB * g + t
                dve.wait_ge(c_rs, START + n + 1)
                dve.wait_ge(c_wo, START + n)
                V.tensor_tensor(OTs[0:UD, :], Ybank[0:UD, GT:GT + P], recT[0:UD, :], ALU.mult)
                V.tensor_tensor(OTs[UD:P, :], Ybank[UD:P, GT + P:GT + 2 * P], recT[UD:P, :],
                                ALU.mult).then_inc(c_norm, 1)

            def c_final(g, t):
                n = GB * g + t
                if t == 0:
                    dve.wait_ge(bo_add, g + 1)
                dve.wait_ge(c_wo, START + n + 1)
                V.tensor_tensor(xt(g, t), bank[3][:, 0:P], xt(g, t), ALU.add).then_inc(c_fin, 1)

            def c_body(g, first, last):
                nxt = 0 if last else g + 1
                for t in range(GB):
                    n1 = (g, t + 1) if t + 1 < GB else (g + 1, 0)
                    before = (g, t - 1) if t else None if first else (g - 1, GB - 1)
                    ahead = t + 1 < GB or not last
                    if before:
                        c_reciprocal(*before)
                    if ahead:
                        c_max(*n1, 0)
                    if before:
                        c_normalize(*before)
                    if ahead:
                        c_center(*n1, 0)
                        c_max(*n1, 1)
                        c_max(*n1, 2)
                    if before:
                        c_final(*before)
                    if ahead:
                        c_center(*n1, 2)
                    if t == 0:
                        norm_stats(2 * NG + 2 + g, nxt)
                    if t == 1:
                        norm_lo(2 * NG + 2 + g, g + 1)
                    if ahead:
                        c_max(*n1, 3)
                    if t == 0:
                        norm_apply(2 * NG + 2 + g, nxt)
                    if t == 1 and not last:
                        c_split(g + 1)
                    if t == 2 and last:
                        route_sub(0)
                        route_vals(mD, 0)
                        route_pick(mD, 0)
                        route_weights(mD, 0)

            c_split(0)
            for s in range(NHG):
                c_max(0, 0, s)
                if s in SUB_EXP:
                    c_center(0, 0, s, first=True)
            c_body(0, True, False)
            with dve.Fori(1, NG - 1) as g:
                c_body(g, False, False)
            c_body(NG - 1, False, True)
            c_reciprocal(NG - 1, GB - 1)
            c_normalize(NG - 1, GB - 1)
            c_final(NG - 1, GB - 1)

            m = mD
            with dve.Fori(0, NG - 1) as g:
                m_body(m, g, (3 * NG + g + 2, m, g + 1))
            m_body(m, NG - 1, None)


_INS = ['x', 'ctx_1024', 'g_xattn', 'g_ffn', 'L0_xattn_W', 'L0_xattn_b', 'L0_ffn_gate_w', 'L0_ffn_gate_b',
        'L0_ffn_w13', 'L0_ffn_w2', 'L0_ffn_w13_s', 'L0_ffn_w2_s', 'L1_xattn_Wq', 'L1_xattn_bq', 'L1_xattn_Wk',
        'L1_xattn_bk', 'L1_xattn_Wv', 'L1_xattn_bv', 'L1_xattn_Wo', 'L1_xattn_bo', 'L1_ffn_router_w',
        'L1_ffn_up_proj', 'L1_ffn_down_proj']


def kernel(**inputs):
    import numpy as _np
    import concourse.bacc as _bacc
    from concourse import mybir as _mybir
    from concourse.bass_utils import run_bass_kernel_spmd as _run

    seed = _np.zeros((P, NC * P), _np.float32)
    for h, c, row, _, n in value_pieces():
        ones = c * P + (1 - h // UH) * UD + h % UH * HD
        seed[row:row + n, ones:ones + HD] = 1.0
    consts = {'ident': _np.eye(P, dtype=_np.float32), 'vs_seed': seed}

    nc = _bacc.Bacc("TRN2", target_bir_lowering=False, num_devices=1)
    arrays, args = {}, []
    for name in _INS + list(consts):
        a = _np.ascontiguousarray(consts[name] if name in consts else inputs[name])
        arrays[f"in_{name}"] = a
        args.append(nc.dram_tensor(f"in_{name}", a.shape, _mybir.dt.from_np(a.dtype), kind="ExternalInput").ap())
    args.append(nc.dram_tensor("out_x", (NB, P, P), _mybir.dt.float32, kind="ExternalOutput").ap())
    flamingo(nc, *args)
    r = _run(nc, [arrays], core_ids=[0])
    return r.results[0]["out_x"]
```

```python
from contextlib import ExitStack

import concourse.bass as bass
from concourse import mybir

F32 = mybir.dt.float32
F32R = mybir.dt.float32r
ALU = mybir.AluOpType
ACT = mybir.ActivationFunctionType
AX = mybir.AxisListType.X

P = 128
NB = 16
S = 77
GB = 4
NG = NB // GB
GT = GB * P
GS = GB * S
NH, HD = 16, 8
HG = 4
NHG = NH // HG
HK = NH * S
NU = 2
UH = NH // NU
UK = UH * S
UD = UH * HD
CU = -(-UK // P)
NC = NU * CU
VW = 3 * HD
EPS = 1e-5
START = 1
LOW = -1e30
GONE = -3e30
SUB_EXP = (0, 3)
BIAS_EXP = (1, 2)
QSCALE = float(HD) ** -0.5


def chunk_rows(c):
    return min(P, UK - c % CU * P)


def chunk_col(c):
    return c // CU * UK + c % CU * P


def chunk_head(c):
    return c % CU * P // S


def value_pieces():
    out = []
    for h in range(NH):
        k = 0
        while k < S:
            at = h % UH * S + k
            n = min(S - k, P - at % P)
            out.append((h, h // UH * CU + at // P, at % P, k, n))
            k += n
    return out


class Moe:

    def __init__(self, name, phase, experts, topk, units, shared, scale, x_base, lo_base, route_base):
        self.name, self.phase, self.E, self.K = name, phase, experts, topk
        self.units, self.shared, self.scale = units, shared, scale
        self.W = experts + 8 - topk
        self.x_base, self.lo_base, self.route_base = x_base, lo_base, route_base


def flamingo(nc, x, ctx, g_xattn, g_ffn, w0, b0, gate_w, gate_b, w13, w2, w13_s, w2_s,
             wq, bq, wk, bk, wv, bv, wo, bo, router_w, up, down, ident, vs_seed, out):
    with ExitStack() as stack:
        at = [16512]

        def sb(name, shape, dt=F32, offset=None):
            size = 4
            for n in shape[1:]:
                size *= n
            if offset is None:
                offset = at[0]
                at[0] += -(-size // 32) * 32
            place[name] = offset
            return nc.alloc_sbuf_tensor_at(name, shape, dt, offset=offset)

        place = {}

        def psum(name, shape=(P, 512)):
            return stack.enter_context(nc.psum_tensor(name, list(shape), F32))

        def sem(name):
            return stack.enter_context(nc.semaphore(name))

        X = sb("X", [P, NB * P])
        xh = sb("xh", [P, 2 * GT], F32R)
        xl = sb("xl", [P, 2 * GT], F32R)
        xf = sb("xf", [P, GT], F32, place["xl"])
        KS = sb("KS", [P, NB * HK], F32R)
        wraw = sb("wraw", [P, 4, P], F32, place["KS"])
        w13raw = sb("w13raw", [P, 17 * P], F32, place["KS"] + 16 * P)
        w2raw = sb("w2raw", [P, NB * 64 + 128], F32, place["KS"] + 16 * P + 4 * 17 * P)
        VS = sb("VS", [P, NB, NC * VW])
        WBH = sb("WBH", [P, 17 * P], F32R)
        WBL = sb("WBL", [P, 17 * P], F32R)
        UPH = sb("UPH", [P, 8 * 2 * P], F32R, place["WBH"])
        UPL = sb("UPL", [P, 8 * 2 * P], F32R, place["WBL"])
        W2T = sb("W2T", [P, 9, P])
        sg = sb("sg", [P, 2, GT])
        hb = sb("hb", [P, 2, GT])
        hs = sb("hs", [64, GT])
        PX = sb("PX", [P, 2, HK], F32, place["sg"])
        kr = sb("kr", [P, NHG, NB * S])
        QS = sb("QS", [P, NHG * GT], F32R, place["kr"])
        VX = sb("VX", [P, 2 * NC * P + 320], F32, place["kr"] + 4 * NHG * GT)
        CN = sb("CN", [P, NB, P])
        upraw = sb("upraw", [P, 8 * 2 * P], F32, place["CN"])
        cT = sb("cT", [P, NB * S])
        downw = sb("downw", [P, 8, P], F32, place["cT"])
        MT = sb("MT", [P, NB * S + 48])
        pt = sb("pt", [P, NC * P], F32, place["MT"])
        Vn = sb("Vn", [P, NB, P])
        bctx = sb("bctx", [1, NB * S])
        ct = sb("ct", [P, GT], F32R, place["bctx"])
        selB = sb("selB", [P, 16, 64], F32R, place["Vn"])
        selD = sb("selD", [16, 8], F32R)
        RK = sb("RK", [P, NHG, 6, 32], F32R)
        RQ = sb("RQ", [P, NHG, 5, 32], F32R, None)
        I = sb("I", [P, P])
        xn = sb("xn", [P, GT])
        WX = sb("WX", [P, 3, P])
        WQH = sb("WQH", [P, P], F32R)
        WQL = sb("WQL", [P, P], F32R)
        W0 = sb("W0", [P, P])
        graw = sb("graw", [24, P])
        GWH = sb("GWH", [P, 24], F32R)
        GWL = sb("GWL", [P, 24], F32R)
        kf = sb("kf", [P, GS], F32, place["sg"])
        kh = sb("kh", [P, GS], F32R, place["sg"] + 1 * 1280)
        kl = sb("kl", [P, GS], F32R, place["sg"] + 2 * 1280)
        PA = sb("PA", [P, GS], F32, place["sg"] + 3 * 1280)
        ptA = sb("ptA", [S, GT], F32, place["sg"] + 4 * 1280)
        qf = sb("qf", [P, GT], F32, place["W2T"])
        qh = sb("qh", [P, GT], F32R, place["W2T"] + 4 * GT)
        qf0 = sb("qf0", [P, GT], F32, place["MT"])
        qh0 = sb("qh0", [P, GT], F32R, place["MT"] + 4 * GT)
        sumT = sb("sumT", [P, P], F32, place["Vn"])
        recT = sb("recT", [P, P], F32, place["Vn"] + 4 * P)
        OTs = sb("OTs", [P, P], F32, place["Vn"] + 8 * P)
        bvr = sb("bvr", [P, P])
        tgbo = sb("tgbo", [P, P])
        gbr = sb("gbr", [P, 16])
        mask4 = sb("mask4", [P, HG])
        ones = sb("ones", [1, P])
        cols = sb("cols", [P, 4])
        tg = sb("tg", [P, 4])
        mhalf = sb("mhalf", [P, GB])
        st = sb("st", [P, GB, 6])
        mv = sb("mv", [P, GB, 2])
        ve = sb("ve", [P, GB])
        rstd = sb("rstd", [P, GB])
        amax = sb("amax", [P, GB])
        asum = sb("asum", [P, 3, GB])
        cmx = sb("cmx", [P, NHG, HG])
        lgT = sb("lgT", [16, GT], F32, place["bctx"] + 4 * GT)
        ql = sb("ql", [P, GT], F32R, place["lgT"])
        lgt = sb("lgt", [P, GB, 16])
        score = sb("score", [P, GB, 16])
        valsB = sb("valsB", [P, GB, 20])
        valsD = sb("valsD", [P, GB, 14])
        repB = sb("repB", [P, GB, 20])
        repD = sb("repD", [P, GB, 14])
        top = sb("top", [P, GB, 8])
        keepB = sb("keepB", [P, GB, 8])
        keepD = sb("keepD", [P, GB, 8])
        rsm = sb("rsm", [P, 2, GB])
        comb = sb("comb", [P, GB, 16])
        CH = sb("CH", [P, GB, 32], F32R)
        assert at[0] <= 229344, at[0]

        bank = [psum(f"bank{i}") for i in range(5)]
        Ybank = psum("Ybank", (P, 2 * 512))
        Tb = psum("Tb")
        bC = [Ybank[:, 0:GT], Ybank[:, GT:2 * GT], bank[4], Tb]
        bOut = [bank[3], Ybank[:, GT:2 * GT]]
        bR0 = [Ybank[:, 0:GT], Tb[:]]
        bVn = [Ybank[:, 0:GT], Ybank[:, GT:2 * GT], bank[3], bank[4]]
        Gb, Ub, Cb = bank[0:2], bank[2:4], bank[4]

        in_id, in_ctx, in_x0, in_x, in_small, in_w, in_w0, in_b0, in_gw, in_col = map(sem, (
            "in_id", "in_ctx", "in_x0", "in_x", "in_small", "in_w", "in_w0", "in_b0", "in_gw", "in_col"))
        gw_hi, sel_rdy = sem("gw_hi"), sem("sel_rdy")
        in_w13, in_w2, in_up, in_seed, in_vs = map(sem, ("in_w13", "in_w2", "in_up", "in_seed", "in_vs"))
        built = sem("built")
        d_set = sem("d_set")
        tg_rdy = sem("tg_rdy")
        su_mm, su_a, su_d = map(sem, ("su_mm", "su_a", "su_d"))
        stats, aggr, var_rdy, rstd_rdy, xn_rdy, xnT, xh_rdy, xl_rdy, x_done = map(sem, (
            "stats", "aggr", "var_rdy", "rstd_rdy", "xn_rdy", "xnT", "xh_rdy", "xl_rdy", "x_done"))
        a_sc, a_max, a_exp, a_ptr, a_ptc, a_sum, a_rec, a_r, a_pv = map(sem, (
            "a_sc", "a_max", "a_exp", "a_ptr", "a_ptc", "a_sum", "a_rec", "a_r", "a_pv"))
        v_mm, v_done, k_mm, k_f, k_h, k_l, rk_mm, kr_done, ks_done = map(sem, (
            "v_mm", "v_done", "k_mm", "k_f", "k_h", "k_l", "rk_mm", "kr_done", "ks_done"))
        route = {n: sem("route_" + n) for n in (
            "mm", "act", "lgT", "exp", "mx", "sub", "score", "vals", "top", "keep", "rep", "msk", "w", "sum", "rec",
            "comb", "hi", "lo", "tr", "rdy")}
        q_mm, q_f, q_h, q_l, qs_mm, qs_done, bo_add = map(sem, (
            "q_mm", "q_f", "q_h", "q_l", "qs_mm", "qs_done", "bo_add"))
        c_sc, c_mx, c_sub, c_exp, c_tr, c_ev, c_pv, c_sum, c_rs, c_norm, c_wo, c_fin = map(sem, (
            "c_sc", "c_mx", "c_sub", "c_exp", "c_tr", "c_ev", "c_pv", "c_sum", "c_rs", "c_norm", "c_wo", "c_fin"))
        vs_zero, vx_rdy, wo_rdy = sem("vs_zero"), sem("vx_rdy"), sem("wo_rdy")
        sh_up, sh_silu, sh_hid = map(sem, ("sh_up", "sh_silu", "sh_hid"))
        up_split, centred = sem("up_split"), sem("centred")
        stored = sem("stored")

        mB = Moe("B", 1, 16, 4, 8, 1, 2.5, 4, 0, 0)
        mD = Moe("D", 3, 8, 2, 8, 0, 1.0, 8, 8, 4)
        for m in (mB, mD):
            m.g_done, m.u_done = sem(m.name + "_gate"), sem(m.name + "_up")
            m.c_done, m.dn = sem(m.name + "_spread"), sem(m.name + "_down")
            m.s_done, m.t2 = sem(m.name + "_silu"), sem(m.name + "_gated")
            m.h_done = sem(m.name + "_hidden")
        mB.wh, mB.wl, mB.wd, mB.sel, mB.vals, mB.rep, mB.keep = WBH, WBL, W2T, selB, valsB, repB, keepB
        mD.wh, mD.wl, mD.wd, mD.sel, mD.vals, mD.rep, mD.keep = UPH, UPL, downw, selD, valsD, repD, keepD
        mB.gcol, mB.ucol = (lambda k: k * P), (lambda k: (8 + k) * P)
        mD.gcol, mD.ucol = (lambda k: 2 * k * P), (lambda k: (2 * k + 1) * P)
        mB.gw, mD.gw = 0, 16
        mB.crow, mD.crow = 96, 0
        mB.spread = lambda k: selB[96:P, 2 * k:2 * k + 2, :].rearrange("p e i -> p (e i)")
        mD.spread = lambda k: selD[:, k:k + 1].to_broadcast([16, P])
        mB.tg, mD.tg = 2, 3

        passed = {e: sem(f"passed_{n}") for e, n in (
            (nc.vector, "dve"), (nc.tensor, "pe"), (nc.gpsimd, "pool"))}

        def wait_apart(eng, semaphore, value):
            eng.wait_ge(semaphore, value)
            eng.sem_inc(passed[eng], 1)

        def slot(g):
            return (g % 2) * GT

        def used(g, k):
            return not (isinstance(g, int) and g == 0 and k < 2)

        pieces = value_pieces()

        block = stack.enter_context(nc.Block())

        @block.sync
        def _(sp):
            def load_x(g, signal):
                sp.dma_start(X[:, g * GT:(g + 1) * GT].rearrange("p (b d) -> p b d", b=GB),
                             x[g * GB:(g + 1) * GB].rearrange("b t d -> t b d")).then_inc(signal, 16)

            sp.dma_start(I[:], ident).then_inc(in_id, 16)
            sp.dma_start(CN[0:S, :, :], ctx.rearrange("b s d -> s b d")).then_inc(in_ctx, 16)
            load_x(0, in_x0)
            raw = w13raw[:, 0:16 * P].rearrange("p (u j d) -> p u j d", u=2, j=8)
            for e in range(2):
                for u in range(2):
                    src = w13[e::2, 64 * u:64 * u + 64, :].rearrange("j i d -> i j d")
                    sp.dma_start(raw[64 * e:64 * e + 64, u], src).then_inc(in_w13, 16)
            sp.dma_start(w13raw[0:64, 16 * P:17 * P], w13_s[64:P, :]).then_inc(in_w13, 16)
            sp.dma_start(w13raw[64:P, 16 * P:17 * P], w13_s[0:64, :]).then_inc(in_w13, 16)
            load_x(1, in_x)
            sp.dma_start(w2raw[:, 0:NB * 64].rearrange("p (e i) -> p e i", e=16),
                         w2.rearrange("e d i -> d e i")).then_inc(in_w2, 16)
            for n in range(2):
                sp.dma_start(w2raw[:, NB * 64 + 64 * n:NB * 64 + 64 * n + 64], w2_s).then_inc(in_w2, 16)
            sp.dma_start(cols[:, 1:2], bq.unsqueeze(1)).then_inc(in_col, 16)
            sp.dma_start(cols[:, 2:3], bk.unsqueeze(1)).then_inc(in_col, 16)
            load_x(2, in_x)
            load_x(3, in_x)
            sp.wait_ge(vs_zero, 1)
            sp.wait_ge(vs_zero, 1)
            sp.wait_ge(v_done, NG)
            for h, c, row, key, n in pieces:
                col = c * VW + (h % UH - chunk_head(c)) * HD
                sp.dma_start(VS[row:row + n, :, col:col + HD],
                             Vn[key:key + n, :, h * HD:(h + 1) * HD]).then_inc(in_vs, 16)
            sp.wait_ge(a_pv, START + NG)
            sp.wait_ge(rk_mm, START + NG * NHG)
            sp.dma_start(upraw[:].rearrange("p (e n) -> p e n", e=8),
                         up.rearrange("e k n -> k e n")).then_inc(in_up, 16)
            sp.dma_start(downw[:], down.rearrange("e k n -> k e n")).then_inc(in_up, 16)
            sp.wait_ge(ks_done, NG * NHG * HG)
            for n in range(2):
                sp.dma_start(VX[:, n * NC * P:(n + 1) * NC * P], vs_seed).then_inc(in_seed, 16)
            for g in range(NG):
                sp.wait_ge(x_done, START + mD.x_base + g + 1)
                sp.dma_start(out[g * GB:(g + 1) * GB].rearrange("b t d -> t b d"),
                             X[:, g * GT:(g + 1) * GT].rearrange("p (b d) -> p b d", b=GB)).then_inc(stored, 16)
            sp.wait_ge(stored, 16 * NG)

        @block.gpsimd
        def _(pool):
            nc.gpsimd.memset(mhalf[:], -0.5)
            nc.gpsimd.memset(valsB[:], LOW)
            nc.gpsimd.memset(valsD[:], LOW)
            nc.gpsimd.memset(keepB[:], LOW)
            nc.gpsimd.memset(keepD[:], LOW)
            nc.gpsimd.memset(RK[:].bitcast(F32), 0.0)
            nc.gpsimd.memset(RQ[:].bitcast(F32), 0.0)
            nc.gpsimd.memset(ones[:], 1.0).then_inc(built, 1)
            pool.dma_start(graw[0:16, :], gate_w).then_inc(in_gw, 16)
            pool.dma_start(graw[16:24, :], router_w).then_inc(in_gw, 16)
            pool.dma_start(cols[:, 0:1], b0.unsqueeze(1)).then_inc(in_b0, 16)
            for dst, src in ((tg[:, 0:2], g_xattn), (tg[:, 2:4], g_ffn)):
                pool.dma_start(dst, src.partition_broadcast(P)).then_inc(in_small, 16)

            def inv_std(n):
                pool.wait_ge(var_rdy, n)
                nc.gpsimd.tensor_tensor(rstd[:], ve[:], mhalf[:], ALU.pow).then_inc(rstd_rdy, 1)

            def spread_keys(g, split_terms):
                for s in split_terms:
                    keys = kr[:, s, bass.ds(g * GS, GS)].rearrange("p (b k) -> p b k", b=GB)
                    dst = KS[:, bass.ds(g * (GB * HK), GB * HK)].rearrange(
                        "p (b s h k) -> p b s h k", b=GB, s=NHG, h=HG)[:, :, s]
                    for h in range(HG):
                        nc.gpsimd.tensor_tensor(dst[:, :, h], keys,
                                                mask4[:, h:h + 1].unsqueeze(2).to_broadcast([P, GB, S]),
                                                ALU.mult).then_inc(ks_done, 1)

            pool.wait_ge(built, 1)
            inv_std(1)
            for dst, src in ((bvr[:], bv), (tgbo[:], bo), (gbr[:], gate_b)):
                pool.dma_start(dst, src.partition_broadcast(P)).then_inc(in_small, 16)
            nc.gpsimd.memset(VS[:], 0.0).then_inc(vs_zero, 1)
            with pool.Fori(1, NG - 1) as g:
                inv_std(g + 1)
            pool.wait_ge(d_set, 1)
            for g in range(NG - 1):
                if g == 0:
                    inv_std(NG)
                pool.wait_ge(kr_done, START + (g + 1) * NHG)
                spread_keys(g, (0,))
                if g == 0:
                    inv_std(NG + 1)
                spread_keys(g, (1,))
            with pool.Fori(0, NG - 2) as g:
                inv_std(NG + g + 2)
                spread_keys(g, (2, 3))
            inv_std(2 * NG)
            spread_keys(NG - 2, (2, 3))
            pool.wait_ge(kr_done, START + NG * NHG)
            spread_keys(NG - 1, range(NHG))
            inv_std(2 * NG + 1)

            def split_up(n):
                part = bass.ds(n * 512, 512)
                nc.gpsimd.tensor_copy(UPH[:, part], upraw[:, part]).then_inc(up_split, 1)
                wait_apart(pool, up_split, 2 * n + 1)
                nc.gpsimd.tensor_tensor(UPL[:, part], upraw[:, part], UPH[:, part].bitcast(F32),
                                        ALU.subtract).then_inc(up_split, 1)

            def add_bo(g):
                wait_apart(pool, xn_rdy, 2 * NG + g + 1)
                xg = X[:, bass.ds(g * GT, GT)].rearrange("p (b d) -> p b d", b=GB)
                nc.gpsimd.tensor_tensor(xg, xg, tgbo[:].unsqueeze(1).to_broadcast([P, GB, P]),
                                        ALU.add).then_inc(bo_add, 1)

            def norm_apply(n, g):
                wait_apart(pool, xnT, n - 1)
                rows = [xn[:].rearrange("p (b d) -> p b d", b=GB),
                        X[:, bass.ds(g * GT, GT)].rearrange("p (b d) -> p b d", b=GB)]
                nc.gpsimd.tensor_tensor(rows[0], rows[1], mv[:, :, 0:1].to_broadcast([P, GB, P]),
                                        ALU.subtract).then_inc(centred, 1)
                wait_apart(pool, centred, n - 2 * NG - 1)
                nc.gpsimd.tensor_tensor(rows[0], rows[0], rstd[:].unsqueeze(2).to_broadcast([P, GB, P]),
                                        ALU.mult).then_inc(xn_rdy, 1)

            def place_values(n, par, first=False):
                if not first:
                    wait_apart(pool, c_pv, START + n - 1)
                src = VS[:, bass.ds(n, 1), :].rearrange("p a (u j d) -> p (a u) j d", u=NU, j=CU)
                step = 2 * P + 3 * HD
                half = CU * P + UD
                for j in (0, 1):
                    at = par * NC * P + j * P + chunk_head(j) * HD
                    dst = VX[:, at:at + NU * half].rearrange("p (u r) -> p u r", u=NU)[:, :, 0:2 * step]
                    dst = dst.rearrange("p u (i r) -> p u i r", i=2)[:, :, :, 0:VW]
                    nc.gpsimd.tensor_copy(dst, src[:, :, j:j + 3:2, :])
                for u in range(NU):
                    at = par * NC * P + u * half + 4 * P + chunk_head(4) * HD
                    i = nc.gpsimd.tensor_copy(VX[:, at:at + 2 * HD], src[:, u, 4, 0:2 * HD])
                i.then_inc(vx_rdy, 1)

            def c_body(g, last):
                for t in range(GB):
                    if not (last and t == GB - 1):
                        place_values(GB * g + t + 1, (t + 1) % 2)
                    if t == 0:
                        add_bo(g)
                    if t == 1:
                        split_up(g)
                    if t == GB - 1 and not last:
                        inv_std(2 * NG + 3 + g)
                        norm_apply(2 * NG + 3 + g, (g + 2) % NG)

            pool.wait_ge(in_seed, 32)
            pool.wait_ge(in_vs, 16 * len(pieces))
            place_values(0, 0, first=True)
            inv_std(2 * NG + 2)
            norm_apply(2 * NG + 2, 1)
            pool.wait_ge(mB.dn, START + NG * mB.units)
            pool.wait_ge(in_up, 32)
            with pool.Fori(0, NG - 1) as g:
                c_body(g, False)
            c_body(NG - 1, True)
            with pool.Fori(0, NG - 1) as g:
                inv_std(3 * NG + g + 2)

        @block.tensor
        def _(pe):
            mm, tr = nc.tensor.matmul, nc.tensor.transpose
            for s in (rk_mm, a_ptr, a_pv, mB.dn, mD.dn, c_tr, c_pv, c_wo):
                pe.sem_inc(s, START)

            pe.wait_ge(in_id, 16)
            pe.wait_ge(in_ctx, 16)
            for g in range(NG):
                for b in range(GB):
                    i = tr(bank[g][:, b * S:(b + 1) * S], CN[0:S, g * GB + b, :], I[0:S, 0:S])
                i.then_inc(su_mm, 1)
            pe.wait_ge(in_w, 16 * 4)
            for n in range(4):
                i = tr(bank[4][:, n * P:(n + 1) * P], wraw[:, n, :], I[:])
            i.then_inc(su_mm, 1)
            pe.wait_ge(in_gw, 32)
            i = tr(Tb[:, 0:24], graw[:], I[0:24, 0:24])
            i.then_inc(su_mm, 1)
            pe.wait_ge(in_w0, 16)
            for g in range(NG):
                pe.wait_ge(su_a, g + 1)
                mm(bank[g][:, 0:GS], W0[:], cT[:, g * GS:(g + 1) * GS], start=True, stop=True).then_inc(su_mm, 1)
            pe.wait_ge(in_b0, 16)
            for g in range(NG):
                if g == 2:
                    pe.wait_ge(su_a, 6)
                    pe.wait_ge(su_d, 1)
                if g == 3:
                    pe.wait_ge(su_d, 2)
                mm(bC[g][0:1, 0:GS], cols[:, 0:1], cT[:, g * GS:(g + 1) * GS],
                   start=True, stop=True).then_inc(su_mm, 1)
            pe.wait_ge(in_w13, 16 * 6)
            for n in range(5):
                if n < 4:
                    pe.wait_ge(su_a, 7 + n)
                else:
                    pe.wait_ge(su_d, 5)
                for j in range(4 * n, min(17, 4 * n + 4)):
                    i = tr(bank[n][:, j % 4 * P:j % 4 * P + P], w13raw[:, j * P:(j + 1) * P], I[:])
                i.then_inc(su_mm, 1)

            def norm_T(n):
                pe.wait_ge(xn_rdy, n)
                for t in range(GB):
                    i = tr(Tb[:, t * P:(t + 1) * P], xn[:, t * P:(t + 1) * P], I[:])
                i.then_inc(xnT, 1)

            pe.wait_ge(su_d, 6)
            norm_T(1)
            pe.wait_ge(in_w2, 16 * 3)
            for n in range(3):
                pe.wait_ge(su_a, 11 + n)
                pe.wait_ge(su_d, 7 + n)
                for j in range(4 * n, min(9, 4 * n + 4)):
                    i = tr(bank[n][:, j % 4 * P:j % 4 * P + P], w2raw[:, j * P:(j + 1) * P], I[:])
                i.then_inc(su_mm, 1)
            for g in range(NG):
                if g >= 2:
                    pe.wait_ge(su_a, 12 + g)
                    pe.wait_ge(su_d, 8 + g)
                for t in range(GB):
                    b = g * GB + t
                    i = mm(bVn[g][0:S, t * P:(t + 1) * P], cT[:, b * S:(b + 1) * S], WX[:, 1, :], start=True, stop=True)
                i.then_inc(v_mm, 1)

            bT, bK, bO, bV = bank[1], bank[2], bank[4], (bank[0], bank[3])

            def a_scores(g):
                pe.wait_ge(xh_rdy, g + 1)
                mm(Ybank[:, bass.ds(slot(g), GS)], ones[0:1, :], bctx[0:1, bass.ds(g * GS, GS)], start=True, stop=False,
                   skip_group_check=True)
                for t in range(GB):
                    i = mm(Ybank[:, bass.ds(slot(g) + t * S, S)], xf[:, t * P:(t + 1) * P],
                           MT[:, bass.ds(g * GS + t * S, S)], start=False, stop=t == GB - 1, skip_group_check=True)
                i.then_inc(a_sc, 1)

            def a_keys(g):
                mm(bK[:, 0:GS], WX[:, 0, :], cT[:, bass.ds(g * GS, GS)], start=True, stop=True).then_inc(k_mm, 1)

            def a_repeat(g, terms):
                if terms[0] == 0:
                    pe.wait_ge(k_l, g + 1)
                for s in terms:
                    pe.wait_ge(kr_done, START + NHG * g + max(0, s - 1))
                    mm(bV[s % 2][:, 0:GS], RK[:, s, 2:6, :].rearrange("p a b -> p (a b)"), kh[:], start=True, stop=False)
                    mm(bV[s % 2][:, 0:GS], RK[:, s, 0:4, :].rearrange("p a b -> p (a b)"), kl[:],
                       start=False, stop=True).then_inc(rk_mm, 1)

            def a_probs_T(g):
                pe.wait_ge(a_exp, g + 1)
                pe.wait_ge(a_ptc, START + g)
                for t in range(GB):
                    i = tr(bT[0:S, t * P:(t + 1) * P], PA[:, t * S:(t + 1) * S], I[:])
                i.then_inc(a_ptr, 1)

            def a_mix(g):
                pe.wait_ge(a_ptc, START + g + 1)
                pe.wait_ge(x_done, START + g)
                for t in range(GB):
                    i = mm(bO[:, t * P:(t + 1) * P], ptA[:, t * P:(t + 1) * P],
                           CN[0:S, bass.ds(g * GB + t, 1), :].rearrange("p a d -> p (a d)"), start=True, stop=True)
                i.then_inc(a_pv, 1)

            pe.wait_ge(built, 1)
            pe.wait_ge(d_set, 1)
            pe.wait_ge(v_done, 2)
            pe.wait_ge(su_a, 18)
            a_scores(0)
            norm_T(2)
            pe.wait_ge(v_done, NG)

            def a_body(g, scores, norm):
                if scores:
                    a_scores(g + 1)
                a_mix(g)
                if norm:
                    norm_T(g + 3)
                a_repeat(g, (0, 1))
                a_probs_T(g + 1)
                a_keys(g + 1)
                a_repeat(g, (2, 3))

            def split3(dst, w, col, xs, inc):
                for n, (wp, xp) in enumerate(((w[0], xh), (w[0], xl), (w[1], xh))):
                    i = mm(dst, wp[:, col:col + P], xp[:, bass.ds(xs, GT)], start=n == 0, stop=n == 2)
                i.then_inc(inc, 1)

            def m_gate(m, g, k):
                split3(Gb[k % 2][:], (m.wh, m.wl), m.gcol(k), slot(g), m.g_done)

            def m_linear(m, g, k):
                split3(Ub[k % 2][:], (m.wh, m.wl), m.ucol(k), slot(g), m.u_done)

            def m_up(m, g, k, ring=True):
                if ring:
                    pe.wait_ge(m.t2, m.units * g + k - 1)
                if k == 0:
                    pe.wait_ge(xl_rdy, m.lo_base + g + 1)
                m_gate(m, g, k)
                m_linear(m, g, k)

            def m_spread(m, g, k):
                pe.wait_ge(m.h_done, START + m.units * g + k)
                if k == 0:
                    pe.wait_ge(route["rdy"], m.route_base + g + 1)
                mm(Cb[:], m.spread(k), ct[m.crow:m.crow + 2 * m.E, :], start=True, stop=True).then_inc(m.c_done, 1)

            def m_down(m, g, k):
                if k == m.units:
                    wait_apart(pe, sh_hid, g + 1)
                else:
                    wait_apart(pe, m.h_done, START + m.units * g + k + 1)
                if k == 0:
                    pe.wait_ge(x_done, START + m.x_base + g - 1)
                rows = slice(0, 64) if k == m.units else slice(0, P)
                for t in range(GB):
                    lhs = hs[rows, t * P:(t + 1) * P] if k == m.units else hb[:, k % 2, t * P:(t + 1) * P]
                    i = mm(Ybank[:, bass.ds(slot(g) + t * P, P)], lhs, m.wd[rows, k, :],
                           start=(k == 0 and t == 0), stop=k == m.units - 1, skip_group_check=True)
                if k < m.units:
                    i.then_inc(m.dn, 1)

            def m_logits(m, g):
                pe.wait_ge(xl_rdy, m.lo_base + g + 1)
                for n, (wp, xp) in enumerate(((GWH, xh), (GWH, xl), (GWL, xh))):
                    i = mm(Tb[0:m.E, :], wp[:, m.gw:m.gw + m.E], xp[:, bass.ds(slot(g), GT)], start=n == 0, stop=n == 2)
                i.then_inc(route["mm"], 1)

            def m_logits_T(m, g):
                wait_apart(pe, route["act"], m.route_base + g + 1)
                for t in range(GB):
                    i = tr(Tb[:, t * m.E:(t + 1) * m.E], lgT[0:m.E, t * P:(t + 1) * P], I[0:m.E, 0:m.E])
                i.then_inc(route["lgT"], 1)

            def m_route_T(m, g):
                pe.wait_ge(route["lo"], m.route_base + g + 1)
                for t in range(GB):
                    i = tr(Tb[0:2 * m.E, t * P:(t + 1) * P], CH[:, t, 0:2 * m.E].bitcast(F32), I[:])
                i.then_inc(route["tr"], 1)

            def m_body(m, g, nxt, then=None):
                more = nxt is not None and nxt[1] is m
                m_spread(m, g, 0)
                route_next = nxt is not None and nxt[1] is not None
                for k in range(m.units):
                    if k == m.units - 1 and route_next:
                        m_route_T(nxt[1], nxt[2])
                    if k + 2 < m.units:
                        m_up(m, g, k + 2)
                    elif more:
                        m_up(m, g + 1, k + 2 - m.units)
                    if k == 0 and m.shared:
                        split3(Tb[:], (m.wh, m.wl), 2 * m.units * P, slot(g), sh_up)
                    if k + 1 < m.units:
                        m_spread(m, g, k + 1)
                    if k == 4 and route_next:
                        m_logits_T(nxt[1], nxt[2])
                    m_down(m, g, k)
                    if k == 1 and m.shared:
                        m_down(m, g, m.units)
                    if k == 1 and nxt is not None:
                        norm_T(nxt[0])
                    if k == 3 and route_next:
                        m_logits(nxt[1], nxt[2])
                    if then:
                        then(k)

            a_probs_T(0)
            a_keys(0)
            with pe.Fori(0, NG - 2) as g:
                a_body(g, True, True)
            pe.wait_ge(sel_rdy, 1)
            a_body(NG - 2, True, True)
            m_logits(mB, 0)
            a_mix(NG - 1)
            m_logits_T(mB, 0)
            a_repeat(NG - 1, range(NHG))

            m = mB
            pe.wait_ge(kr_done, START + NG * NHG)
            m_up(m, 0, 0, ring=False)
            m_route_T(m, 0)
            m_up(m, 0, 1, ring=False)
            pe.wait_ge(x_done, START + NG)
            m_body(m, 0, (NG + 2, m, 1))
            with pe.Fori(1, NG - 1) as g:
                m_body(m, g, (NG + g + 2, m, g + 1))

            bS3 = [bank[0], bank[1], bank[2], bank[0]]
            bP = [bank[4], Ybank[:, 0:GT], bank[4]]

            def c_query(g):
                pe.wait_ge(xl_rdy, NG + g + 1)
                for n, (wp, xp) in enumerate(((WQH, xh), (WQH, xl), (WQL, xh))):
                    i = mm(Tb[:], wp[:], xp[:, bass.ds(slot(g), GT)], start=n == 0, stop=n == 2)
                i.then_inc(q_mm, 1)

            def c_repeat(g, s):
                if s == 0:
                    pe.wait_ge(q_l, g + 1)
                pe.wait_ge(qs_done, NHG * g + s)
                mm(Tb[:], RQ[:, s, 1:5, :].rearrange("p a b -> p (a b)"), qh[:], start=True, stop=False)
                mm(Tb[:], RQ[:, s, 0:4, :].rearrange("p a b -> p (a b)"), ql[:],
                   start=False, stop=True).then_inc(qs_mm, 1)

            def c_repeat_first(s):
                if s == 0:
                    pe.wait_ge(q_l, 1)
                if s >= 2:
                    pe.wait_ge(qs_done, s - 1)
                mm(bR0[s % 2], RQ[:, s, 1:5, :].rearrange("p a b -> p (a b)"), qh0[:], start=True, stop=False)
                mm(bR0[s % 2], RQ[:, s, 0:4, :].rearrange("p a b -> p (a b)"), ql[:],
                   start=False, stop=True).then_inc(qs_mm, 1)

            def c_scores(g, t, s, first=False):
                n = GB * g + t
                if t == 0:
                    pe.wait_ge(qs_done, NHG * g + s + 1)
                if s == 0:
                    pe.wait_ge(c_sub, len(SUB_EXP) * n)
                if s == 1 and not (t == 0 and first):
                    pe.wait_ge(c_exp, NHG * n - 1)
                if s == 3:
                    pe.wait_ge(c_sub, len(SUB_EXP) * n + 1)
                q = QS[:, s * GT + t * P:s * GT + (t + 1) * P]
                mm(bS3[s][:, 0:HG * S], q, KS[:, bass.ds(n * HK + s * HG * S, HG * S)],
                   start=True, stop=True).then_inc(c_sc, 1)

            need = [2, 4, 4]

            def c_transpose(g, t, r):
                n = GB * g + t
                pe.wait_ge(c_exp, NHG * n + need[r])
                pe.wait_ge(c_ev, START + 3 * n + (1 if r == 2 else 0))
                for c in range(4 * r, min(NC, 4 * r + 4)):
                    w = chunk_rows(c)
                    i = tr(bP[r][0:w, c % 4 * P:c % 4 * P + P], PX[:, t % 2, chunk_col(c):chunk_col(c) + w], I[:])
                i.then_inc(c_tr, 1)

            def c_mix(g, t, u, first):
                n = GB * g + t
                if u == 0:
                    pe.wait_ge(c_ev, START + 3 * n + 3)
                    pe.wait_ge(vx_rdy, n + 1)
                    if not (first and t == 0):
                        pe.wait_ge(c_fin, START + n - 1)
                    if first and t == 1:
                        pe.wait_ge(x_done, START + 2 * NG)
                for c in range(u * CU, (u + 1) * CU):
                    w = chunk_rows(c)
                    v = (t % 2 * NC + c) * P
                    i = mm(bOut[t % 2][:, u * P:(u + 1) * P], VX[0:w, v:v + P], pt[0:w, c * P:(c + 1) * P],
                           start=c % CU == 0, stop=c % CU == CU - 1)
                if u == NU - 1:
                    i.then_inc(c_pv, 1)

            def c_project(g, t):
                n = GB * g + t
                pe.wait_ge(c_norm, START + n + 1)
                mm(bOut[t % 2][:, 2 * P:3 * P], OTs[:], WX[:, 2, :], start=True, stop=True).then_inc(c_wo, 1)

            def c_body(g, first, last):
                for t in range(GB):
                    n1 = (g, t + 1) if t + 1 < GB else (g + 1, 0)
                    ahead = t + 1 < GB or not last
                    end = t == GB - 1 and last
                    for s in range(3):
                        if s == 0 and ahead:
                            c_scores(*n1, 0)
                        c_transpose(g, t, s)
                        if t == 3 and not last and s == 0:
                            c_repeat(g + 1, 3)
                        if s and ahead:
                            c_scores(*n1, s)
                        if s == 0 and (t > 1 or not first):
                            c_project(*((g, t - 2) if t > 1 else (g - 1, t + 2)))
                        if s == 2 and t == 1:
                            if not last:
                                c_query(g + 1)
                            else:
                                m_logits(mD, 0)
                    if end:
                        pe.wait_ge(up_split, 8)
                        pe.wait_ge(in_up, 32)
                        pe.wait_ge(c_exp, NHG * NB)
                        m_gate(mD, 0, 0)
                        m_linear(mD, 0, 0)
                    if ahead:
                        c_scores(*n1, 3)
                    if t == 2 and not last:
                        c_repeat(g + 1, 0)
                    c_mix(g, t, 0, first)
                    if t == 0:
                        norm_T(2 * NG + 2 + g)
                    if t == 2 and not last:
                        c_repeat(g + 1, 1)
                    if end:
                        m_gate(mD, 0, 1)
                        c_project(g, t - 1)
                    c_mix(g, t, 1, first)
                    if t == 2 and not last:
                        c_repeat(g + 1, 2)
                    if t == 1 and last:
                        m_logits_T(mD, 0)

            def c_ahead(k):
                if k == 3:
                    c_query(0)
                if k == 5:
                    pe.wait_ge(x_done, START + 2 * NG - 1)
                    c_repeat_first(0)
                    c_repeat_first(1)
                if k >= 6:
                    c_repeat_first(k - 4)
                if k == mB.units - 1:
                    pe.wait_ge(ks_done, NG * NHG * HG)
                    pe.wait_ge(mB.h_done, START + mB.units * (NG - 1) + mB.units)
                    for s in range(3):
                        c_scores(0, 0, s, first=True)

            m_body(mB, NG - 1, (2 * NG + 1, None, 0), c_ahead)
            pe.wait_ge(wo_rdy, 1)
            c_scores(0, 0, 3)
            c_body(0, True, False)
            with pe.Fori(1, NG - 1) as g:
                c_body(g, False, False)
            c_body(NG - 1, False, True)
            m_route_T(mD, 0)
            pe.wait_ge(c_fin, START + NB - 1)
            m_linear(mD, 0, 1)
            c_project(NG - 1, GB - 1)

            m = mD
            m_body(m, 0, (3 * NG + 2, m, 1))
            with pe.Fori(1, NG - 1) as g:
                m_body(m, g, (3 * NG + g + 2, m, g + 1))
            m_body(m, NG - 1, None)

        @block.scalar
        def _(act):
            A = nc.scalar.activation
            for s in (kr_done, a_ptc, c_ev):
                act.sem_inc(s, START)
            act.dma_start(W0[:], w0).then_inc(in_w0, 16)
            for n, w in enumerate((wq, wk, wv, wo)):
                act.dma_start(wraw[:, n, :], w).then_inc(in_w, 16)

            for g in range(NG):
                act.wait_ge(su_mm, g + 1)
                A(cT[:, g * GS:(g + 1) * GS], bank[g][:, 0:GS], ACT.Copy).then_inc(su_a, 1)
            act.wait_ge(su_mm, 5)
            A(WQH[:], bank[4][:, 0:P], ACT.Copy).then_inc(su_a, 1)
            A(WX[:].rearrange("p a d -> p (a d)"), bank[4][:, P:4 * P], ACT.Copy).then_inc(su_a, 1)
            for g in range(NG):
                act.wait_ge(su_mm, 7 + g)
                A(MT[:, g * GS:(g + 1) * GS], bank[g][:, 0:GS], ACT.Copy).then_inc(su_a, 1)
            act.wait_ge(in_small, 16 * 5)
            A(tg[:], tg[:], ACT.Tanh).then_inc(tg_rdy, 1)
            act.wait_ge(in_col, 32)
            A(cols[:, 1:2], cols[:, 1:2], ACT.Copy, scale=QSCALE).then_inc(tg_rdy, 1)
            for n in range(5):
                act.wait_ge(su_mm, 15 + n)
                w = (min(17, 4 * n + 4) - 4 * n) * P
                A(WBH[:, 4 * n * P:4 * n * P + w], bank[n][:, 0:w], ACT.Copy).then_inc(su_a, 1)
            act.wait_ge(xnT, 1)
            A(xf[:], Tb[:], ACT.Copy).then_inc(xh_rdy, 1)
            for n in range(3):
                act.wait_ge(su_mm, 20 + n)
                w = min(9, 4 * n + 4) - 4 * n
                A(W2T[:, 4 * n:4 * n + w, :].rearrange("p a d -> p (a d)"), bank[n][:, 0:w * P],
                  ACT.Copy).then_inc(su_a, 1)

            def norm_hi(n, dst):
                act.wait_ge(xnT, n)
                A(dst, Tb[:], ACT.Copy).then_inc(xh_rdy, 1)

            norm_hi(2, xf[:])

            def a_exps(g):
                act.wait_ge(a_max, g + 1)
                act.wait_ge(a_ptr, START + g)
                for t in range(GB):
                    i = A(PA[:, t * S:(t + 1) * S], Ybank[:, bass.ds(slot(g) + t * S, S)], ACT.Exp,
                          bias=amax[:, t:t + 1])
                i.then_inc(a_exp, 1)

            def a_probs(g):
                act.wait_ge(a_ptr, START + g + 1)
                act.wait_ge(a_pv, START + g)
                A(ptA[:], bank[1][0:S, :], ACT.Copy).then_inc(a_ptc, 1)

            def a_body(g, nxt, more):
                act.wait_ge(k_mm, g + 1)
                A(kf[:], bank[2][:, 0:GS], ACT.Identity, bias=cols[:, 2:3]).then_inc(k_f, 1)
                act.wait_ge(k_f, g + 1)
                act.wait_ge(rk_mm, START + NHG * g)
                A(kh[:], kf[:], ACT.Copy).then_inc(k_h, 1)
                if more:
                    a_exps(g + 1)
                else:
                    m_route_act(mB, 0)
                for s in range(NHG):
                    act.wait_ge(rk_mm, START + NHG * g + s + 1)
                    A(kr[:, s, bass.ds(g * GS, GS)], bank[3 * (s % 2)][:, 0:GS], ACT.Copy).then_inc(kr_done, 1)
                    if s == 0 and nxt is not None:
                        norm_hi(g + 3, nxt)
                    if s == 1 and more:
                        a_probs(g + 1)

            def m_silu(m, g, k):
                act.wait_ge(m.g_done, m.units * g + k + 1)
                if used(g, k):
                    act.wait_ge(m.h_done, START + m.units * g + k - 1)
                A(sg[:, k % 2, :], Gb[k % 2][:], ACT.Silu).then_inc(m.s_done, 1)

            def m_route_act(m, g):
                act.wait_ge(route["mm"], m.route_base + g + 1)
                if m is mB:
                    A(lgT[0:m.E, :], Tb[0:m.E, :], ACT.Tanh, scale=0.5).then_inc(route["act"], 1)
                else:
                    A(lgT[0:m.E, :], Tb[0:m.E, :], ACT.Copy).then_inc(route["act"], 1)

            def m_route_exp(m, g):
                if m is mD:
                    act.wait_ge(route["sub"], g + 1)
                    A(score[:, :, 0:8], lgt[:, :, 0:8], ACT.Exp).then_inc(route["exp"], 1)

            def m_route_copy(m, g):
                act.wait_ge(route["tr"], m.route_base + g + 1)
                A(ct[m.crow:m.crow + 2 * m.E, :], Tb[0:2 * m.E, :], ACT.Copy).then_inc(route["rdy"], 1)

            def m_body(m, g, nxt, then=None, begun=0):
                for k in range(m.units):
                    if k >= begun:
                        m_silu(m, g, k)
                    if then:
                        then(k)
                    if nxt is not None and k == 2:
                        norm_hi(nxt[0], xh[:, bass.ds(slot(nxt[2]), GT)])
                    if nxt is not None and nxt[1] is not None and k == 4:
                        m_route_act(nxt[1], nxt[2])
                    if nxt is not None and nxt[1] is not None and k == 5:
                        m_route_exp(nxt[1], nxt[2])
                    if nxt is not None and nxt[1] is not None and k == m.units - 1:
                        m_route_copy(nxt[1], nxt[2])
                    if k == 1 and m.shared:
                        act.wait_ge(sh_up, g + 1)
                        if used(g, 0):
                            act.wait_ge(m.dn, START + m.units * (g - 1) + 3)
                        A(hs[:], Tb[64:P, :], ACT.Silu).then_inc(sh_silu, 1)

            a_exps(0)
            a_probs(0)
            with act.Fori(0, NG - 2) as g:
                a_body(g, xf[:], True)
            a_body(NG - 2, xh[:, 0:GT], True)
            a_body(NG - 1, None, False)

            m = mB
            m_silu(m, 0, 0)
            m_route_copy(m, 0)
            m_silu(m, 0, 1)
            m_body(m, 0, (NG + 2, m, 1), begun=2)
            with act.Fori(1, NG - 1) as g:
                m_body(m, g, (NG + g + 2, m, g + 1))

            def c_query(g, to=qf):
                act.wait_ge(q_mm, g + 1)
                if to is qf:
                    act.wait_ge(q_l, g)
                A(to[:], Tb[:], ACT.Identity, bias=cols[:, 1:2], scale=QSCALE).then_inc(q_f, 1)

            def c_repeat(g, s, src=Tb):
                act.wait_ge(qs_mm, NHG * g + s + 1)
                A(QS[:, s * GT:(s + 1) * GT], src[:], ACT.Copy).then_inc(qs_done, 1)

            bSa = [bank[0], bank[1], bank[2], bank[0]]

            def c_exps(g, t, s, first=False):
                n = GB * g + t
                p = PX[:, t % 2, s * HG * S:(s + 1) * HG * S]
                if s in BIAS_EXP:
                    act.wait_ge(c_mx, NHG * n + s + 1)
                    if not first:
                        act.wait_ge(c_tr, START + 3 * n - 3)
                    for h in range(HG):
                        i = A(p[:, h * S:(h + 1) * S], bSa[s][:, h * S:(h + 1) * S], ACT.Exp,
                              bias=cmx[:, s, h:h + 1])
                else:
                    act.wait_ge(c_sub, len(SUB_EXP) * n + SUB_EXP.index(s) + 1)
                    i = A(p, p, ACT.Exp)
                i.then_inc(c_exp, 1)

            bPa = [bank[4], Ybank[:, 0:GT], bank[4]]

            def c_copy(g, t, r):
                n = GB * g + t
                act.wait_ge(c_tr, START + 3 * n + r + 1)
                act.wait_ge(c_pv, START + n)
                w = min(NC, 4 * r + 4) * P - 4 * r * P
                A(pt[:, 4 * r * P:4 * r * P + w], bPa[r][:, 0:w], ACT.Copy).then_inc(c_ev, 1)

            def c_sums(g, t):
                n = GB * g + t
                act.wait_ge(c_pv, START + n + 1)
                act.wait_ge(c_rs, START + n)
                A(sumT[0:UD, :], bOut[t % 2][UD:P, 0:P], ACT.Copy)
                A(sumT[UD:P, :], bOut[t % 2][0:UD, P:2 * P], ACT.Copy).then_inc(c_sum, 1)

            def c_body(g, first, last):
                for t in range(GB):
                    n1 = (g, t + 1) if t + 1 < GB else (g + 1, 0)
                    if t or not first:
                        c_sums(*((g, t - 1) if t else (g - 1, GB - 1)))
                    for r in range(3):
                        c_copy(g, t, r)
                        if t == 3 and not last and r == 0:
                            c_repeat(g + 1, 3)
                    if t == 1 and not last:
                        c_query(g + 1)
                    if t == 1 and last:
                        m_route_act(mD, 0)
                    if t == 2 and last:
                        m_route_exp(mD, 0)
                    for s in range(NHG):
                        if t + 1 < GB or not last:
                            c_exps(*n1, s)
                        if t == 2 and not last and s != 1:
                            c_repeat(g + 1, (0, None, 1, 2)[s])
                    if t == 0:
                        norm_hi(2 * NG + 2 + g, xh[:, bass.ds(slot(g + 1), GT)])

            def c_ahead(k):
                if k == 4:
                    c_query(0, qf0)
                if k == 6:
                    act.wait_ge(ks_done, NG * NHG * HG)
                    c_repeat(0, 0, bR0[0])
                    c_repeat(0, 1, bR0[1])
                if k == 7:
                    c_repeat(0, 2, bR0[0])
                    c_repeat(0, 3, bR0[1])

            m_body(m, NG - 1, (2 * NG + 1, None, 0), c_ahead)
            for s in range(NHG):
                c_exps(0, 0, s, first=True)
            c_body(0, True, False)
            with act.Fori(1, NG - 1) as g:
                c_body(g, False, False)
            c_body(NG - 1, False, True)
            c_sums(NG - 1, GB - 1)
            m_silu(mD, 0, 0)
            m_silu(mD, 0, 1)
            m_route_copy(mD, 0)

            m = mD
            m_body(m, 0, (3 * NG + 2, m, 1), begun=2)
            with act.Fori(1, NG - 1) as g:
                m_body(m, g, (3 * NG + g + 2, m, g + 1))
            m_body(m, NG - 1, None)

        @block.vector
        def _(dve):
            V = nc.vector
            for s in (x_done, mB.h_done, mD.h_done, c_norm, c_fin, c_rs):
                dve.sem_inc(s, START)
            dve.wait_ge(in_id, 16)
            dve.wait_ge(built, 1)
            heads = I[:].rearrange("p (s r) -> p s r", s=NHG)
            for n in (2, 3):
                V.tensor_copy(RK[:, :, n, :], heads)
            for n in (1, 3):
                V.tensor_copy(RQ[:, :, n, :], heads)
            V.tensor_reduce(mask4[:], I[:].rearrange("p (t h d) -> p h t d", t=4, h=HG), mybir.AxisListType.XY,
                            ALU.add).then_inc(d_set, 1)

            def xt(g, t):
                return X[:, bass.ds(g * GT + t * P, P)]

            def norm_stats(n, g):
                for t in range(GB):
                    i = V.bn_stats(st[:, t, :], xt(g, t))
                i.then_inc(stats, 1)
                wait_apart(dve, stats, n)
                for t in range(GB):
                    i = V.bn_aggr(mv[:, t, :], st[:, t, :])
                i.then_inc(aggr, 1)
                dve.wait_ge(aggr, n)
                V.tensor_scalar(ve[:], mv[:, :, 1], EPS, None, ALU.add).then_inc(var_rdy, 1)

            def norm_apply(n, g, first=False):
                dve.wait_ge(rstd_rdy, n)
                if not first:
                    dve.wait_ge(xnT, n - 1)
                for t in range(GB):
                    i = V.tensor_scalar(xn[:, t * P:(t + 1) * P], xt(g, t), mv[:, t, 0:1], rstd[:, t:t + 1],
                                        ALU.subtract, ALU.mult)
                i.then_inc(xn_rdy, 1)

            def norm_lo(n, g):
                dve.wait_ge(xh_rdy, n)
                V.tensor_tensor(xl[:, bass.ds(slot(g), GT)], Tb[:], xh[:, bass.ds(slot(g), GT)].bitcast(F32),
                                ALU.subtract).then_inc(xl_rdy, 1)

            dve.wait_ge(in_x0, 16)
            norm_stats(1, 0)
            norm_apply(1, 0, first=True)
            V.tensor_tensor(selD[:], I[0:16, 0:8], I[0:16, 8:16], ALU.add)
            V.tensor_tensor(selB[96:P], I[96:P, 96:112].unsqueeze(2).to_broadcast([32, 16, 64]),
                            I[96:P, 112:P].unsqueeze(2).to_broadcast([32, 16, 64]), ALU.add).then_inc(sel_rdy, 1)
            dve.wait_ge(su_a, 6)
            V.tensor_tensor(WQL[:], bank[4][:, 0:P], WQH[:].bitcast(F32), ALU.subtract).then_inc(su_d, 1)
            dve.wait_ge(su_mm, 6)
            V.tensor_copy(GWH[:], Tb[:, 0:24]).then_inc(gw_hi, 1)
            dve.wait_ge(gw_hi, 1)
            V.tensor_tensor(GWL[:], Tb[:, 0:24], GWH[:].bitcast(F32), ALU.subtract).then_inc(su_d, 1)
            for g in range(NG):
                dve.wait_ge(su_mm, 11 + g)
                V.tensor_copy(bctx[0:1, g * GS:(g + 1) * GS], bC[g][0:1, 0:GS]).then_inc(su_d, 1)
            for n in range(5):
                dve.wait_ge(su_a, 11 + n)
                w = (min(17, 4 * n + 4) - 4 * n) * P
                c = 4 * n * P
                V.tensor_tensor(WBL[:, c:c + w], bank[n][:, 0:w], WBH[:, c:c + w].bitcast(F32),
                                ALU.subtract).then_inc(su_d, 1)
            dve.wait_ge(in_x, 16 * (NG - 1))
            def values(g):
                dve.wait_ge(v_mm, g + 1)
                V.tensor_tensor(Vn[0:S, g * GB:(g + 1) * GB, :], bVn[g][0:S, :].rearrange("p (b d) -> p b d", b=GB),
                                bvr[0:S, :].unsqueeze(1).to_broadcast([S, GB, P]), ALU.add).then_inc(v_done, 1)

            norm_stats(2, 1)
            dve.wait_ge(in_small, 16 * 5)
            values(0)
            values(1)
            norm_apply(2, 1)

            def a_maxima(g):
                dve.wait_ge(a_sc, g + 1)
                sc = Ybank[:, bass.ds(slot(g), GS)].rearrange("p (t k) -> p t k", t=GB)
                V.tensor_reduce(amax[:], sc, AX, ALU.max, negate=True).then_inc(a_max, 1)

            def a_body(g, nxt, more, stats_of=None):
                dve.wait_ge(a_exp, g + 1)
                V.reduce_sum(asum[:, 0, :], PA[:].rearrange("p (t k) -> p t k", t=GB), AX).then_inc(a_sum, 1)
                if more and nxt is not None:
                    norm_apply(g + 3, nxt)
                    a_maxima(g + 1)
                dve.wait_ge(k_h, g + 1)
                V.tensor_tensor(kl[:], kf[:], kh[:].bitcast(F32), ALU.subtract).then_inc(k_l, 1)
                dve.wait_ge(a_sum, g + 1)
                V.reciprocal(asum[:, 1, :], asum[:, 0, :]).then_inc(a_rec, 1)
                if stats_of is not None:
                    norm_stats(g + 4, stats_of)
                dve.wait_ge(a_rec, g + 1)
                V.tensor_scalar(asum[:, 2, :], asum[:, 1, :], tg[:, 0:1], None, ALU.mult).then_inc(a_r, 1)
                if not more:
                    route_vals(mB, 0)
                    route_pick(mB, 0)
                    route_weights(mB, 0)
                dve.wait_ge(a_r, g + 1)
                dve.wait_ge(a_pv, START + g + 1)
                for t in range(GB):
                    i = V.scalar_tensor_tensor(out=xt(g, t), in0=bank[4][:, t * P:(t + 1) * P],
                                               scalar=asum[:, 2, t:t + 1], in1=xt(g, t), op0=ALU.mult, op1=ALU.add)
                i.then_inc(x_done, 1)

            def route_vals(m, g):
                n = m.route_base + g + 1
                if m is mB:
                    dve.wait_ge(route["lgT"], n)
                    V.tensor_scalar(score[:], Tb[:, 0:GB * 16].rearrange("p (t e) -> p t e", t=GB), 0.5, 0.5, ALU.mult, ALU.add).then_inc(route["score"], 1)
                    dve.wait_ge(route["score"], n)
                    V.tensor_tensor(m.vals[:, :, 0:m.E], score[:], gbr[:].unsqueeze(1).to_broadcast([P, GB, 16]),
                                    ALU.add).then_inc(route["vals"], 1)
                else:
                    dve.wait_ge(route["exp"], g + 1)
                    V.tensor_copy(m.vals[:, :, 0:m.E], score[:, :, 0:8]).then_inc(route["vals"], 1)

            def route_sub(g):
                dve.wait_ge(route["lgT"], mD.route_base + g + 1)
                lg = Tb[:, 0:GB * 8].rearrange("p (t e) -> p t e", t=GB)
                V.reduce_max(rsm[:, 0, :], lg, AX).then_inc(route["mx"], 1)
                dve.wait_ge(route["mx"], g + 1)
                V.tensor_tensor(lgt[:, :, 0:8], lg, rsm[:, 0, :].unsqueeze(2).to_broadcast([P, GB, 8]),
                                ALU.subtract).then_inc(route["sub"], 1)

            def route_pick(m, g):
                n = m.route_base + g + 1
                wait_apart(dve, route["vals"], n)
                for t in range(GB):
                    i = V.max(top[:, t, :], m.vals[:, t, :])
                i.then_inc(route["top"], 1)
                dve.wait_ge(route["top"], n)
                V.tensor_copy(m.keep[:, :, 0:m.K], top[:, :, 0:m.K]).then_inc(route["keep"], 1)
                wait_apart(dve, route["keep"], n)
                for t in range(GB):
                    i = V.match_replace(m.rep[:, t, :], m.keep[:, t, :], m.vals[:, t, :], GONE)
                i.then_inc(route["rep"], 1)

            def route_weights(m, g):
                n = m.route_base + g + 1
                E = m.E
                dve.wait_ge(route["rep"], n)
                V.tensor_tensor(comb[:, :, 0:E], m.rep[:, :, 0:E], m.vals[:, :, 0:E], ALU.is_lt).then_inc(route["msk"], 1)
                dve.wait_ge(route["msk"], n)
                V.tensor_tensor(comb[:, :, 0:E], comb[:, :, 0:E], score[:, :, 0:E], ALU.mult).then_inc(route["w"], 1)
                dve.wait_ge(route["w"], n)
                V.reduce_sum(rsm[:, 0, :], comb[:, :, 0:E], AX).then_inc(route["sum"], 1)
                dve.wait_ge(route["sum"], n)
                V.reciprocal(rsm[:, 1, :], rsm[:, 0, :]).then_inc(route["rec"], 1)
                dve.wait_ge(route["rec"], n)
                V.scalar_tensor_tensor(out=comb[:, :, 0:E], in0=comb[:, :, 0:E], scalar=m.scale,
                                       in1=rsm[:, 1, :].unsqueeze(2).to_broadcast([P, GB, E]),
                                       op0=ALU.mult, op1=ALU.mult).then_inc(route["comb"], 1)
                dve.wait_ge(route["comb"], n)
                V.tensor_copy(CH[:, :, 0:E], comb[:, :, 0:E]).then_inc(route["hi"], 1)
                dve.wait_ge(route["hi"], n)
                V.tensor_tensor(CH[:, :, E:2 * E], comb[:, :, 0:E], CH[:, :, 0:E].bitcast(F32),
                                ALU.subtract).then_inc(route["lo"], 1)

            def m_hidden(m, g, k):
                dve.wait_ge(m.s_done, m.units * g + k + 1)
                dve.wait_ge(m.u_done, m.units * g + k + 1)
                V.tensor_tensor(sg[:, k % 2, :], sg[:, k % 2, :], Ub[k % 2][:], ALU.mult).then_inc(m.t2, 1)
                dve.wait_ge(m.t2, m.units * g + k + 1)
                dve.wait_ge(m.c_done, m.units * g + k + 1)
                if used(g, k):
                    dve.wait_ge(m.dn, START + m.units * g + k - 1)
                V.tensor_tensor(hb[:, k % 2, :], sg[:, k % 2, :], Cb[:], ALU.mult).then_inc(m.h_done, 1)

            def m_update(m, g):
                dve.wait_ge(m.dn, START + m.units * (g + 1))
                for t in range(GB):
                    i = V.scalar_tensor_tensor(out=xt(g, t), in0=Ybank[:, bass.ds(slot(g) + t * P, P)],
                                               scalar=tg[:, m.tg:m.tg + 1], in1=xt(g, t), op0=ALU.mult, op1=ALU.add)
                i.then_inc(x_done, 1)

            def m_body(m, g, nxt, then=None):
                for k in range(m.units):
                    m_hidden(m, g, k)
                    if then:
                        then(k)
                    if k == 1 and m.shared:
                        dve.wait_ge(sh_silu, g + 1)
                        V.tensor_tensor(hs[:], hs[:], Tb[0:64, :], ALU.mult).then_inc(sh_hid, 1)
                    if k == 3 and used(g, 0):
                        m_update(m, g - 1)
                    if nxt is None:
                        continue
                    n, nm, ng = nxt
                    if k == 0:
                        norm_stats(n, ng)
                    if k == 1:
                        norm_apply(n, ng)
                    if k == 2:
                        norm_lo(n, ng)
                    if nm is mD and k == 4:
                        route_sub(ng)
                    if nm is not None and k == 4 + (nm is mD):
                        route_vals(nm, ng)
                    if nm is not None and k == 5:
                        route_pick(nm, ng)
                    if nm is not None and k == 6:
                        route_weights(nm, ng)
                if then:
                    then(m.units)

            a_maxima(0)
            values(2)
            values(3)
            dve.wait_ge(tg_rdy, 1)
            V.tensor_scalar(WX[:, 2, :], WX[:, 2, :], tg[:, 1:2], None, ALU.mult).then_inc(wo_rdy, 1)
            V.tensor_scalar(tgbo[:], tgbo[:], tg[:, 1:2], None, ALU.mult).then_inc(d_set, 1)
            norm_stats(3, 2)
            with dve.Fori(0, NG - 3) as g:
                a_body(g, g + 2, True, g + 3)
            dve.wait_ge(x_done, START + 1)
            a_body(NG - 3, NG - 1, True, 0)
            a_body(NG - 2, 0, True)
            norm_lo(NG + 1, 0)
            a_body(NG - 1, None, False)

            m = mB
            m_body(m, 0, (NG + 2, m, 1))
            with dve.Fori(1, NG - 1) as g:
                m_body(m, g, (NG + g + 2, m, g + 1))

            def c_split_high(g, whole=qf, high=qh):
                dve.wait_ge(q_f, g + 1)
                dve.wait_ge(qs_mm, NHG * g)
                V.tensor_copy(high[:], whole[:]).then_inc(q_h, 1)

            def c_split_low(g, whole=qf, high=qh):
                dve.wait_ge(q_h, g + 1)
                V.tensor_tensor(ql[:], whole[:], high[:].bitcast(F32), ALU.subtract).then_inc(q_l, 1)

            bSd = [bank[0], bank[1], bank[2], bank[0]]

            def c_max(g, t, s):
                n = GB * g + t
                dve.wait_ge(c_sc, NHG * n + s + 1)
                V.tensor_reduce(cmx[:, s, :], bSd[s][:, 0:HG * S].rearrange("p (h k) -> p h k", h=HG), AX, ALU.max,
                                negate=True).then_inc(c_mx, 1)

            def c_center(g, t, s, first=False):
                n = GB * g + t
                dve.wait_ge(c_mx, NHG * n + s + 1)
                if not first:
                    dve.wait_ge(c_tr, START + 3 * n - 3)
                V.tensor_tensor(PX[:, t % 2, s * HG * S:(s + 1) * HG * S].rearrange("p (h k) -> p h k", h=HG),
                                bSd[s][:, 0:HG * S].rearrange("p (h k) -> p h k", h=HG),
                                cmx[:, s, :].unsqueeze(2).to_broadcast([P, HG, S]), ALU.add).then_inc(c_sub, 1)

            def c_reciprocal(g, t):
                n = GB * g + t
                dve.wait_ge(c_sum, n + 1)
                V.reciprocal(recT[:], sumT[:]).then_inc(c_rs, 1)

            def c_normalize(g, t):
                n = GB * g + t
                dve.wait_ge(c_rs, START + n + 1)
                dve.wait_ge(c_wo, START + n)
                V.tensor_tensor(OTs[0:UD, :], bOut[t % 2][0:UD, 0:P], recT[0:UD, :], ALU.mult)
                V.tensor_tensor(OTs[UD:P, :], bOut[t % 2][UD:P, P:2 * P], recT[UD:P, :],
                                ALU.mult).then_inc(c_norm, 1)

            def c_final(g, t):
                n = GB * g + t
                if t == 0:
                    dve.wait_ge(bo_add, g + 1)
                dve.wait_ge(c_wo, START + n + 1)
                V.tensor_tensor(xt(g, t), bOut[t % 2][:, 2 * P:3 * P], xt(g, t), ALU.add).then_inc(c_fin, 1)

            def c_body(g, first, last):
                for t in range(GB):
                    n1 = (g, t + 1) if t + 1 < GB else (g + 1, 0)
                    before = (g, t - 1) if t else None if first else (g - 1, GB - 1)
                    before2 = (g, t - 2) if t > 1 else None if first else (g - 1, t + 2)
                    ahead = t + 1 < GB or not last
                    end = t == GB - 1 and last
                    if ahead:
                        c_max(*n1, 0)
                    if before2:
                        c_final(*before2)
                    if ahead:
                        c_center(*n1, 0)
                        c_max(*n1, 1)
                    if t == 1:
                        norm_lo(2 * NG + 2 + g, g + 1)
                    if t == 2 and last:
                        route_sub(0)
                    if ahead:
                        c_max(*n1, 2)
                        c_max(*n1, 3)
                        c_center(*n1, 3)
                    if t == GB - 1 and not last:
                        norm_stats(2 * NG + 3 + g, (g + 2) % NG)
                    if before:
                        c_reciprocal(*before)
                        c_normalize(*before)
                    if t == 1 and not last:
                        c_split_high(g + 1)
                        c_split_low(g + 1)
                    if t == 2 and last:
                        route_vals(mD, 0)
                        route_pick(mD, 0)
                    if end:
                        route_weights(mD, 0)
                        c_final(g, t - 1)

            def c_ahead(k):
                if k == 4:
                    c_split_high(0, qf0, qh0)
                    c_split_low(0, qf0, qh0)
                if k == mB.units:
                    for s in range(3):
                        c_max(0, 0, s)
                        if s in SUB_EXP:
                            c_center(0, 0, s, first=True)

            m_body(m, NG - 1, (2 * NG + 1, None, 0), c_ahead)
            c_max(0, 0, 3)
            c_center(0, 0, 3, first=True)
            m_update(mB, NG - 1)
            norm_stats(2 * NG + 2, 1)
            c_body(0, True, False)
            with dve.Fori(1, NG - 1) as g:
                c_body(g, False, False)
            c_body(NG - 1, False, True)
            c_reciprocal(NG - 1, GB - 1)
            c_normalize(NG - 1, GB - 1)
            c_final(NG - 1, GB - 1)

            m = mD
            m_body(m, 0, (3 * NG + 2, m, 1))
            with dve.Fori(1, NG - 1) as g:
                m_body(m, g, (3 * NG + g + 2, m, g + 1))
            m_body(m, NG - 1, None)
            m_update(m, NG - 1)


_INS = ['x', 'ctx_1024', 'g_xattn', 'g_ffn', 'L0_xattn_W', 'L0_xattn_b', 'L0_ffn_gate_w', 'L0_ffn_gate_b',
        'L0_ffn_w13', 'L0_ffn_w2', 'L0_ffn_w13_s', 'L0_ffn_w2_s', 'L1_xattn_Wq', 'L1_xattn_bq', 'L1_xattn_Wk',
        'L1_xattn_bk', 'L1_xattn_Wv', 'L1_xattn_bv', 'L1_xattn_Wo', 'L1_xattn_bo', 'L1_ffn_router_w',
        'L1_ffn_up_proj', 'L1_ffn_down_proj']


def kernel(**inputs):
    import numpy as _np
    import concourse.bacc as _bacc
    from concourse import mybir as _mybir
    from concourse.bass_utils import run_bass_kernel_spmd as _run

    seed = _np.zeros((P, NC * P), _np.float32)
    for h, c, row, _, n in value_pieces():
        ones = c * P + (1 - h // UH) * UD + h % UH * HD
        seed[row:row + n, ones:ones + HD] = 1.0
    consts = {'ident': _np.eye(P, dtype=_np.float32), 'vs_seed': seed}

    nc = _bacc.Bacc("TRN2", target_bir_lowering=False, num_devices=1)
    arrays, args = {}, []
    for name in _INS + list(consts):
        a = _np.ascontiguousarray(consts[name] if name in consts else inputs[name])
        arrays[f"in_{name}"] = a
        args.append(nc.dram_tensor(f"in_{name}", a.shape, _mybir.dt.from_np(a.dtype), kind="ExternalInput").ap())
    args.append(nc.dram_tensor("out_x", (NB, P, P), _mybir.dt.float32, kind="ExternalOutput").ap())
    flamingo(nc, *args)
    r = _run(nc, [arrays], core_ids=[0])
    return r.results[0]["out_x"]
```
